# Optimizing a Trainium2 kernel written in Bass

```python
import numpy as np
import jax
import jax.numpy as jnp

def _softmax(x, axis=-1):
    return jax.nn.softmax(x, axis=axis)

def _gelu(x):
    return jax.nn.gelu(x, approximate=True)

def _silu(x):
    return jax.nn.silu(x)

def _sigmoid(x):
    return jax.nn.sigmoid(x)

def _layernorm(x, axis=-1, eps=1e-05):
    m = jnp.mean(x, axis=axis, keepdims=True)
    v = jnp.var(x, axis=axis, keepdims=True)
    return (x - m) / jnp.sqrt(v + eps)

def _scatter_add(tgt, idx, src, axis=0):
    return tgt.at[idx].add(src)

def _segment_sum(src, seg, n):
    return jax.ops.segment_sum(src, seg, n)
kernel_name = 'mk_adaln_d1_jaxref_r4_5c3852'

def setup_inputs(seed: int=0):
    np.random.seed(seed)
    _w = jnp.asarray

    def _L0_attn_setup():
        import jax, jax.numpy as jnp
        import numpy as np
        B, T, NE, H = (4, 256, 256, 16)
        HS = NE // H
        EPS = 0.00064

        def _forward(x, time_maa_x, time_maa, maa_w1, maa_w2, decay_w1, decay_w2, aaa_w1, aaa_w2, kkk_w1, kkk_w2, gate_w1, gate_w2, ma_w1, ma_w2, mk_w1, mk_w2, time_decay, time_faaaa, time_aaaaa, time_misc_a, time_misc_k, Wr, Wk, Wv, Wo, ln_w, ln_b):
            Bx, Tx, C = x.shape
            xx = jnp.pad(x, ((0, 0), (1, 0), (0, 0)))[:, :Tx] - x
            mix = x + xx * time_maa_x
            lo = jnp.tanh(jnp.einsum('btc,dc->btd', mix, maa_w1)).reshape(Bx, Tx, 4, 32)
            lo = jnp.einsum('btgk,gkc->gbtc', lo, maa_w2)
            xm = x[None] + xx[None] * (lo + time_maa)
            xrg, xwa, xk, xv = (xm[0], xm[1], xm[2], xm[3])
            r = xrg @ Wr.T
            g = jnp.tanh(xrg @ gate_w1.T) @ gate_w2
            k = xk @ Wk.T
            v = xv @ Wv.T
            w2 = jnp.tanh(xwa @ decay_w1.T) @ decay_w2
            w = -jax.nn.softplus(-(time_decay + w2)) - 0.5
            kk = k + jnp.tanh(xk @ kkk_w1.T) @ kkk_w2
            kkh = kk.reshape(Bx, Tx, H, HS)
            kk = (kkh / jnp.maximum(jnp.linalg.norm(kkh, axis=-1, keepdims=True), 1e-12)).reshape(Bx, Tx, C)
            a = jax.nn.sigmoid(time_aaaaa + xwa @ aaa_w1.T @ aaa_w2)
            ma = jax.nn.sigmoid(time_misc_a + xwa @ ma_w1.T @ ma_w2)
            k = k * ma + k * a * (1.0 - ma)
            mk = jax.nn.sigmoid(time_misc_k + xk @ mk_w1.T @ mk_w2)
            k = k * jnp.exp(w * mk)
            b = -kk * a

            def to_th(t):
                return t.reshape(Bx, Tx, H, HS).transpose(1, 0, 2, 3)
            qt, wt, kt, vt, at, bt = map(to_th, (r, w, k, v, kk, b))
            wt = jnp.exp(-jnp.exp(wt))

            def step(s, inp):
                q_, w_, k_, v_, a_, b_ = inp
                sa = jnp.einsum('bhij,bhj->bhi', s, a_)
                s = s * w_[:, :, None, :] + sa[..., None] * b_[:, :, None, :] + v_[..., None] * k_[:, :, None, :]
                return (s, jnp.einsum('bhij,bhj->bhi', s, q_))
            s0 = jnp.zeros((Bx, H, HS, HS), x.dtype)
            _, y = jax.lax.scan(step, s0, (qt, wt, kt, vt, at, bt))
            y = y.transpose(1, 0, 2, 3).reshape(Bx, Tx, C)
            yg = y.reshape(Bx, Tx, H, HS)
            mu = yg.mean(-1, keepdims=True)
            var = ((yg - mu) ** 2).mean(-1, keepdims=True)
            y = ((yg - mu) / jnp.sqrt(var + EPS)).reshape(Bx, Tx, C) * ln_w + ln_b
            rk = (r.reshape(Bx, Tx, H, HS) * k.reshape(Bx, Tx, H, HS) * time_faaaa.reshape(H, HS)).sum(-1, keepdims=True)
            y = y + (rk * v.reshape(Bx, Tx, H, HS)).reshape(Bx, Tx, C)
            return y * g @ Wo.T
        key = jax.random.key(seed)
        ks = jax.random.split(key, 30)

        def rn(k, shape, s):
            return jax.random.normal(k, shape, jnp.float32) * s
        d = {}
        d['x'] = jax.random.normal(ks[0], (B, T, NE), jnp.float32)
        d['time_maa_x'] = jax.random.uniform(ks[1], (NE,), jnp.float32)
        d['time_maa'] = jax.random.uniform(ks[2], (4, 1, 1, NE), jnp.float32)
        d['maa_w1'] = rn(ks[3], (128, NE), 0.02)
        d['maa_w2'] = rn(ks[4], (4, 32, NE), 0.02)
        d['decay_w1'] = rn(ks[5], (64, NE), 0.02)
        d['decay_w2'] = rn(ks[6], (64, NE), 0.02)
        d['aaa_w1'] = rn(ks[7], (16, NE), 0.02)
        d['aaa_w2'] = rn(ks[8], (16, NE), 0.02)
        d['kkk_w1'] = rn(ks[9], (16, NE), 0.02)
        d['kkk_w2'] = rn(ks[10], (16, NE), 0.02)
        d['gate_w1'] = rn(ks[11], (128, NE), 0.02)
        d['gate_w2'] = rn(ks[12], (128, NE), 0.02)
        d['ma_w1'] = rn(ks[13], (16, NE), 0.02)
        d['ma_w2'] = rn(ks[14], (16, NE), 0.02)
        d['mk_w1'] = rn(ks[15], (16, NE), 0.02)
        d['mk_w2'] = rn(ks[16], (16, NE), 0.02)
        d['time_decay'] = jnp.linspace(-6.5, -1.5, NE, dtype=jnp.float32)
        d['time_faaaa'] = rn(ks[17], (NE,), 0.02)
        d['time_aaaaa'] = rn(ks[18], (NE,), 0.02)
        d['time_misc_a'] = rn(ks[19], (NE,), 0.02)
        d['time_misc_k'] = rn(ks[20], (NE,), 0.02)
        d['Wr'] = rn(ks[21], (NE, NE), 0.5 / NE ** 0.5)
        d['Wk'] = rn(ks[22], (NE, NE), 0.05 / NE ** 0.5)
        d['Wv'] = rn(ks[23], (NE, NE), 0.5 / NE ** 0.5)
        d['Wo'] = rn(ks[24], (NE, NE), 1.0 / NE ** 0.5)
        d['ln_w'] = jnp.ones((NE,), jnp.float32)
        d['ln_b'] = jnp.zeros((NE,), jnp.float32)
        return d
    _L0_attn_in = _L0_attn_setup()

    def _L0_ffn_setup():
        import jax, jax.numpy as jnp
        import numpy as np
        DIM = 256
        DEPTH = 2
        HEADS = 8
        DIM_HEAD = 64
        WINDOW = 128
        INNER = HEADS * DIM_HEAD
        HID = int(DIM * 4 * 2 / 3)
        B, N = (2, 2048)
        QK_SCALE = 8.0

        def shift_token(t):
            t1, t2 = jnp.split(t, 2, axis=-1)
            t2 = jnp.pad(t2, ((0, 0), (1, 0), (0, 0)))[:, :-1]
            return jnp.concatenate([t1, t2], axis=-1)

        def l2norm(t):
            return t / jnp.clip(jnp.linalg.norm(t, axis=-1, keepdims=True), 1e-12)

        def rotate_half(x):
            x1, x2 = jnp.split(x, 2, axis=-1)
            return jnp.concatenate([-x2, x1], axis=-1)

        def rotary_xpos(q, k):
            n = q.shape[-2]
            half_idx = jnp.arange(0, DIM_HEAD, 2, dtype=jnp.float32)
            inv_freq = 1.0 / 10000.0 ** (half_idx / DIM_HEAD)
            t = jnp.arange(n, dtype=jnp.float32)
            freqs = t[:, None] * inv_freq[None, :]
            freqs = jnp.concatenate([freqs, freqs], axis=-1)
            base = (half_idx + 0.4 * DIM_HEAD) / (1.4 * DIM_HEAD)
            power = (t - n // 2) / float(WINDOW // 2)
            scale = base[None, :] ** power[:, None]
            scale = jnp.concatenate([scale, scale], axis=-1)
            cos, sin = (jnp.cos(freqs), jnp.sin(freqs))
            q = q * cos * scale + rotate_half(q) * sin * scale
            k = k * cos / scale + rotate_half(k) * sin / scale
            return (q, k)

        def local_attention(q, k, v):
            b, h, n, d = q.shape
            w = n // WINDOW
            bq = q.reshape(b, h, w, WINDOW, d) * QK_SCALE
            bk = k.reshape(b, h, w, WINDOW, d)
            bv = v.reshape(b, h, w, WINDOW, d)

            def look_around(t):
                p = jnp.pad(t, ((0, 0), (0, 0), (1, 0), (0, 0), (0, 0)))
                return jnp.concatenate([p[:, :, :w], p[:, :, 1:]], axis=3)
            bk, bv = (look_around(bk), look_around(bv))
            bt = jnp.arange(n).reshape(w, WINDOW)
            btp = jnp.pad(bt, ((1, 0), (0, 0)), constant_values=-1)
            btk = jnp.concatenate([btp[:w], btp[1:]], axis=1)
            sim = jnp.einsum('bhwid,bhwjd->bhwij', bq, bk)
            i = bt[:, :, None]
            j = btk[:, None, :]
            mask = (i < j) | (i > j + WINDOW) | (j == -1)
            sim = jnp.where(mask, -jnp.finfo(sim.dtype).max, sim)
            attn = jax.nn.softmax(sim, axis=-1)
            out = jnp.einsum('bhwij,bhwjd->bhwid', attn, bv)
            return out.reshape(b, h, n, d)

        def _layer(x, wqkv, qs, ksc, wo, lg, lb, w1, b1, w2, b2):
            b, n, _ = x.shape
            h = shift_token(x)
            qkv = h @ wqkv
            q, k, v = jnp.split(qkv, 3, axis=-1)
            to_heads = lambda t: t.reshape(b, n, HEADS, DIM_HEAD).transpose(0, 2, 1, 3)
            q, k, v = (to_heads(q), to_heads(k), to_heads(v))
            q = l2norm(q) * qs
            k = l2norm(k) * ksc
            q, k = rotary_xpos(q, k)
            o = local_attention(q, k, v)
            o = o.transpose(0, 2, 1, 3).reshape(b, n, INNER)
            x = x + o @ wo
            h = shift_token(x)
            mu = h.mean(-1, keepdims=True)
            var = h.var(-1, keepdims=True)
            h = (h - mu) / jnp.sqrt(var + 1e-05) * lg + lb
            h = h @ w1 + b1
            a, g = jnp.split(h, 2, axis=-1)
            h = a * jax.nn.gelu(g, approximate=False)
            x = x + h @ w2 + b2
            return x
        key = jax.random.key(seed)
        ks = jax.random.split(key, 6)
        return {'x': jax.random.normal(ks[0], (B, N, DIM), jnp.float32), 'wqkv': jax.random.normal(ks[1], (DEPTH, DIM, 3 * INNER), jnp.float32) * 0.02, 'q_scale': jnp.ones((DEPTH, DIM_HEAD), jnp.float32), 'k_scale': jnp.ones((DEPTH, DIM_HEAD), jnp.float32), 'wo': jax.random.normal(ks[2], (DEPTH, INNER, DIM), jnp.float32) * 0.02, 'ln_g': jnp.ones((DEPTH, DIM), jnp.float32), 'ln_b': jnp.zeros((DEPTH, DIM), jnp.float32), 'w1': jax.random.normal(ks[3], (DEPTH, DIM, 2 * HID), jnp.float32) * 0.02, 'b1': jnp.zeros((DEPTH, 2 * HID), jnp.float32), 'w2': jax.random.normal(ks[4], (DEPTH, HID, DIM), jnp.float32) * 0.02, 'b2': jnp.zeros((DEPTH, DIM), jnp.float32)}
    _L0_ffn_in = _L0_ffn_setup()
    _L0_c = _w((lambda *s: np.random.randn(*s).astype(np.float32) * 0.05)(2, 256))
    _L0_wmod = _w((lambda *s: np.random.randn(*s).astype(np.float32) * 0.05)(256, 6 * 256) * 256 ** (-0.5))
    _d = {'L0_attn_x': _L0_attn_in['x'], 'L0_attn_time_maa_x': _L0_attn_in['time_maa_x'], 'L0_attn_time_maa': _L0_attn_in['time_maa'], 'L0_attn_maa_w1': _L0_attn_in['maa_w1'], 'L0_attn_maa_w2': _L0_attn_in['maa_w2'], 'L0_attn_decay_w1': _L0_attn_in['decay_w1'], 'L0_attn_decay_w2': _L0_attn_in['decay_w2'], 'L0_attn_aaa_w1': _L0_attn_in['aaa_w1'], 'L0_attn_aaa_w2': _L0_attn_in['aaa_w2'], 'L0_attn_kkk_w1': _L0_attn_in['kkk_w1'], 'L0_attn_kkk_w2': _L0_attn_in['kkk_w2'], 'L0_attn_gate_w1': _L0_attn_in['gate_w1'], 'L0_attn_gate_w2': _L0_attn_in['gate_w2'], 'L0_attn_ma_w1': _L0_attn_in['ma_w1'], 'L0_attn_ma_w2': _L0_attn_in['ma_w2'], 'L0_attn_mk_w1': _L0_attn_in['mk_w1'], 'L0_attn_mk_w2': _L0_attn_in['mk_w2'], 'L0_attn_time_decay': _L0_attn_in['time_decay'], 'L0_attn_time_faaaa': _L0_attn_in['time_faaaa'], 'L0_attn_time_aaaaa': _L0_attn_in['time_aaaaa'], 'L0_attn_time_misc_a': _L0_attn_in['time_misc_a'], 'L0_attn_time_misc_k': _L0_attn_in['time_misc_k'], 'L0_attn_Wr': _L0_attn_in['Wr'], 'L0_attn_Wk': _L0_attn_in['Wk'], 'L0_attn_Wv': _L0_attn_in['Wv'], 'L0_attn_Wo': _L0_attn_in['Wo'], 'L0_attn_ln_w': _L0_attn_in['ln_w'], 'L0_attn_ln_b': _L0_attn_in['ln_b'], 'L0_ffn_wqkv': _L0_ffn_in['wqkv'], 'L0_ffn_q_scale': _L0_ffn_in['q_scale'], 'L0_ffn_k_scale': _L0_ffn_in['k_scale'], 'L0_ffn_wo': _L0_ffn_in['wo'], 'L0_ffn_ln_g': _L0_ffn_in['ln_g'], 'L0_ffn_ln_b': _L0_ffn_in['ln_b'], 'L0_ffn_w1': _L0_ffn_in['w1'], 'L0_ffn_b1': _L0_ffn_in['b1'], 'L0_ffn_w2': _L0_ffn_in['w2'], 'L0_ffn_b2': _L0_ffn_in['b2'], 'L0_c': _L0_c, 'L0_wmod': _L0_wmod}
    _x0 = _d['L0_attn_x']
    _d['L0_attn_x'] = jax.random.normal(jax.random.fold_in(jax.random.key(seed), 1), (2, 4096, 256), dtype=_x0.dtype)
    del _x0
    return _d

def reference(L0_attn_x, L0_attn_time_maa_x, L0_attn_time_maa, L0_attn_maa_w1, L0_attn_maa_w2, L0_attn_decay_w1, L0_attn_decay_w2, L0_attn_aaa_w1, L0_attn_aaa_w2, L0_attn_kkk_w1, L0_attn_kkk_w2, L0_attn_gate_w1, L0_attn_gate_w2, L0_attn_ma_w1, L0_attn_ma_w2, L0_attn_mk_w1, L0_attn_mk_w2, L0_attn_time_decay, L0_attn_time_faaaa, L0_attn_time_aaaaa, L0_attn_time_misc_a, L0_attn_time_misc_k, L0_attn_Wr, L0_attn_Wk, L0_attn_Wv, L0_attn_Wo, L0_attn_ln_w, L0_attn_ln_b, L0_ffn_wqkv, L0_ffn_q_scale, L0_ffn_k_scale, L0_ffn_wo, L0_ffn_ln_g, L0_ffn_ln_b, L0_ffn_w1, L0_ffn_b1, L0_ffn_w2, L0_ffn_b2, L0_c, L0_wmod):

    def _L0_attn_ref(x, time_maa_x, time_maa, maa_w1, maa_w2, decay_w1, decay_w2, aaa_w1, aaa_w2, kkk_w1, kkk_w2, gate_w1, gate_w2, ma_w1, ma_w2, mk_w1, mk_w2, time_decay, time_faaaa, time_aaaaa, time_misc_a, time_misc_k, Wr, Wk, Wv, Wo, ln_w, ln_b):
        import jax, jax.numpy as jnp
        import numpy as np
        B, T, NE, H = (4, 256, 256, 16)
        HS = NE // H
        EPS = 0.00064

        def _forward(x, time_maa_x, time_maa, maa_w1, maa_w2, decay_w1, decay_w2, aaa_w1, aaa_w2, kkk_w1, kkk_w2, gate_w1, gate_w2, ma_w1, ma_w2, mk_w1, mk_w2, time_decay, time_faaaa, time_aaaaa, time_misc_a, time_misc_k, Wr, Wk, Wv, Wo, ln_w, ln_b):
            Bx, Tx, C = x.shape
            xx = jnp.pad(x, ((0, 0), (1, 0), (0, 0)))[:, :Tx] - x
            mix = x + xx * time_maa_x
            lo = jnp.tanh(jnp.einsum('btc,dc->btd', mix, maa_w1)).reshape(Bx, Tx, 4, 32)
            lo = jnp.einsum('btgk,gkc->gbtc', lo, maa_w2)
            xm = x[None] + xx[None] * (lo + time_maa)
            xrg, xwa, xk, xv = (xm[0], xm[1], xm[2], xm[3])
            r = xrg @ Wr.T
            g = jnp.tanh(xrg @ gate_w1.T) @ gate_w2
            k = xk @ Wk.T
            v = xv @ Wv.T
            w2 = jnp.tanh(xwa @ decay_w1.T) @ decay_w2
            w = -jax.nn.softplus(-(time_decay + w2)) - 0.5
            kk = k + jnp.tanh(xk @ kkk_w1.T) @ kkk_w2
            kkh = kk.reshape(Bx, Tx, H, HS)
            kk = (kkh / jnp.maximum(jnp.linalg.norm(kkh, axis=-1, keepdims=True), 1e-12)).reshape(Bx, Tx, C)
            a = jax.nn.sigmoid(time_aaaaa + xwa @ aaa_w1.T @ aaa_w2)
            ma = jax.nn.sigmoid(time_misc_a + xwa @ ma_w1.T @ ma_w2)
            k = k * ma + k * a * (1.0 - ma)
            mk = jax.nn.sigmoid(time_misc_k + xk @ mk_w1.T @ mk_w2)
            k = k * jnp.exp(w * mk)
            b = -kk * a

            def to_th(t):
                return t.reshape(Bx, Tx, H, HS).transpose(1, 0, 2, 3)
            qt, wt, kt, vt, at, bt = map(to_th, (r, w, k, v, kk, b))
            wt = jnp.exp(-jnp.exp(wt))

            def step(s, inp):
                q_, w_, k_, v_, a_, b_ = inp
                sa = jnp.einsum('bhij,bhj->bhi', s, a_)
                s = s * w_[:, :, None, :] + sa[..., None] * b_[:, :, None, :] + v_[..., None] * k_[:, :, None, :]
                return (s, jnp.einsum('bhij,bhj->bhi', s, q_))
            s0 = jnp.zeros((Bx, H, HS, HS), x.dtype)
            _, y = jax.lax.scan(step, s0, (qt, wt, kt, vt, at, bt))
            y = y.transpose(1, 0, 2, 3).reshape(Bx, Tx, C)
            yg = y.reshape(Bx, Tx, H, HS)
            mu = yg.mean(-1, keepdims=True)
            var = ((yg - mu) ** 2).mean(-1, keepdims=True)
            y = ((yg - mu) / jnp.sqrt(var + EPS)).reshape(Bx, Tx, C) * ln_w + ln_b
            rk = (r.reshape(Bx, Tx, H, HS) * k.reshape(Bx, Tx, H, HS) * time_faaaa.reshape(H, HS)).sum(-1, keepdims=True)
            y = y + (rk * v.reshape(Bx, Tx, H, HS)).reshape(Bx, Tx, C)
            return y * g @ Wo.T
        return _forward(x, time_maa_x, time_maa, maa_w1, maa_w2, decay_w1, decay_w2, aaa_w1, aaa_w2, kkk_w1, kkk_w2, gate_w1, gate_w2, ma_w1, ma_w2, mk_w1, mk_w2, time_decay, time_faaaa, time_aaaaa, time_misc_a, time_misc_k, Wr, Wk, Wv, Wo, ln_w, ln_b)

    def _L0_ffn_ref(x, wqkv, q_scale, k_scale, wo, ln_g, ln_b, w1, b1, w2, b2):
        import jax, jax.numpy as jnp
        import numpy as np
        DIM = 256
        DEPTH = 2
        HEADS = 8
        DIM_HEAD = 64
        WINDOW = 128
        INNER = HEADS * DIM_HEAD
        HID = int(DIM * 4 * 2 / 3)
        B, N = (2, 2048)
        QK_SCALE = 8.0

        def shift_token(t):
            t1, t2 = jnp.split(t, 2, axis=-1)
            t2 = jnp.pad(t2, ((0, 0), (1, 0), (0, 0)))[:, :-1]
            return jnp.concatenate([t1, t2], axis=-1)

        def l2norm(t):
            return t / jnp.clip(jnp.linalg.norm(t, axis=-1, keepdims=True), 1e-12)

        def rotate_half(x):
            x1, x2 = jnp.split(x, 2, axis=-1)
            return jnp.concatenate([-x2, x1], axis=-1)

        def rotary_xpos(q, k):
            n = q.shape[-2]
            half_idx = jnp.arange(0, DIM_HEAD, 2, dtype=jnp.float32)
            inv_freq = 1.0 / 10000.0 ** (half_idx / DIM_HEAD)
            t = jnp.arange(n, dtype=jnp.float32)
            freqs = t[:, None] * inv_freq[None, :]
            freqs = jnp.concatenate([freqs, freqs], axis=-1)
            base = (half_idx + 0.4 * DIM_HEAD) / (1.4 * DIM_HEAD)
            power = (t - n // 2) / float(WINDOW // 2)
            scale = base[None, :] ** power[:, None]
            scale = jnp.concatenate([scale, scale], axis=-1)
            cos, sin = (jnp.cos(freqs), jnp.sin(freqs))
            q = q * cos * scale + rotate_half(q) * sin * scale
            k = k * cos / scale + rotate_half(k) * sin / scale
            return (q, k)

        def local_attention(q, k, v):
            b, h, n, d = q.shape
            w = n // WINDOW
            bq = q.reshape(b, h, w, WINDOW, d) * QK_SCALE
            bk = k.reshape(b, h, w, WINDOW, d)
            bv = v.reshape(b, h, w, WINDOW, d)

            def look_around(t):
                p = jnp.pad(t, ((0, 0), (0, 0), (1, 0), (0, 0), (0, 0)))
                return jnp.concatenate([p[:, :, :w], p[:, :, 1:]], axis=3)
            bk, bv = (look_around(bk), look_around(bv))
            bt = jnp.arange(n).reshape(w, WINDOW)
            btp = jnp.pad(bt, ((1, 0), (0, 0)), constant_values=-1)
            btk = jnp.concatenate([btp[:w], btp[1:]], axis=1)
            sim = jnp.einsum('bhwid,bhwjd->bhwij', bq, bk)
            i = bt[:, :, None]
            j = btk[:, None, :]
            mask = (i < j) | (i > j + WINDOW) | (j == -1)
            sim = jnp.where(mask, -jnp.finfo(sim.dtype).max, sim)
            attn = jax.nn.softmax(sim, axis=-1)
            out = jnp.einsum('bhwij,bhwjd->bhwid', attn, bv)
            return out.reshape(b, h, n, d)

        def _layer(x, wqkv, qs, ksc, wo, lg, lb, w1, b1, w2, b2):
            b, n, _ = x.shape
            h = shift_token(x)
            qkv = h @ wqkv
            q, k, v = jnp.split(qkv, 3, axis=-1)
            to_heads = lambda t: t.reshape(b, n, HEADS, DIM_HEAD).transpose(0, 2, 1, 3)
            q, k, v = (to_heads(q), to_heads(k), to_heads(v))
            q = l2norm(q) * qs
            k = l2norm(k) * ksc
            q, k = rotary_xpos(q, k)
            o = local_attention(q, k, v)
            o = o.transpose(0, 2, 1, 3).reshape(b, n, INNER)
            x = x + o @ wo
            h = shift_token(x)
            mu = h.mean(-1, keepdims=True)
            var = h.var(-1, keepdims=True)
            h = (h - mu) / jnp.sqrt(var + 1e-05) * lg + lb
            h = h @ w1 + b1
            a, g = jnp.split(h, 2, axis=-1)
            h = a * jax.nn.gelu(g, approximate=False)
            x = x + h @ w2 + b2
            return x
        for l in range(DEPTH):
            x = _layer(x, wqkv[l], q_scale[l], k_scale[l], wo[l], ln_g[l], ln_b[l], w1[l], b1[l], w2[l], b2[l])
        return x
    x = L0_attn_x
    mod = (_silu(L0_c) @ L0_wmod).reshape(L0_c.shape[0], 6, 1, -1)
    sa, ca, ga, sb, cb, gb = (mod[:, 0], mod[:, 1], mod[:, 2], mod[:, 3], mod[:, 4], mod[:, 5])
    ga = (2 * (ga >= 0) - 1) * jnp.maximum(jnp.abs(ga), 0.25)
    gb = (2 * (gb >= 0) - 1) * jnp.maximum(jnp.abs(gb), 0.25)
    h = _layernorm(x, axis=-1) * (1 + ca) + sa
    x = x + ga * _L0_attn_ref(h, L0_attn_time_maa_x, L0_attn_time_maa, L0_attn_maa_w1, L0_attn_maa_w2, L0_attn_decay_w1, L0_attn_decay_w2, L0_attn_aaa_w1, L0_attn_aaa_w2, L0_attn_kkk_w1, L0_attn_kkk_w2, L0_attn_gate_w1, L0_attn_gate_w2, L0_attn_ma_w1, L0_attn_ma_w2, L0_attn_mk_w1, L0_attn_mk_w2, L0_attn_time_decay, L0_attn_time_faaaa, L0_attn_time_aaaaa, L0_attn_time_misc_a, L0_attn_time_misc_k, L0_attn_Wr, L0_attn_Wk, L0_attn_Wv, L0_attn_Wo, L0_attn_ln_w, L0_attn_ln_b)
    h = _layernorm(x, axis=-1) * (1 + cb) + sb
    x = x + gb * _L0_ffn_ref(h, L0_ffn_wqkv, L0_ffn_q_scale, L0_ffn_k_scale, L0_ffn_wo, L0_ffn_ln_g, L0_ffn_ln_b, L0_ffn_w1, L0_ffn_b1, L0_ffn_w2, L0_ffn_b2)
    return x

_drawn_inputs = setup_inputs


def setup_inputs(seed=0):
    import zlib

    import numpy as np

    out = dict(_drawn_inputs(seed))
    spreads = {'L0_attn_ln_w': (1.0, 0.2),
     'L0_attn_ln_b': (0.0, 0.1),
     'L0_ffn_q_scale': (1.0, 0.2),
     'L0_ffn_k_scale': (1.0, 0.2),
     'L0_ffn_ln_g': (1.0, 0.2),
     'L0_ffn_ln_b': (0.0, 0.1),
     'L0_ffn_b1': (0.0, 0.1),
     'L0_ffn_b2': (0.0, 0.1)}
    factors = {}
    for name, (base, spread) in spreads.items():
        noise = np.random.default_rng([zlib.crc32(name.encode()), seed]).standard_normal(out[name].shape)
        drawn = base * np.exp(spread * noise) if base else spread * noise
        out[name] = jnp.asarray(drawn.astype(out[name].dtype))
    for name, factor in factors.items():
        out[name] = (out[name] * factor).astype(out[name].dtype)
    return out
```

```python
import math

import concourse.bass as bass
from concourse import mybir
from contextlib import ExitStack

F32 = mybir.dt.float32
BF16 = mybir.dt.bfloat16
ALU = mybir.AluOpType
ACT = mybir.ActivationFunctionType
AX = mybir.AxisListType

P = 128
NB = 2
C = 256
CC = C // P
HS = 16
CH = 16
NCH = P // CH
HP = P // HS
HEADS = 8
DH = 64
INNER = HEADS * DH
HID = 682
MT = 6
MW = 114
START = 2
LN_EXP = "natural_log_exp_and_others"
KAPPA = math.exp(-0.5)
LNSCALE = 2.0 ** 40
MASKED = -1.0e30

MIX_W = [("maa1", 2 * 128), ("wr", 2 * C), ("gate1", 2 * 128), ("wa1", 2 * 128), ("wk", 2 * C), ("kk1", 2 * 128),
         ("wv", 2 * C), ("maa2_0", C), ("maa2_1", C), ("maa2_2", C), ("maa2_3", C), ("gate2", C), ("decay2", C),
         ("aaa2", C), ("ma2", C), ("kkk2", C), ("mk2", C)]
VECS = ["maa_x", "maa0", "maa1", "maa2", "maa3", "decay", "aaaaa", "misc_a", "misc_k", "faaaa", "ln_w", "ln_b"]


def places(parts):
    at, out = 0, {}
    for name, n in parts:
        out[name] = (at, n)
        at += n
    return out, at


class Signal:

    def __init__(self, sem, step, ahead):
        self.sem, self.step, self.ahead = sem, step, ahead

    def after(self, unit, back=0):
        return (unit + (self.ahead + 1 - back)) * self.step


def signals(nc, ctx, names, streams, tag, ahead=START):
    out = {}
    for item in names.split():
        name, _, step = item.partition(":")
        made = [Signal(ctx.enter_context(nc.semaphore(f"{tag}_{name}{b}")), int(step or 1), ahead) for b in range(streams)]
        out[name] = made
    return out


def start_signals(nc, plain, *tables):
    with nc.Block() as block:
        @block.gpsimd
        def _(pool):
            for sem in plain:
                pool.sem_clear(sem)
            for table in tables:
                for made in table.values():
                    for s in made:
                        pool.sem_clear(s.sem)
                        pool.sem_inc(s.sem, s.ahead * s.step)


def setup_stage(nc, persist, a):
    modc, rows, constant = persist["modc"], persist["rows"], persist["const"]
    with ExitStack() as ctx:
        sb = lambda n, s, d=F32: ctx.enter_context(nc.sbuf_tensor(n, s, d))
        sem = lambda n: ctx.enter_context(nc.semaphore(n))
        wmod = sb("wmod", [P, CC, 6 * C])
        cT = sb("cT", [P, CC, NB])
        ex = sb("ex", [P, CC, NB])
        den = sb("den", [P, CC, NB])
        inv = sb("inv", [P, CC, NB])
        sc = sb("sc", [P, CC, NB])
        scb = sb("scb", [P, CC, NB, P])
        ones = sb("ones", [P, P])
        raw = sb("raw", [P, 24])
        neg = sb("neg", [P, 4 * C])
        mag = sb("mag", [P, 4 * C])
        sgn = sb("sgn", [P, 4 * C])
        rraw = sb("rraw", [P, 4 * C])
        pm = ctx.enter_context(nc.psum_tensor("pmod", [P, 512], F32))
        pr = [ctx.enter_context(nc.psum_tensor(f"prow{k}", [P, 512], F32)) for k in range(2)]
        s_in, s_ex, s_v, s_sc, s_mm, s_rr, s_end = map(sem, ["su_in", "su_ex", "su_v", "su_sc", "su_mm", "su_rr", "su_end"])
        with nc.Block() as block:
            @block.sync
            def _(sp):
                sp.dma_start(wmod[:], a["wmod"]).then_inc(s_in, 16)
                sp.dma_start(cT[:], a["c_t"]).then_inc(s_in, 16)
                sp.dma_start(persist["vec"][:], a["vecs"]).then_inc(s_in, 16)
                sp.dma_start(persist["ident"][:], a["ident"]).then_inc(s_in, 16)

            @block.scalar
            def _(act):
                act.wait_ge(s_in, 64)
                nc.scalar.activation(ex[:], cT[:], ACT.Exp, scale=-1.0).then_inc(s_ex, 1)

            @block.gpsimd
            def _(pool):
                for k, v in enumerate([1e-5, 1.0, 20.0 * math.log(2.0), 0.00064, 0.0, 0.0, 0.0, 0.0]):
                    nc.gpsimd.memset(constant[:, k:k + 1], v)
                nc.gpsimd.memset(ones[:], 1.0).then_inc(s_end, 1)
                pool.wait_ge(s_end, 1)

            @block.vector
            def _(dve):
                dve.wait_ge(s_ex, 1)
                nc.vector.tensor_scalar(den[:], ex[:], 1.0, None, ALU.add).then_inc(s_v, 1)
                dve.wait_ge(s_v, 1)
                nc.vector.reciprocal(inv[:], den[:]).then_inc(s_v, 1)
                dve.wait_ge(s_v, 2)
                nc.vector.tensor_tensor(sc[:], inv[:], cT[:], ALU.mult).then_inc(s_v, 1)
                dve.wait_ge(s_v, 3)
                dve.wait_ge(s_end, 1)
                for k in range(CC):
                    for b in range(NB):
                        nc.vector.tensor_scalar(scb[:, k, b, :], ones[:], sc[:, k, b:b + 1], None, ALU.mult).then_inc(s_sc, 1)
                nc.vector.tensor_scalar(persist["half"][:], persist["vec"][:, 6:9, :], 0.5, None, ALU.mult).then_inc(s_v, 1)
                dve.wait_ge(s_mm, 1)
                nc.vector.tensor_copy(raw[:], pm[:, 0:24])
                for k in range(2):
                    last = nc.vector.tensor_copy(rraw[:, 512 * k:512 * (k + 1)], pr[k][:])
                last.then_inc(s_v, 1)
                dve.wait_ge(s_v, 5)
                nc.vector.tensor_copy(modc[:], raw[:]).then_inc(s_v, 1)
                dve.wait_ge(s_v, 6)
                for j in (1, 4):
                    nc.vector.tensor_scalar(modc[:, 4 * j:4 * j + 4], raw[:, 4 * j:4 * j + 4], 1.0, None, ALU.add)
                nc.vector.tensor_scalar(neg[:], rraw[:], -1.0, None, ALU.mult)
                nc.vector.tensor_scalar(sgn[:], rraw[:], 0.0, 2.0, ALU.is_ge, ALU.mult).then_inc(s_v, 1)
                dve.wait_ge(s_v, 7)
                nc.vector.tensor_tensor(mag[:], rraw[:], neg[:], ALU.max).then_inc(s_v, 1)
                dve.wait_ge(s_v, 8)
                nc.vector.tensor_scalar(neg[:], mag[:], 0.25, None, ALU.max).then_inc(s_v, 1)
                dve.wait_ge(s_v, 9)
                nc.vector.scalar_tensor_tensor(out=rows[:], in0=sgn[:], scalar=-1.0, in1=neg[:], op0=ALU.add,
                                               op1=ALU.mult).then_inc(s_v, 1)
                dve.wait_ge(s_v, 10)

            @block.tensor
            def _(pe):
                pe.wait_ge(s_sc, CC * NB)
                for j in range(6):
                    for m in range(CC):
                        for k in range(CC):
                            at = 4 * j + 2 * m
                            nc.tensor.matmul(pm[:, at:at + NB], wmod[:, k, j * C + m * P:j * C + (m + 1) * P], sc[:, k, :],
                                             start=(k == 0), stop=(k == CC - 1))
                for q, j in enumerate((2, 5)):
                    for b in range(NB):
                        for k in range(CC):
                            last = nc.tensor.matmul(pr[q][:, b * C:(b + 1) * C], scb[:, k, b, :], wmod[:, k, j * C:(j + 1) * C],
                                                    start=(k == 0), stop=(k == CC - 1))
                last.then_inc(s_mm, 1)


def mix_stage(nc, persist, a, T):
    NW = T // P
    modc, vec, half, const, ident = (persist[k] for k in ("modc", "vec", "half", "const", "ident"))
    W, ncols = places(MIX_W)
    with ExitStack() as ctx:
        sb = lambda n, s, d=F32: [ctx.enter_context(nc.sbuf_tensor(f"{n}{b}", s, d)) for b in range(NB)]
        wp = ctx.enter_context(nc.sbuf_tensor("mixw", [P, ncols], F32))
        ones16 = ctx.enter_context(nc.sbuf_tensor("ones16", [P, P], F32))
        bonus = ctx.enter_context(nc.sbuf_tensor("bonus", [P, CC, P], F32))
        resets = ctx.enter_context(nc.sbuf_tensor("resets", [P, CC * P], F32))
        xt, xn = sb("xt", [P, C]), sb("xn", [P, C])
        st, mv, lnv, rstd = sb("st", [P, 6]), sb("mv", [P, 2]), sb("lnv", [P, 1]), sb("rstd", [P, 1])
        h, xx, mix = sb("h", [P, CC, P + 1]), sb("xx", [P, CC, P]), sb("mix", [P, CC, P])
        lot, tm, xm = sb("lot", [P, P]), sb("tm", [P, 4, CC, P]), sb("xm", [P, 4, CC, P])
        th_g, th_w, th_k = sb("th_g", [P, P]), sb("th_w", [P, P]), sb("th_k", [P, P])
        full = [P, CC, P]
        r, k, v, zb, ta, tma, tmk = (sb(n, full) for n in ("r", "k", "v", "zb", "ta", "tma", "tmk"))
        kk, sq, nn, rn, az, ez, lz, nm, L1 = (sb(n, full) for n in ("kk", "sq", "nn", "rn", "az", "ez", "lz", "nm", "L1"))
        sg, cum, cprev, mkp, wm, ek = (sb(n, full) for n in ("sg", "cum", "cprev", "mkp", "wm", "ek"))
        gam, gami, gamp = (sb(n, full) for n in ("gam", "gami", "gamp"))
        kkn, aa, ba, m1, pq, kf, k2, k3, rk3 = (sb(n, full) for n in ("kkn", "aa", "ba", "m1", "pq", "kf", "k2", "k3", "rk3"))
        cm = sb("cm", [P, CC, 4, P])
        gr = sb("gr", [P, 2, CC, P])
        gl = sb("gl", [P, CC, NCH])
        vt = sb("vt", [P, C])
        pause = ctx.enter_context(nc.sbuf_tensor("pause", [P, NB], F32))
        bank = [[ctx.enter_context(nc.psum_tensor(f"mx{n}{b}", [P, 512], F32)) for n in "ABCD"] for b in range(NB)]
        S = signals(nc, ctx, "x_in:16 stats mean_var ln_var rstd xn xT carry h xx mix lo lo_tanh pm tm xm hidden rk_ps v_ps "
                    "hidden_sb rk_sb v_sb da_ps mm_ps g_ps kk_ps zb gates g_sb kk sq norm_ps clamped ln_norm inv_norm "
                    "abs_z exp_z ln_z min_z log_sig sig mk wm ek cum cprev gam gami gamp kkn a_t q_t aa ba b_t m1 pq kf "
                    "k2 k3 k_t rk3 rk_ps2 rkv gl vT_ps vT stored:48 v_stored:128", NB, "mx")
        s_w, s_c = ctx.enter_context(nc.semaphore("mx_w")), ctx.enter_context(nc.semaphore("mx_c"))
        start_signals(nc, (s_w, s_c), S)
        w = lambda name: wp[:, W[name][0]:W[name][0] + W[name][1]]
        w2 = lambda name: w(name).rearrange("p (k m) -> p k m", k=CC)
        flat = lambda t: t[:].rearrange("p c t -> p (c t)")
        vc = lambda name, c: vec[:, VECS.index(name), c:c + 1]
        with nc.Block() as block:
            @block.sync
            def _(sp):
                sp.dma_start(wp[:], a["mix_w"]).then_inc(s_w, 16)
                sp.dma_start(ones16[:], a["ones16"]).then_inc(s_w, 16)
                sp.dma_start(resets[:], a["resets"]).then_inc(s_w, 16)
                with sp.Fori(0, NW) as i:
                    for b in range(NB):
                        sp.wait_ge(S["xn"][b].sem, S["xn"][b].after(i, 1))
                        sp.dma_start(xt[b][:], a["x"][b, bass.ds(i * P, P), :]).then_inc(S["x_in"][b].sem, 16)
                    for b in range(NB):
                        sp.wait_ge(S["vT"][b].sem, S["vT"][b].after(i))
                        for c in range(NCH):
                            sp.dma_start(a["v_stack"][b, bass.ds(i, 1)].rearrange("o (h t) g c i -> (o c) t g h i", t=CH)[c],
                                         vt[b][c * CH:(c + 1) * CH, :].rearrange("t (g h i) -> t g h i", g=CC, h=HP)
                                         ).then_inc(S["v_stored"][b].sem, 16)
                        sp.wait_ge(S["a_t"][b].sem, S["a_t"][b].after(i))
                        sp.wait_ge(S["q_t"][b].sem, S["q_t"][b].after(i))
                        sp.wait_ge(S["b_t"][b].sem, S["b_t"][b].after(i))
                        sp.wait_ge(S["k_t"][b].sem, S["k_t"][b].after(i))
                        sp.dma_start(a["cm"][b, bass.ds(i, 1)].rearrange("o p n -> (o p) n"),
                                     cm[b][:].rearrange("p g x t -> p (g x t)")).then_inc(S["stored"][b].sem, 16)
                        sp.wait_ge(S["gl"][b].sem, S["gl"][b].after(i))
                        sp.dma_start(a["gl"][b, bass.ds(i, 1)].rearrange("o p n -> (o p) n"),
                                     gl[b][:].rearrange("p g c -> p (g c)")).then_inc(S["stored"][b].sem, 16)
                        sp.wait_ge(S["rkv"][b].sem, S["rkv"][b].after(i))
                        sp.wait_ge(S["g_sb"][b].sem, S["g_sb"][b].after(i))
                        sp.dma_start(a["gr"][b, bass.ds(i, 1)].rearrange("o p n -> (o p) n"),
                                     gr[b][:].rearrange("p x c t -> p (x c t)")).then_inc(S["stored"][b].sem, 16)
                for b in range(NB):
                    sp.wait_ge(S["stored"][b].sem, S["stored"][b].after(NW - 1))
                    sp.wait_ge(S["v_stored"][b].sem, S["v_stored"][b].after(NW - 1))

            @block.vector
            def _(dve):
                dve.wait_ge(s_w, 48)
                for b in range(NB):
                    nc.vector.memset(h[b][:], 0.0)
                for c in range(CC):
                    last = nc.vector.tensor_scalar(bonus[:, c, :], ones16[:], vc("faaaa", c), None, ALU.mult)
                last.then_inc(s_c, 1)
                with dve.Fori(0, NW) as i:
                    for b in range(NB):
                        dve.wait_ge(S["x_in"][b].sem, S["x_in"][b].after(i))
                        nc.vector.bn_stats(st[b][:], xt[b][:]).then_inc(S["stats"][b].sem, 1)
                    for b in range(NB):
                        dve.wait_ge(S["stats"][b].sem, S["stats"][b].after(i))
                        dve.wait_ge(S["ln_var"][b].sem, S["ln_var"][b].after(i, 1))
                        nc.vector.memset(pause[:, b:b + 1], 0.0)
                        nc.vector.bn_aggr(mv[b][:], st[b][:]).then_inc(S["mean_var"][b].sem, 1)
                    for b in range(NB):
                        dve.wait_ge(S["rstd"][b].sem, S["rstd"][b].after(i))
                        dve.wait_ge(S["xT"][b].sem, S["xT"][b].after(i, 1))
                        nc.vector.tensor_scalar(xn[b][:], xt[b][:], mv[b][:, 0:1], rstd[b][:], ALU.subtract, ALU.mult
                                                ).then_inc(S["xn"][b].sem, 1)
                    for b in range(NB):
                        dve.wait_ge(S["h"][b].sem, S["h"][b].after(i))
                        nc.vector.tensor_tensor(xx[b][:], h[b][:, :, 0:P], h[b][:, :, 1:P + 1], ALU.subtract
                                                ).then_inc(S["xx"][b].sem, 1)
                    for b in range(NB):
                        dve.wait_ge(S["xx"][b].sem, S["xx"][b].after(i))
                        dve.wait_ge(S["lo"][b].sem, S["lo"][b].after(i, 1))
                        for c in range(CC):
                            last = nc.vector.scalar_tensor_tensor(out=mix[b][:, c, :], in0=xx[b][:, c, :], scalar=vc("maa_x", c),
                                                                  in1=h[b][:, c, 1:P + 1], op0=ALU.mult, op1=ALU.add)
                        last.then_inc(S["mix"][b].sem, 1)
                    for b in range(NB):
                        dve.wait_ge(S["pm"][b].sem, S["pm"][b].after(i))
                        dve.wait_ge(S["xm"][b].sem, S["xm"][b].after(i, 1))
                        for g in range(4):
                            for c in range(CC):
                                src = bank[b][2 + g // 2][:, (g % 2) * C + c * P:(g % 2) * C + (c + 1) * P]
                                last = nc.vector.scalar_tensor_tensor(out=tm[b][:, g, c, :], in0=src, scalar=vc(f"maa{g}", c),
                                                                      in1=xx[b][:, c, :], op0=ALU.add, op1=ALU.mult)
                        last.then_inc(S["tm"][b].sem, 1)
                    for b in range(NB):
                        dve.wait_ge(S["kk_ps"][b].sem, S["kk_ps"][b].after(i))
                        dve.wait_ge(S["rk_sb"][b].sem, S["rk_sb"][b].after(i))
                        nc.vector.tensor_tensor(kk[b][:], bank[b][0][:, 0:C].rearrange("p (c t) -> p c t", c=CC), k[b][:],
                                                ALU.add).then_inc(S["kk"][b].sem, 1)
                    for b in range(NB):
                        dve.wait_ge(S["zb"][b].sem, S["zb"][b].after(i))
                        nc.vector.tensor_scalar(nm[b][:], zb[b][:], 0.0, None, ALU.min).then_inc(S["min_z"][b].sem, 1)
                        dve.wait_ge(S["gates"][b].sem, S["gates"][b].after(i))
                        nc.vector.tensor_scalar(mkp[b][:], tmk[b][:], 0.5, 0.5, ALU.mult, ALU.add).then_inc(S["mk"][b].sem, 1)
                        nc.vector.tensor_scalar(aa[b][:], ta[b][:], 0.5, 0.5, ALU.mult, ALU.add).then_inc(S["aa"][b].sem, 1)
                        nc.vector.tensor_scalar(m1[b][:], tma[b][:], -1.0, None, ALU.add).then_inc(S["m1"][b].sem, 1)
                        dve.wait_ge(S["norm_ps"][b].sem, S["norm_ps"][b].after(i))
                        nc.vector.tensor_scalar(nn[b][:], bank[b][0][:, C:2 * C].rearrange("p (c t) -> p c t", c=CC), 1e-24, None,
                                                ALU.max).then_inc(S["clamped"][b].sem, 1)
                        dve.wait_ge(S["m1"][b].sem, S["m1"][b].after(i))
                        nc.vector.scalar_tensor_tensor(out=pq[b][:], in0=ta[b][:], scalar=-1.0, in1=m1[b][:], op0=ALU.add,
                                                       op1=ALU.mult).then_inc(S["pq"][b].sem, 1)
                    for b in range(NB):
                        dve.wait_ge(S["ln_z"][b].sem, S["ln_z"][b].after(i))
                        dve.wait_ge(S["min_z"][b].sem, S["min_z"][b].after(i))
                        nc.vector.tensor_tensor(L1[b][:], nm[b][:], lz[b][:], ALU.subtract).then_inc(S["log_sig"][b].sem, 1)
                        dve.wait_ge(S["pq"][b].sem, S["pq"][b].after(i))
                        nc.vector.tensor_scalar(kf[b][:], pq[b][:], -0.25, 1.0, ALU.mult, ALU.add).then_inc(S["kf"][b].sem, 1)
                    for b in range(NB):
                        dve.wait_ge(S["mk"][b].sem, S["mk"][b].after(i))
                        dve.wait_ge(S["log_sig"][b].sem, S["log_sig"][b].after(i))
                        nc.vector.scalar_tensor_tensor(out=wm[b][:], in0=L1[b][:], scalar=-0.5, in1=mkp[b][:], op0=ALU.add,
                                                       op1=ALU.mult).then_inc(S["wm"][b].sem, 1)
                        dve.wait_ge(S["kf"][b].sem, S["kf"][b].after(i))
                        nc.vector.tensor_tensor(k2[b][:], k[b][:], kf[b][:], ALU.mult).then_inc(S["k2"][b].sem, 1)
                    for b in range(NB):
                        dve.wait_ge(S["sig"][b].sem, S["sig"][b].after(i))
                        nc.vector.tensor_tensor_scan(flat(cum[b]), resets[:], flat(sg[b]), 0.0, ALU.mult, ALU.add
                                                     ).then_inc(S["cum"][b].sem, 1)
                    for b in range(NB):
                        dve.wait_ge(S["inv_norm"][b].sem, S["inv_norm"][b].after(i))
                        nc.vector.tensor_tensor(kkn[b][:], kk[b][:], rn[b][:], ALU.mult).then_inc(S["kkn"][b].sem, 1)
                        dve.wait_ge(S["k2"][b].sem, S["k2"][b].after(i))
                        dve.wait_ge(S["ek"][b].sem, S["ek"][b].after(i))
                        nc.vector.tensor_tensor(k3[b][:], k2[b][:], ek[b][:], ALU.mult).then_inc(S["k3"][b].sem, 1)
                    for b in range(NB):
                        dve.wait_ge(S["stored"][b].sem, S["stored"][b].after(i, 1))
                        dve.wait_ge(S["kkn"][b].sem, S["kkn"][b].after(i))
                        dve.wait_ge(S["gamp"][b].sem, S["gamp"][b].after(i))
                        nc.vector.tensor_tensor(cm[b][:, :, 0, :], kkn[b][:], gamp[b][:], ALU.mult).then_inc(S["a_t"][b].sem, 1)
                        dve.wait_ge(S["k3"][b].sem, S["k3"][b].after(i))
                        dve.wait_ge(S["gami"][b].sem, S["gami"][b].after(i))
                        nc.vector.tensor_tensor(cm[b][:, :, 3, :], k3[b][:], gami[b][:], ALU.mult).then_inc(S["k_t"][b].sem, 1)
                        dve.wait_ge(S["ba"][b].sem, S["ba"][b].after(i))
                        nc.vector.scalar_tensor_tensor(out=cm[b][:, :, 2, :], in0=ba[b][:], scalar=-1.0, in1=gami[b][:],
                                                       op0=ALU.mult, op1=ALU.mult).then_inc(S["b_t"][b].sem, 1)
                    for b in range(NB):
                        dve.wait_ge(S["rk_ps2"][b].sem, S["rk_ps2"][b].after(i))
                        nc.vector.tensor_tensor(gr[b][:, 1], bank[b][1][:, 0:C].rearrange("p (c t) -> p c t", c=CC), v[b][:],
                                                ALU.mult).then_inc(S["rkv"][b].sem, 1)

            @block.gpsimd
            def _(pool):
                with pool.Fori(0, NW) as i:
                    for b in range(NB):
                        pool.wait_ge(S["tm"][b].sem, S["tm"][b].after(i))
                        pool.wait_ge(S["v_ps"][b].sem, S["v_ps"][b].after(i, 1))
                        nc.gpsimd.tensor_tensor(xm[b][:], tm[b][:], h[b][:, :, 1:P + 1].unsqueeze(1).broadcast_to([P, 4, CC, P]),
                                                ALU.add).then_inc(S["xm"][b].sem, 1)
                    for b in range(NB):
                        pool.wait_ge(S["cum"][b].sem, S["cum"][b].after(i))
                        nc.gpsimd.tensor_tensor(cprev[b][:], cum[b][:], sg[b][:], ALU.subtract).then_inc(S["cprev"][b].sem, 1)
                    for b in range(NB):
                        pool.wait_ge(S["kkn"][b].sem, S["kkn"][b].after(i))
                        pool.wait_ge(S["aa"][b].sem, S["aa"][b].after(i))
                        nc.gpsimd.tensor_tensor(ba[b][:], kkn[b][:], aa[b][:], ALU.mult).then_inc(S["ba"][b].sem, 1)
                        pool.wait_ge(S["k3"][b].sem, S["k3"][b].after(i))
                        nc.gpsimd.tensor_tensor(rk3[b][:], r[b][:], k3[b][:], ALU.mult).then_inc(S["rk3"][b].sem, 1)
                        pool.wait_ge(S["gam"][b].sem, S["gam"][b].after(i))
                        pool.wait_ge(S["stored"][b].sem, S["stored"][b].after(i, 1))
                        nc.gpsimd.tensor_tensor(cm[b][:, :, 1, :], r[b][:], gam[b][:], ALU.mult).then_inc(S["q_t"][b].sem, 1)
                        nc.gpsimd.tensor_copy(gl[b][:], gam[b][:].rearrange("p g (c t) -> p g c t", t=CH)[:, :, :, CH - 1]
                                              ).then_inc(S["gl"][b].sem, 1)

            @block.scalar
            def _(act):
                with act.Fori(0, NW) as i:
                    act.preload_act_table_set(LN_EXP)
                    for b in range(NB):
                        act.wait_ge(S["mean_var"][b].sem, S["mean_var"][b].after(i))
                        nc.scalar.activation(lnv[b][:], mv[b][:, 1:2], ACT.Ln, bias=const[:, 0:1]).then_inc(S["ln_var"][b].sem, 1)
                        act.wait_ge(S["ln_var"][b].sem, S["ln_var"][b].after(i))
                        act.wait_ge(S["xn"][b].sem, S["xn"][b].after(i, 1))
                        nc.scalar.activation(rstd[b][:], lnv[b][:], ACT.Exp, scale=-0.5).then_inc(S["rstd"][b].sem, 1)
                    for b in range(NB):
                        act.wait_ge(S["xT"][b].sem, S["xT"][b].after(i))
                        act.wait_ge(S["xm"][b].sem, S["xm"][b].after(i, 1))
                        act.wait_ge(S["h"][b].sem, S["h"][b].after(i, 1))
                        nc.scalar.copy(h[b][:, :, 0:1], h[b][:, :, P:P + 1]).then_inc(S["carry"][b].sem, 1)
                        act.wait_ge(S["carry"][b].sem, S["carry"][b].after(i))
                        for c in range(CC):
                            last = nc.scalar.activation(h[b][:, c, 1:P + 1], bank[b][0][:, c * P:(c + 1) * P], ACT.Identity,
                                                        scale=modc[:, 4 + 2 * c + b:5 + 2 * c + b], bias=modc[:, 2 * c + b:2 * c + b + 1])
                        last.then_inc(S["h"][b].sem, 1)
                    for b in range(NB):
                        act.wait_ge(S["lo"][b].sem, S["lo"][b].after(i))
                        act.wait_ge(S["pm"][b].sem, S["pm"][b].after(i, 1))
                        nc.scalar.activation(lot[b][:], bank[b][1][:, 0:P], ACT.Tanh).then_inc(S["lo_tanh"][b].sem, 1)
                    for b in range(NB):
                        act.wait_ge(S["hidden"][b].sem, S["hidden"][b].after(i))
                        act.wait_ge(S["kk_ps"][b].sem, S["kk_ps"][b].after(i, 1))
                        act.wait_ge(S["g_ps"][b].sem, S["g_ps"][b].after(i, 1))
                        nc.scalar.activation(th_w[b][0:64, :], bank[b][1][0:64, 0:P], ACT.Tanh)
                        nc.scalar.copy(th_w[b][64:128, :], bank[b][1][64:128, 0:P])
                        nc.scalar.activation(th_g[b][:], bank[b][1][:, P:2 * P], ACT.Tanh)
                        nc.scalar.activation(th_k[b][0:64, :], bank[b][1][0:64, 2 * P:3 * P], ACT.Tanh)
                        nc.scalar.copy(th_k[b][64:128, :], bank[b][1][64:128, 2 * P:3 * P]).then_inc(S["hidden_sb"][b].sem, 1)
                        act.wait_ge(S["rk_ps"][b].sem, S["rk_ps"][b].after(i))
                        act.wait_ge(S["q_t"][b].sem, S["q_t"][b].after(i, 1))
                        act.wait_ge(S["k2"][b].sem, S["k2"][b].after(i, 1))
                        nc.scalar.copy(flat(r[b]), bank[b][0][:, 0:C])
                        nc.scalar.copy(flat(k[b]), bank[b][0][:, C:2 * C]).then_inc(S["rk_sb"][b].sem, 1)
                        act.wait_ge(S["v_ps"][b].sem, S["v_ps"][b].after(i))
                        act.wait_ge(S["rkv"][b].sem, S["rkv"][b].after(i, 1))
                        nc.scalar.copy(flat(v[b]), bank[b][2][:, 0:C]).then_inc(S["v_sb"][b].sem, 1)
                    for b in range(NB):
                        act.wait_ge(S["da_ps"][b].sem, S["da_ps"][b].after(i))
                        act.wait_ge(S["pq"][b].sem, S["pq"][b].after(i, 1))
                        act.wait_ge(S["aa"][b].sem, S["aa"][b].after(i, 1))
                        act.wait_ge(S["abs_z"][b].sem, S["abs_z"][b].after(i, 1))
                        for c in range(CC):
                            last = nc.scalar.activation(zb[b][:, c, :], bank[b][3][:, c * P:(c + 1) * P], ACT.Identity, bias=vc("decay", c))
                        last.then_inc(S["zb"][b].sem, 1)
                        for c in range(CC):
                            nc.scalar.activation(ta[b][:, c, :], bank[b][3][:, C + c * P:C + (c + 1) * P], ACT.Tanh, scale=0.5,
                                                 bias=half[:, 0, c:c + 1])
                        act.wait_ge(S["mm_ps"][b].sem, S["mm_ps"][b].after(i))
                        for c in range(CC):
                            nc.scalar.activation(tma[b][:, c, :], bank[b][1][:, c * P:(c + 1) * P], ACT.Tanh, scale=0.5,
                                                 bias=half[:, 1, c:c + 1])
                        for c in range(CC):
                            last = nc.scalar.activation(tmk[b][:, c, :], bank[b][1][:, C + c * P:C + (c + 1) * P], ACT.Tanh, scale=0.5,
                                                        bias=half[:, 2, c:c + 1])
                        last.then_inc(S["gates"][b].sem, 1)
                    act.preload_act_table_set(LN_EXP)
                    for b in range(NB):
                        act.wait_ge(S["kk"][b].sem, S["kk"][b].after(i))
                        nc.scalar.activation(sq[b][:], kk[b][:], ACT.Square).then_inc(S["sq"][b].sem, 1)
                        act.wait_ge(S["g_ps"][b].sem, S["g_ps"][b].after(i))
                        act.wait_ge(S["stored"][b].sem, S["stored"][b].after(i, 1))
                        nc.scalar.copy(gr[b][:, 0].rearrange("p c t -> p (c t)"), bank[b][2][:, 0:C]).then_inc(S["g_sb"][b].sem, 1)
                        act.wait_ge(S["vT_ps"][b].sem, S["vT_ps"][b].after(i))
                        act.wait_ge(S["v_stored"][b].sem, S["v_stored"][b].after(i, 1))
                        nc.scalar.copy(vt[b][:], bank[b][2][:, C:2 * C]).then_inc(S["vT"][b].sem, 1)
                        act.wait_ge(S["zb"][b].sem, S["zb"][b].after(i))
                        nc.scalar.activation(az[b][:], zb[b][:], ACT.Abs).then_inc(S["abs_z"][b].sem, 1)
                    for b in range(NB):
                        act.wait_ge(S["abs_z"][b].sem, S["abs_z"][b].after(i))
                        nc.scalar.activation(ez[b][:], az[b][:], ACT.Exp, scale=-1.0).then_inc(S["exp_z"][b].sem, 1)
                    for b in range(NB):
                        act.wait_ge(S["exp_z"][b].sem, S["exp_z"][b].after(i))
                        nc.scalar.activation(lz[b][:], ez[b][:], ACT.Ln, bias=const[:, 1:2]).then_inc(S["ln_z"][b].sem, 1)
                    for b in range(NB):
                        act.wait_ge(S["clamped"][b].sem, S["clamped"][b].after(i))
                        nc.scalar.activation(az[b][:], nn[b][:], ACT.Ln, scale=LNSCALE).then_inc(S["ln_norm"][b].sem, 1)
                        act.wait_ge(S["log_sig"][b].sem, S["log_sig"][b].after(i))
                        nc.scalar.activation(sg[b][:], L1[b][:], ACT.Exp).then_inc(S["sig"][b].sem, 1)
                    for b in range(NB):
                        act.wait_ge(S["ln_norm"][b].sem, S["ln_norm"][b].after(i))
                        nc.scalar.activation(rn[b][:], az[b][:], ACT.Exp, scale=-0.5, bias=const[:, 2:3]).then_inc(S["inv_norm"][b].sem, 1)
                        act.wait_ge(S["wm"][b].sem, S["wm"][b].after(i))
                        nc.scalar.activation(ek[b][:], wm[b][:], ACT.Exp).then_inc(S["ek"][b].sem, 1)
                    for b in range(NB):
                        act.wait_ge(S["cum"][b].sem, S["cum"][b].after(i))
                        act.wait_ge(S["gl"][b].sem, S["gl"][b].after(i, 1))
                        nc.scalar.activation(gam[b][:], cum[b][:], ACT.Exp, scale=-KAPPA).then_inc(S["gam"][b].sem, 1)
                        nc.scalar.activation(gami[b][:], cum[b][:], ACT.Exp, scale=KAPPA).then_inc(S["gami"][b].sem, 1)
                        act.wait_ge(S["cprev"][b].sem, S["cprev"][b].after(i))
                        nc.scalar.activation(gamp[b][:], cprev[b][:], ACT.Exp, scale=-KAPPA).then_inc(S["gamp"][b].sem, 1)

            @block.tensor
            def _(pe):
                mm = nc.tensor.matmul

                def project(out, name, m0, m1_, x):
                    for kc in range(CC):
                        last_ = mm(out, w2(name)[:, kc, m0:m1_], x[:, kc, :], start=(kc == 0), stop=(kc == CC - 1))
                    return last_

                pe.wait_ge(s_w, 48)
                pe.wait_ge(s_c, 1)
                with pe.Fori(0, NW) as i:
                    for b in range(NB):
                        A, B, Cb, D = bank[b]
                        pe.wait_ge(S["xn"][b].sem, S["xn"][b].after(i))
                        pe.wait_ge(S["clamped"][b].sem, S["clamped"][b].after(i, 1))
                        pe.wait_ge(S["kk"][b].sem, S["kk"][b].after(i, 1))
                        for c in range(CC):
                            last = nc.tensor.transpose(A[:, c * P:(c + 1) * P], xn[b][:, c * P:(c + 1) * P], ident[:])
                        last.then_inc(S["xT"][b].sem, 1)
                    for b in range(NB):
                        A, B, Cb, D = bank[b]
                        pe.wait_ge(S["mix"][b].sem, S["mix"][b].after(i))
                        pe.wait_ge(S["rkv"][b].sem, S["rkv"][b].after(i, 1))
                        project(B[:, 0:P], "maa1", 0, P, mix[b]).then_inc(S["lo"][b].sem, 1)
                    for b in range(NB):
                        A, B, Cb, D = bank[b]
                        pe.wait_ge(S["lo_tanh"][b].sem, S["lo_tanh"][b].after(i))
                        pe.wait_ge(S["vT"][b].sem, S["vT"][b].after(i, 1))
                        pe.wait_ge(S["gates"][b].sem, S["gates"][b].after(i, 1))
                        for g in range(4):
                            for c in range(CC):
                                at = (g % 2) * C + c * P
                                last = mm([Cb, D][g // 2][:, at:at + P], w(f"maa2_{g}")[:, c * P:(c + 1) * P], lot[b][:],
                                          start=True, stop=True)
                        last.then_inc(S["pm"][b].sem, 1)
                    for b in range(NB):
                        A, B, Cb, D = bank[b]
                        pe.wait_ge(S["xm"][b].sem, S["xm"][b].after(i))
                        project(B[:, 0:P], "wa1", 0, P, xm[b][:, 1])
                        project(B[:, P:2 * P], "gate1", 0, P, xm[b][:, 0])
                        project(B[:, 2 * P:3 * P], "kk1", 0, P, xm[b][:, 2]).then_inc(S["hidden"][b].sem, 1)
                        for m in range(CC):
                            project(A[:, m * P:(m + 1) * P], "wr", m * P, (m + 1) * P, xm[b][:, 0])
                        for m in range(CC):
                            last = project(A[:, C + m * P:C + (m + 1) * P], "wk", m * P, (m + 1) * P, xm[b][:, 2])
                        last.then_inc(S["rk_ps"][b].sem, 1)
                        for m in range(CC):
                            last = project(Cb[:, m * P:(m + 1) * P], "wv", m * P, (m + 1) * P, xm[b][:, 3])
                        last.then_inc(S["v_ps"][b].sem, 1)
                    for b in range(NB):
                        A, B, Cb, D = bank[b]
                        pe.wait_ge(S["hidden_sb"][b].sem, S["hidden_sb"][b].after(i))
                        for m in range(CC):
                            mm(D[:, m * P:(m + 1) * P], w("decay2")[:, m * P:(m + 1) * P], th_w[b][:], start=True, stop=True)
                        for m in range(CC):
                            last = mm(D[:, C + m * P:C + (m + 1) * P], w("aaa2")[:, m * P:(m + 1) * P], th_w[b][:],
                                      start=True, stop=True)
                        last.then_inc(S["da_ps"][b].sem, 1)
                        for m in range(CC):
                            mm(B[:, m * P:(m + 1) * P], w("ma2")[:, m * P:(m + 1) * P], th_w[b][:], start=True, stop=True)
                        for m in range(CC):
                            last = mm(B[:, C + m * P:C + (m + 1) * P], w("mk2")[:, m * P:(m + 1) * P], th_k[b][:],
                                      start=True, stop=True)
                        last.then_inc(S["mm_ps"][b].sem, 1)
                        pe.wait_ge(S["rk_sb"][b].sem, S["rk_sb"][b].after(i))
                        for m in range(CC):
                            last = mm(A[:, m * P:(m + 1) * P], w("kkk2")[:, m * P:(m + 1) * P], th_k[b][:], start=True, stop=True)
                        last.then_inc(S["kk_ps"][b].sem, 1)
                        pe.wait_ge(S["v_sb"][b].sem, S["v_sb"][b].after(i))
                        for m in range(CC):
                            last = mm(Cb[:, m * P:(m + 1) * P], w("gate2")[:, m * P:(m + 1) * P], th_g[b][:], start=True, stop=True)
                        last.then_inc(S["g_ps"][b].sem, 1)
                    for b in range(NB):
                        A, B, Cb, D = bank[b]
                        pe.wait_ge(S["g_sb"][b].sem, S["g_sb"][b].after(i))
                        for c in range(CC):
                            last = nc.tensor.transpose(Cb[:, C + c * P:C + (c + 1) * P], v[b][:, c, :], ident[:])
                        last.then_inc(S["vT_ps"][b].sem, 1)
                        pe.wait_ge(S["sq"][b].sem, S["sq"][b].after(i))
                        mm(A[:, C:2 * C], ones16[:], flat(sq[b]), start=True, stop=True).then_inc(S["norm_ps"][b].sem, 1)
                    for b in range(NB):
                        A, B, Cb, D = bank[b]
                        pe.wait_ge(S["rk3"][b].sem, S["rk3"][b].after(i))
                        pe.wait_ge(S["gates"][b].sem, S["gates"][b].after(i))
                        for c in range(CC):
                            last = mm(B[:, c * P:(c + 1) * P], bonus[:, c, :], rk3[b][:, c, :], start=True, stop=True)
                        last.then_inc(S["rk_ps2"][b].sem, 1)


def scan_stage(nc, persist, a, T):
    NW = T // P
    BG = NB * CC
    HALF = NCH // 2
    const, ident = persist["const"], persist["ident"]
    with ExitStack() as ctx:
        sb = lambda n, s: ctx.enter_context(nc.sbuf_tensor("sc_" + n, s, F32))
        cm = sb("cm", [P, NB, CC, 4, P])
        v = [sb(f"v{k}", [P, NB, CC, HALF, HS]) for k in range(2)]
        gl = [sb(f"gl{k}", [P, NB, CC, HALF]) for k in range(2)]
        bx, kx = ([sb(f"{n}{k}", [P, BG, HP, CH]) for k in range(2)] for n in ("bx", "kx"))
        ax, qx = ([sb(f"{n}{c}", [P, BG, HP, CH]) for c in range(NCH)] for n in ("ax", "qx"))
        bT, kT = ([sb(f"{n}{c}", [P, BG, P]) for c in range(NCH)] for n in ("bT", "kT"))
        att = sb("att", [P, NCH, BG, 2, 2, CH])
        tt = [sb(f"tt{k}", [P, HALF, BG, CH]) for k in range(2)]
        d_ak, d_t, d_qb, d_qk = ([sb(f"{n}{k}", [P, BG, HP, CH]) for k in range(2)] for n in ("d_ak", "d_t", "d_qb", "d_qk"))
        prob = [sb(f"prob{k}", [P, CH, CH]) for k in range(2)]
        sol = [sb(f"sol{k}", [P, CH, CH]) for k in range(2)]
        step_ = sb("step", [P, CH * CH])
        causal, headmask, eye = sb("causal", [P, 2, CH]), sb("headmask", [P, HP]), sb("eye", [P, CH, CH])
        state = [sb(f"state{k}", [P, BG, HS]) for k in range(2)]
        p_sb, sa_sb = sb("p", [P, BG, HS]), sb("sa", [P, BG, HS])
        y = [sb(f"y{k}", [P, HALF, BG, HS]) for k in range(2)]
        dev, ysq, yn = (sb(n, [P, HALF * BG, HS]) for n in ("dev", "ysq", "yn"))
        mean, mean16, var, lnv, rs = (sb(n, [P, HALF * BG]) for n in ("mean", "mean16", "var", "lnv", "rs"))
        ps = lambda n: ctx.enter_context(nc.psum_tensor("sc_" + n, [P, 512], F32))
        P_ps, SA_ps, S_ps, Y_ps, AB_ps, TB_ps, TK_ps = (ps(n) for n in ("P", "SA", "S", "Y", "AB", "TB", "TK"))
        S = signals(nc, ctx, "bk_x aq_x ab_ps tb_ps tk_ps att_sb bT kT d_ak d_t d_qb d_qk p_ps p_sb sa_ps sa_sb s_ps s_sb y_ps y_sb",
                    1, "sc", ahead=2 * NCH)
        Wn = signals(nc, ctx, "cm_in:32", 1, "sw")
        Hf = signals(nc, ctx, "v_in:64 att_out:16 prob_in:16 solved inv_out:16 tt_in:16 sum dev ysq var lnv rs yn mean y_out:16", 2, "sh")
        s_c, s_chain, s_state = (ctx.enter_context(nc.semaphore(n)) for n in ("sc_const", "sc_chain", "sc_state0"))
        start_signals(nc, (s_c, s_chain, s_state), S, Wn, Hf)
        S = {k_: v_[0] for k_, v_ in S.items()}
        cm_in = Wn["cm_in"][0]
        chain = [0]

        def bg(t, q):
            return t[:, q // CC, q % CC]

        def chunk_tokens(c):
            return slice(c * CH, (c + 1) * CH)

        with nc.Block() as block:
            @block.sync
            def _(sp):
                sp.dma_start(causal[:], a["causal"]).then_inc(s_c, 16)
                sp.dma_start(headmask[:], a["headmask"]).then_inc(s_c, 16)
                sp.dma_start(eye[:], a["eye16"][:, 0]).then_inc(s_c, 16)

                def load_cm(u):
                    sp.wait_ge(S["aq_x"].sem, S["aq_x"].after(u * NCH - 1))
                    sp.wait_ge(S["ab_ps"].sem, S["ab_ps"].after(u * NCH - 1))
                    for b in range(NB):
                        sp.dma_start(cm[:, b].rearrange("p g x t -> p (g x t)"),
                                     a["cm"][b, bass.ds(u, 1)].rearrange("o p n -> (o p) n")).then_inc(cm_in.sem, 16)

                def load_v(u, k):
                    sp.wait_ge(S["y_ps"].sem, S["y_ps"].after(u * NCH - NCH + HALF * (k + 1) - 1))
                    sp.wait_ge(S["s_sb"].sem, S["s_sb"].after(u * NCH - NCH + HALF * (k + 1) - 1))
                    for b in range(NB):
                        sp.dma_start(v[k][:, b], a["v_stack"][b, bass.ds(u, 1), :, :, k * HALF:(k + 1) * HALF, :]
                                     .rearrange("o p g c i -> (o p) g c i")).then_inc(Hf["v_in"][k].sem, 16)
                        sp.dma_start(gl[k][:, b], a["gl"][b, bass.ds(u, 1)].rearrange("o p (g c) -> (o p) g c", g=CC)
                                     [:, :, k * HALF:(k + 1) * HALF]).then_inc(Hf["v_in"][k].sem, 16)

                def pose(u, k):
                    sp.wait_ge(S["att_sb"].sem, S["att_sb"].after(u * NCH + HALF * (k + 1) - 1))
                    q = bass.ds(2 * u + k, 1)
                    sp.dma_start(a["att"][q].rearrange("o (c q) h m t -> (o h m) c q t", c=HALF),
                                 att[:, k * HALF:(k + 1) * HALF, :, 0, 0, :]).then_inc(Hf["att_out"][k].sem, 16)
                    sp.wait_ge(Hf["att_out"][k].sem, Hf["att_out"][k].after(u))
                    sp.wait_ge(Hf["solved"][k].sem, Hf["solved"][k].after(u, 1))
                    sp.dma_start(prob[k][:], a["att"][q].rearrange("o q h m t -> (o q h) m t")).then_inc(Hf["prob_in"][k].sem, 16)

                def fetch(u, k):
                    q = bass.ds(2 * u + k, 1)
                    sp.wait_ge(Hf["solved"][k].sem, Hf["solved"][k].after(u))
                    sp.dma_start(a["inv"][q].rearrange("o q h m t -> (o q h) m t"), sol[k][:]).then_inc(Hf["inv_out"][k].sem, 16)
                    sp.wait_ge(Hf["inv_out"][k].sem, Hf["inv_out"][k].after(u))
                    sp.wait_ge(S["d_t"].sem, S["d_t"].after(u * NCH + HALF * (k + 1) - 1 - NCH))
                    sp.dma_start(tt[k][:], a["inv"][q].rearrange("o (c q) h m t -> (o h m) c q t", c=HALF)).then_inc(Hf["tt_in"][k].sem, 16)

                def store_y(u, k):
                    sp.wait_ge(Hf["yn"][k].sem, Hf["yn"][k].after(u))
                    sp.dma_start(a["y_stack"][bass.ds(u, 1), k].rearrange("o p n -> (o p) n"),
                                 yn[:].rearrange("p q i -> p (q i)")).then_inc(Hf["y_out"][k].sem, 16)

                load_cm(0)
                load_v(0, 0)
                load_v(0, 1)
                pose(0, 0)
                fetch(0, 0)
                pose(0, 1)

                def body(u, more):
                    if more:
                        load_cm(u + 1)
                    fetch(u, 1)
                    if more:
                        pose(u + 1, 0)
                        load_v(u + 1, 0)
                    store_y(u, 0)
                    if more:
                        fetch(u + 1, 0)
                        pose(u + 1, 1)
                        load_v(u + 1, 1)
                    store_y(u, 1)

                with sp.Fori(0, NW - 1) as i:
                    body(i, True)
                body(NW - 1, False)
                for k in range(2):
                    sp.wait_ge(Hf["y_out"][k].sem, Hf["y_out"][k].after(NW - 1))

            @block.gpsimd
            def _(pool):
                def expand(dst, x, c):
                    src = cm[:].rearrange("p b g x t -> p (b g) x t")[:, :, x, chunk_tokens(c)]
                    return nc.gpsimd.tensor_tensor(dst[:], src.unsqueeze(2).broadcast_to([P, BG, HP, CH]),
                                                   headmask[:].unsqueeze(1).unsqueeze(3).broadcast_to([P, BG, HP, CH]), ALU.mult)

                def prepare(u, c):
                    n = u * NCH + c
                    if c == 0:
                        pool.wait_ge(cm_in.sem, cm_in.after(u))
                    pool.wait_ge(S["tk_ps"].sem, S["tk_ps"].after(n, 2))
                    expand(bx[c % 2], 2, c)
                    expand(kx[c % 2], 3, c).then_inc(S["bk_x"].sem, 1)
                    pool.wait_ge(S["y_ps"].sem, S["y_ps"].after(n, NCH))
                    expand(ax[c], 0, c)
                    expand(qx[c], 1, c).then_inc(S["aq_x"].sem, 1)

                pool.wait_ge(s_c, 48)
                with pool.Fori(0, NW) as i:
                    for c in range(NCH):
                        prepare(i, c)

            @block.tensor
            def _(pe):
                mm = nc.tensor.matmul

                def prepare_products(u, c):
                    n = u * NCH + c
                    pe.wait_ge(S["bk_x"].sem, S["bk_x"].after(n))
                    pe.wait_ge(S["att_sb"].sem, S["att_sb"].after(n, 1))
                    for q in range(BG):
                        rhs = bg(cm, q)[:, 0:2, chunk_tokens(c)]
                        for x, src in enumerate((bx, kx)):
                            at = (2 * q + x) * 2 * CH
                            last = mm(AB_ps[:, at:at + 2 * CH], src[c % 2][:, q].rearrange("p h t -> p (h t)"), rhs, start=True, stop=True)
                    last.then_inc(S["ab_ps"].sem, 1)

                def prepare_transposes(u, c):
                    n = u * NCH + c
                    for src, bank, free, done in ((bx, TB_ps, "bT", "tb_ps"), (kx, TK_ps, "kT", "tk_ps")):
                        pe.wait_ge(S[free].sem, S[free].after(n, 1))
                        for q in range(BG):
                            last = nc.tensor.transpose(bank[:, q * P:(q + 1) * P], src[c % 2][:, q].rearrange("p h t -> p (h t)"), ident[:])
                        last.then_inc(S[done].sem, 1)

                def stacked(bank, lhs, rhs, first, last_):
                    for q in range(BG):
                        ins = mm(bank[:, q * HS:(q + 1) * HS], lhs(q), rhs(q), start=first and q == 0, stop=last_, skip_group_check=True)
                    return ins

                diag = lambda t: (lambda q: t[:, q].rearrange("p h t -> p (h t)"))

                def values(c):
                    return lambda q: bg(v[c // HALF], q)[:, c % HALF, :]

                def value_part(n, c):
                    pe.wait_ge(S["d_ak"].sem, S["d_ak"].after(n))
                    pe.wait_ge(S["p_sb"].sem, S["p_sb"].after(n, 1))
                    stacked(P_ps, diag(d_ak[c % 2]), values(c), True, False)

                def chunk(u, c, more):
                    n = u * NCH + c
                    s_in = state[c % 2]
                    pe.wait_ge(S["aq_x"].sem, S["aq_x"].after(n))
                    pe.wait_ge(S["s_sb"].sem, S["s_sb"].after(n, 1))
                    stacked(P_ps, diag(ax[c]), lambda q: s_in[:, q], False, True).then_inc(S["p_ps"].sem, 1)
                    pe.wait_ge(S["y_sb"].sem, S["y_sb"].after(n, 1))
                    stacked(Y_ps, diag(qx[c]), lambda q: s_in[:, q], True, False)
                    pe.wait_ge(S["d_qk"].sem, S["d_qk"].after(n))
                    stacked(Y_ps, diag(d_qk[c % 2]), values(c), False, False)
                    pe.wait_ge(S["d_t"].sem, S["d_t"].after(n))
                    pe.wait_ge(S["sa_sb"].sem, S["sa_sb"].after(n, 1))
                    pe.wait_ge(S["p_sb"].sem, S["p_sb"].after(n))
                    stacked(SA_ps, diag(d_t[c % 2]), lambda q: p_sb[:, q], True, True).then_inc(S["sa_ps"].sem, 1)
                    mm(S_ps[:, 0:BG * HS], ident[:], s_in[:].rearrange("p q i -> p (q i)"), start=True, stop=False, skip_group_check=True)
                    pe.wait_ge(S["kT"].sem, S["kT"].after(n))
                    stacked(S_ps, lambda q: kT[c][:, q], values(c), False, False)
                    if more:
                        prepare_products(u + 1, c)
                    pe.wait_ge(S["sa_sb"].sem, S["sa_sb"].after(n))
                    stacked(S_ps, lambda q: bT[c][:, q], lambda q: sa_sb[:, q], False, True).then_inc(S["s_ps"].sem, 1)
                    pe.wait_ge(S["d_qb"].sem, S["d_qb"].after(n))
                    stacked(Y_ps, diag(d_qb[c % 2]), lambda q: sa_sb[:, q], False, True).then_inc(S["y_ps"].sem, 1)
                    if c < NCH - 1 or more:
                        k = (c + 1) % NCH
                        if k % HALF == 0:
                            pe.wait_ge(Hf["v_in"][k // HALF].sem, Hf["v_in"][k // HALF].after(u + (c + 1) // NCH))
                        value_part(n + 1, k)
                    if more:
                        prepare_transposes(u + 1, c)

                for c in range(NCH):
                    prepare_products(0, c)
                    prepare_transposes(0, c)
                pe.wait_ge(Hf["v_in"][0].sem, Hf["v_in"][0].after(0))
                pe.wait_ge(s_state, 1)
                pe.wait_ge(S["aq_x"].sem, S["aq_x"].after(NCH - 1))
                value_part(0, 0)
                with pe.Fori(0, NW - 1) as i:
                    for c in range(NCH):
                        chunk(i, c, True)
                for c in range(NCH):
                    chunk(NW - 1, c, False)

            @block.scalar
            def _(act):
                def prepare(u, c):
                    n = u * NCH + c
                    act.wait_ge(S["tb_ps"].sem, S["tb_ps"].after(n))
                    act.wait_ge(S["s_ps"].sem, S["s_ps"].after(n, NCH))
                    nc.scalar.copy(bT[c][:].rearrange("p q t -> p (q t)"), TB_ps[:]).then_inc(S["bT"].sem, 1)
                    act.wait_ge(S["tk_ps"].sem, S["tk_ps"].after(n))
                    nc.scalar.copy(kT[c][:].rearrange("p q t -> p (q t)"), TK_ps[:]).then_inc(S["kT"].sem, 1)

                def head_norm(u, k):
                    act.wait_ge(Hf["dev"][k].sem, Hf["dev"][k].after(u))
                    nc.scalar.activation(ysq[:], dev[:], ACT.Square).then_inc(Hf["ysq"][k].sem, 1)
                    act.wait_ge(Hf["var"][k].sem, Hf["var"][k].after(u))
                    nc.scalar.activation(lnv[:], var[:], ACT.Ln, scale=1.0 / HS, bias=const[:, 3:4]).then_inc(Hf["lnv"][k].sem, 1)
                    act.wait_ge(Hf["lnv"][k].sem, Hf["lnv"][k].after(u))
                    nc.scalar.activation(rs[:], lnv[:], ACT.Exp, scale=-0.5).then_inc(Hf["rs"][k].sem, 1)

                def chunk(u, c, more):
                    n = u * NCH + c
                    act.wait_ge(S["sa_ps"].sem, S["sa_ps"].after(n))
                    act.wait_ge(S["y_ps"].sem, S["y_ps"].after(n, 1))
                    nc.scalar.copy(sa_sb[:].rearrange("p q i -> p (q i)"), SA_ps[:, 0:BG * HS]).then_inc(S["sa_sb"].sem, 1)
                    act.wait_ge(S["y_ps"].sem, S["y_ps"].after(n))
                    if c % HALF == 0:
                        act.wait_ge(Hf["dev"][c // HALF].sem, Hf["dev"][c // HALF].after(u, 1))
                        act.wait_ge(Hf["sum"][c // HALF].sem, Hf["sum"][c // HALF].after(u, 1))
                    nc.scalar.copy(y[c // HALF][:, c % HALF].rearrange("p q i -> p (q i)"), Y_ps[:, 0:BG * HS]).then_inc(S["y_sb"].sem, 1)
                    if more:
                        prepare(u + 1, c)
                    if c == HALF:
                        head_norm(u, 0)
                    if c == NCH - 1:
                        head_norm(u, 1)

                act.preload_act_table_set(LN_EXP)
                for c in range(NCH):
                    prepare(0, c)
                with act.Fori(0, NW - 1) as i:
                    for c in range(NCH):
                        chunk(i, c, True)
                for c in range(NCH):
                    chunk(NW - 1, c, False)

            @block.vector
            def _(dve):
                dve.wait_ge(s_c, 48)
                nc.vector.memset(state[0][:], 0.0).then_inc(s_state, 1)

                def mask_products(u, c):
                    n = u * NCH + c
                    dve.wait_ge(S["ab_ps"].sem, S["ab_ps"].after(n))
                    if c % HALF == 0:
                        dve.wait_ge(Hf["att_out"][c // HALF].sem, Hf["att_out"][c // HALF].after(u, 1))
                    dve.wait_ge(S["d_qk"].sem, S["d_qk"].after(n, NCH))
                    dve.wait_ge(S["d_qb"].sem, S["d_qb"].after(n, NCH))
                    dve.wait_ge(S["d_ak"].sem, S["d_ak"].after(n, NCH))
                    nc.vector.tensor_tensor(att[:, c].rearrange("p q x y t -> p (q x) (y t)"),
                                            AB_ps[:, 0:4 * BG * CH].rearrange("p (q t) -> p q t", q=2 * BG),
                                            causal[:].rearrange("p y t -> p (y t)").unsqueeze(1).broadcast_to([P, 2 * BG, 2 * CH]),
                                            ALU.mult).then_inc(S["att_sb"].sem, 1)

                def diagonal(dst, src, done):
                    nc.vector.tensor_tensor(dst[:], src.unsqueeze(2).broadcast_to([P, BG, HP, CH]),
                                            headmask[:].unsqueeze(1).unsqueeze(3).broadcast_to([P, BG, HP, CH]), ALU.mult
                                            ).then_inc(done.sem, 1)

                def diagonals(u, c, which):
                    n = u * NCH + c
                    k = c % 2
                    if which == 0:
                        dve.wait_ge(S["y_ps"].sem, S["y_ps"].after(n, 2))
                        dve.wait_ge(S["att_sb"].sem, S["att_sb"].after(n))
                        diagonal(d_ak[k], att[:, c, :, 1, 0, :], S["d_ak"])
                        diagonal(d_qk[k], att[:, c, :, 1, 1, :], S["d_qk"])
                    else:
                        diagonal(d_qb[k], att[:, c, :, 0, 1, :], S["d_qb"])
                        if c % HALF == 0:
                            dve.wait_ge(Hf["tt_in"][c // HALF].sem, Hf["tt_in"][c // HALF].after(u))
                        diagonal(d_t[k], tt[c // HALF][:, c % HALF], S["d_t"])

                def solve(u, k, m0, m1, wrap):
                    x = sol[k]
                    if m0 == 0:
                        dve.wait_ge(Hf["prob_in"][k].sem, Hf["prob_in"][k].after(u))
                        dve.wait_ge(Hf["inv_out"][k].sem, Hf["inv_out"][k].after(u, 1))
                        nc.vector.tensor_copy(x[:], eye[:]).then_inc(s_chain, 1)
                        chain[0] += 1
                    for m in range(m0, m1):
                        rows, cols = m + 1, CH - 1 - m
                        prod = step_[:, 0:rows * cols].rearrange("p (r t) -> p r t", r=rows)
                        dve.wait_ge(s_chain, chain[0])
                        nc.vector.tensor_tensor(prod, prob[k][:, m:m + 1, m + 1:CH].broadcast_to([P, rows, cols]),
                                                x[:, 0:rows, m:m + 1].broadcast_to([P, rows, cols]), ALU.mult).then_inc(s_chain, 1)
                        chain[0] += 1
                        dve.wait_ge(s_chain, chain[0])
                        ins = nc.vector.tensor_tensor(x[:, 0:rows, m + 1:CH], x[:, 0:rows, m + 1:CH], prod, ALU.add)
                        if m < CH - 2:
                            ins.then_inc(s_chain, 1)
                            chain[0] += 1
                        else:
                            ins.then_inc(Hf["solved"][k].sem, 1)
                            dve.sem_clear(s_chain)
                            chain[0] = 0

                def head_norm(u, k):
                    yk = y[k][:].rearrange("p c q i -> p (c q) i")
                    dve.wait_ge(S["y_sb"].sem, S["y_sb"].after(u * NCH + HALF * (k + 1) - 1))
                    nc.vector.tensor_reduce(mean[:], yk, AX.X, ALU.add).then_inc(Hf["sum"][k].sem, 1)
                    dve.wait_ge(Hf["sum"][k].sem, Hf["sum"][k].after(u))
                    nc.vector.tensor_scalar(mean16[:], mean[:], 1.0 / HS, None, ALU.mult).then_inc(Hf["mean"][k].sem, 1)
                    dve.wait_ge(Hf["mean"][k].sem, Hf["mean"][k].after(u))
                    nc.vector.tensor_tensor(dev[:], yk, mean16[:].unsqueeze(2).broadcast_to([P, HALF * BG, HS]), ALU.subtract
                                            ).then_inc(Hf["dev"][k].sem, 1)

                def head_norm_end(u, k):
                    dve.wait_ge(Hf["ysq"][k].sem, Hf["ysq"][k].after(u))
                    nc.vector.tensor_reduce(var[:], ysq[:], AX.X, ALU.add).then_inc(Hf["var"][k].sem, 1)
                    dve.wait_ge(Hf["rs"][k].sem, Hf["rs"][k].after(u))
                    dve.wait_ge(Hf["y_out"][1 - k].sem, Hf["y_out"][1 - k].after(u, 1 - k))
                    nc.vector.tensor_tensor(yn[:].rearrange("p (g cb) i -> p cb g i", g=CC), dev[:].rearrange("p (cb g) i -> p cb g i", g=CC),
                                            rs[:].rearrange("p (cb g) -> p cb g", g=CC).unsqueeze(3).broadcast_to([P, HALF * NB, CC, HS]),
                                            ALU.mult).then_inc(Hf["yn"][k].sem, 1)

                def chunk(u, c, more):
                    n = u * NCH + c
                    ahead = c < NCH - 1 or more
                    nu, ncn = (u, c + 1) if c < NCH - 1 else (u + 1, 0)
                    dve.wait_ge(S["p_ps"].sem, S["p_ps"].after(n))
                    dve.wait_ge(S["sa_ps"].sem, S["sa_ps"].after(n, 1))
                    nc.vector.tensor_copy(p_sb[:].rearrange("p q i -> p (q i)"), P_ps[:, 0:BG * HS]).then_inc(S["p_sb"].sem, 1)
                    if ahead:
                        diagonals(nu, ncn, 0)
                    if c in (1, 2):
                        solve(u, 1, *((0, 8) if c == 1 else (8, CH - 1)), c)
                    if c in (5, 6) and more:
                        solve(u + 1, 0, *((0, 8) if c == 5 else (8, CH - 1)), c)
                    dve.wait_ge(S["s_ps"].sem, S["s_ps"].after(n))
                    dve.wait_ge(S["y_ps"].sem, S["y_ps"].after(n, 1))
                    nc.vector.tensor_tensor(state[(c + 1) % 2][:], S_ps[:, 0:BG * HS].rearrange("p (q i) -> p q i", q=BG),
                                            gl[c // HALF][:].rearrange("p b g c -> p (b g) c")[:, :, c % HALF:c % HALF + 1]
                                            .broadcast_to([P, BG, HS]), ALU.mult).then_inc(S["s_sb"].sem, 1)
                    if more:
                        mask_products(u + 1, c)
                    if ahead:
                        diagonals(nu, ncn, 1)
                    if c == HALF:
                        head_norm(u, 0)
                        head_norm_end(u, 0)
                    if c == NCH - 1:
                        head_norm(u, 1)
                        head_norm_end(u, 1)

                for c in range(NCH):
                    mask_products(0, c)
                dve.wait_ge(Hf["v_in"][0].sem, Hf["v_in"][0].after(0))
                diagonals(0, 0, 0)
                solve(0, 0, 0, CH - 1, -1)
                diagonals(0, 0, 1)
                with dve.Fori(0, NW - 1) as i:
                    for c in range(NCH):
                        chunk(i, c, True)
                for c in range(NCH):
                    chunk(NW - 1, c, False)


def gate_stage(nc, persist, a, T):
    NW = T // P
    SW = 2
    modc, rows, vec, const, ident = (persist[k] for k in ("modc", "rows", "vec", "const", "ident"))
    streams = [(w, b) for w in range(SW) for b in range(NB)]
    with ExitStack() as ctx:
        sb = lambda n, s: [ctx.enter_context(nc.sbuf_tensor(f"ga_{n}{k}", s, F32)) for k in range(len(streams))]
        wo = ctx.enter_context(nc.sbuf_tensor("ga_wo", [P, CC, C], F32))
        wos = [ctx.enter_context(nc.sbuf_tensor(f"ga_wos{b}", [P, CC, C], F32)) for b in range(NB)]
        zero = ctx.enter_context(nc.sbuf_tensor("ga_zero", [P, CC, 1], F32))
        pause = ctx.enter_context(nc.sbuf_tensor("ga_pause", [P, len(streams)], F32))
        yt, gr, xt = sb("yt", [P, C]), sb("gr", [P, 2, C]), sb("xt", [P, C])
        yl, z1, z, xa = sb("yl", [P, C]), sb("z1", [P, C]), sb("z", [P, C]), sb("xa", [P, C])
        st, mv, lnv, rstd = sb("st", [P, 6]), sb("mv", [P, 2]), sb("lnv", [P, 1]), sb("rstd", [P, 1])
        xn, h0 = sb("xn", [P, C]), sb("h0", [P, C])
        bank = [[ctx.enter_context(nc.psum_tensor(f"ga{n}{k}", [P, 512], F32)) for n in "AB"] for k in range(len(streams))]
        S = signals(nc, ctx, "y_in:128 gr_in:16 x_in:16 yT yl z1 z out_ps xa stats mean_var ln_var rstd xn xT h0 xa_out:16 h0_out:16",
                    len(streams), "ga")
        s_c, s_ws, s_zero = (ctx.enter_context(nc.semaphore(f"ga_{n}")) for n in ("const", "wos", "zero"))
        start_signals(nc, (s_c, s_ws, s_zero), S)
        each = lambda: enumerate(streams)
        with nc.Block() as block:
            @block.sync
            def _(sp):
                sp.dma_start(wo[:], a["wo_attn"]).then_inc(s_c, 16)

                def load_y(i):
                    for k, (w, b) in each():
                        sp.wait_ge(S["yT"][k].sem, S["yT"][k].after(i, 1))
                        for c in range(NCH):
                            sp.dma_start(yt[k][c * CH:(c + 1) * CH, :].rearrange("t (g h i) -> t g h i", g=CC, h=HP),
                                         a["y_stack"][bass.ds(i * SW + w, 1), c * 2 // NCH].rearrange(
                                             "o (h t) (g c b i) -> (o c) b t g h i", t=CH, b=NB, g=CC, i=HS)[c % (NCH // 2), b]
                                         ).then_inc(S["y_in"][k].sem, 16)

                def load_gr(i):
                    for k, (w, b) in each():
                        sp.wait_ge(S["z"][k].sem, S["z"][k].after(i, 1))
                        sp.dma_start(gr[k][:], a["gr"][b, bass.ds(i * SW + w, 1)].rearrange("o p (x n) -> (o p) x n", x=2)
                                     ).then_inc(S["gr_in"][k].sem, 16)

                def load_x(i):
                    for k, (w, b) in each():
                        sp.wait_ge(S["xa"][k].sem, S["xa"][k].after(i, 1))
                        sp.dma_start(xt[k][:], a["x"][b, bass.ds((i * SW + w) * P, P), :]).then_inc(S["x_in"][k].sem, 16)

                def body(i, more):
                    if more:
                        load_y(i + 1)
                        load_gr(i + 1)
                        load_x(i + 1)
                    for k, (w, b) in each():
                        sp.wait_ge(S["xa"][k].sem, S["xa"][k].after(i))
                        sp.dma_start(a["xa"][b, bass.ds((i * SW + w) * P, P), :], xa[k][:]).then_inc(S["xa_out"][k].sem, 16)
                    for k, (w, b) in each():
                        sp.wait_ge(S["h0"][k].sem, S["h0"][k].after(i))
                        sp.dma_start(a["h0"][b, :, :, bass.ds((i * SW + w) * P + 1, P)], h0[k][:].rearrange("p (c t) -> p c t", c=CC)
                                     ).then_inc(S["h0_out"][k].sem, 16)

                load_y(0)
                load_gr(0)
                load_x(0)
                with sp.Fori(0, NW // SW - 1) as i:
                    body(i, True)
                body(NW // SW - 1, False)
                for k, _ in each():
                    sp.wait_ge(S["xa_out"][k].sem, S["xa_out"][k].after(NW // SW - 1))
                    sp.wait_ge(S["h0_out"][k].sem, S["h0_out"][k].after(NW // SW - 1))

            @block.scalar
            def _(act):
                act.preload_act_table_set(LN_EXP)
                act.wait_ge(s_zero, 1)
                for b in range(NB):
                    act.dma_start(a["h0"][b, :, :, 0:1], zero[:], allow_slow_non_contiguous=True).then_inc(s_zero, 16)
                with act.Fori(0, NW // SW) as i:
                    for k, (w, b) in each():
                        act.wait_ge(S["yT"][k].sem, S["yT"][k].after(i))
                        act.wait_ge(S["z1"][k].sem, S["z1"][k].after(i, 1))
                        for c in range(CC):
                            last = nc.scalar.activation(yl[k][:, c * P:(c + 1) * P], bank[k][0][:, c * P:(c + 1) * P], ACT.Identity,
                                                        scale=vec[:, 10, c:c + 1], bias=vec[:, 11, c:c + 1])
                        last.then_inc(S["yl"][k].sem, 1)
                    for k, (w, b) in each():
                        act.wait_ge(S["mean_var"][k].sem, S["mean_var"][k].after(i))
                        nc.scalar.activation(lnv[k][:], mv[k][:, 1:2], ACT.Ln, bias=const[:, 0:1]).then_inc(S["ln_var"][k].sem, 1)
                        act.wait_ge(S["ln_var"][k].sem, S["ln_var"][k].after(i))
                        act.wait_ge(S["xn"][k].sem, S["xn"][k].after(i, 1))
                        nc.scalar.activation(rstd[k][:], lnv[k][:], ACT.Exp, scale=-0.5).then_inc(S["rstd"][k].sem, 1)
                    for k, (w, b) in each():
                        act.wait_ge(S["xT"][k].sem, S["xT"][k].after(i))
                        act.wait_ge(S["h0_out"][k].sem, S["h0_out"][k].after(i, 1))
                        for c in range(CC):
                            last = nc.scalar.activation(h0[k][:, c * P:(c + 1) * P], bank[k][1][:, c * P:(c + 1) * P], ACT.Identity,
                                                        scale=modc[:, 16 + 2 * c + b:17 + 2 * c + b],
                                                        bias=modc[:, 12 + 2 * c + b:13 + 2 * c + b])
                        last.then_inc(S["h0"][k].sem, 1)
                act.wait_ge(s_zero, 1 + 16 * NB)

            @block.vector
            def _(dve):
                nc.vector.memset(zero[:], 0.0).then_inc(s_zero, 1)
                dve.wait_ge(s_c, 16)
                for b in range(NB):
                    last = nc.vector.tensor_tensor(wos[b][:], wo[:], rows[:, b * C:(b + 1) * C].unsqueeze(1).broadcast_to([P, CC, C]), ALU.mult)
                last.then_inc(s_ws, 1)
                with dve.Fori(0, NW // SW) as i:
                    for k, (w, b) in each():
                        dve.wait_ge(S["yl"][k].sem, S["yl"][k].after(i))
                        dve.wait_ge(S["gr_in"][k].sem, S["gr_in"][k].after(i))
                        dve.wait_ge(S["z"][k].sem, S["z"][k].after(i, 1))
                        nc.vector.tensor_tensor(z1[k][:], yl[k][:], gr[k][:, 1], ALU.add).then_inc(S["z1"][k].sem, 1)
                    for k, (w, b) in each():
                        dve.wait_ge(S["z1"][k].sem, S["z1"][k].after(i))
                        dve.wait_ge(S["out_ps"][k].sem, S["out_ps"][k].after(i, 1))
                        nc.vector.tensor_tensor(z[k][:], z1[k][:], gr[k][:, 0], ALU.mult).then_inc(S["z"][k].sem, 1)
                    for k, (w, b) in each():
                        dve.wait_ge(S["out_ps"][k].sem, S["out_ps"][k].after(i))
                        dve.wait_ge(S["x_in"][k].sem, S["x_in"][k].after(i))
                        dve.wait_ge(S["xa_out"][k].sem, S["xa_out"][k].after(i, 1))
                        nc.vector.tensor_tensor(xa[k][:], bank[k][0][:, C:2 * C], xt[k][:], ALU.add).then_inc(S["xa"][k].sem, 1)
                    for k, (w, b) in each():
                        dve.wait_ge(S["xa"][k].sem, S["xa"][k].after(i))
                        nc.vector.bn_stats(st[k][:], xa[k][:]).then_inc(S["stats"][k].sem, 1)
                    for k, (w, b) in each():
                        dve.wait_ge(S["stats"][k].sem, S["stats"][k].after(i))
                        dve.wait_ge(S["ln_var"][k].sem, S["ln_var"][k].after(i, 1))
                        nc.vector.memset(pause[:, k:k + 1], 0.0)
                        nc.vector.bn_aggr(mv[k][:], st[k][:]).then_inc(S["mean_var"][k].sem, 1)
                    for k, (w, b) in each():
                        dve.wait_ge(S["rstd"][k].sem, S["rstd"][k].after(i))
                        dve.wait_ge(S["xT"][k].sem, S["xT"][k].after(i, 1))
                        nc.vector.tensor_scalar(xn[k][:], xa[k][:], mv[k][:, 0:1], rstd[k][:], ALU.subtract, ALU.mult
                                                ).then_inc(S["xn"][k].sem, 1)

            @block.tensor
            def _(pe):
                pe.wait_ge(s_ws, 1)
                with pe.Fori(0, NW // SW) as i:
                    for k, (w, b) in each():
                        pe.wait_ge(S["y_in"][k].sem, S["y_in"][k].after(i))
                        pe.wait_ge(S["yl"][k].sem, S["yl"][k].after(i, 1))
                        pe.wait_ge(S["xa"][k].sem, S["xa"][k].after(i, 1))
                        for c in range(CC):
                            last = nc.tensor.transpose(bank[k][0][:, c * P:(c + 1) * P], yt[k][:, c * P:(c + 1) * P], ident[:])
                        last.then_inc(S["yT"][k].sem, 1)
                    for k, (w, b) in each():
                        pe.wait_ge(S["z"][k].sem, S["z"][k].after(i))
                        for c in range(CC):
                            last = nc.tensor.matmul(bank[k][0][:, C:2 * C], z[k][:, c * P:(c + 1) * P], wos[b][:, c, :],
                                                    start=(c == 0), stop=(c == CC - 1))
                        last.then_inc(S["out_ps"][k].sem, 1)
                    for k, (w, b) in each():
                        pe.wait_ge(S["xn"][k].sem, S["xn"][k].after(i))
                        pe.wait_ge(S["h0"][k].sem, S["h0"][k].after(i, 1))
                        for c in range(CC):
                            last = nc.tensor.transpose(bank[k][1][:, c * P:(c + 1) * P], xn[k][:, c * P:(c + 1) * P], ident[:])
                        last.then_inc(S["xT"][k].sem, 1)


def local_stage(nc, persist, a, T, layer):
    NW = T // P
    NHP = HEADS // 2
    LAST = layer == 1
    rows, const, ident = (persist[k] for k in ("rows", "const", "ident"))
    src = a["h1"] if LAST else a["h0"]
    G = ((0, 1), (2, 3), (4, 5))
    with ExitStack() as ctx:
        one = lambda n, s, d=F32: ctx.enter_context(nc.sbuf_tensor(f"l{layer}_{n}", s, d))
        two = lambda n, s, d=F32: [one(f"{n}{k}", s, d) for k in range(2)]
        wqkv, wo = one("wqkv", [P, CC, 3 * INNER]), one("wo", [P, NHP, C])
        w1, w2 = one("w1", [P, CC, 2, MT * MW]), one("w2", [MW, MT, C])
        b1, b1c, lngb = one("b1", [MW, 2, MT]), one("b1c", [MW, 2, MT]), one("lngb", [P, 3, CC])
        qks, rot, tab = one("qks", [P, 4, DH]), two("rot", [P, 4, DH]), two("tab", [P, 4, DH])
        wm = one("wm", [P, 2 * P])
        identb, mean_w = one("identb", [P, P], BF16), one("mean_w", [P, P])
        mask = [two(f"mask{s}_", [P, 2, P], BF16) for s in range(NB)]
        hT = [two(f"h{s}_", [P, CC, P + 1]) for s in range(NB)]
        x1 = [two(f"x1{s}_", [P, CC, P + 1]) for s in range(NB)]
        sqq, sqk, q1, q2, qr, kn, k1, k2, kr = (two(n, [P, HEADS, DH]) for n in "sqq sqk q1 q2 qr kn k1 k2 kr".split())
        ss, ssc, lnn, rn = (two(n, [P, 2 * HEADS]) for n in ("ss", "ssc", "lnn", "rn"))
        rq8, mx, nb, sums, rinv = (two(n, [P, HEADS]) for n in ("rq8", "mx", "nb", "sums", "rinv"))
        qz, kT = two("qz", [P, HEADS, P]), two("kT", [P, NHP, 2, P])
        V, prob, pT = two("V", [P, 2, HEADS, DH]), two("prob", [P, HEADS, 2 * P]), two("pT", [P, HEADS, 2, P])
        o, oT = two("o", [P, HEADS, DH]), two("oT", [P, NHP, P])
        dev, dsq, hn, hout = (two(n, [P, CC, P]) for n in ("dev", "dsq", "hn", "hout"))
        lnv, rstd = two("lnv", [P, P]), two("rstd", [P, P])
        gel, hid = two("gel", [MW, MT, P]), two("hid", [MW, MT, P])
        if LAST:
            xat, t1, outt = two("xat", [P, C]), two("t1", [P, C]), two("outt", [P, C])
        else:
            zero = one("zero", [P, CC, 1])
        bank = [[ctx.enter_context(nc.psum_tensor(f"l{layer}{n}{s}", [P, 512], F32)) for n in "ABCD"] for s in range(NB)]
        sems = {n: ctx.enter_context(nc.semaphore(f"l{layer}_{n}")) for n in ("w", "set", "prep", "bias", "zero")}
        R = signals(nc, ctx, "rot_in:16 tab", 1, f"l{layer}r")
        S = signals(nc, ctx, "h_in:16 q_ps k_ps v_ps qsq ksq v_sb ss clamped ln_n rn rq8 kn qm qr k12 kr qT_ps kT_ps qz kT "
                    "mask0 pv o oT_ps oT wo_ps carry x1 mean_ps dev dsq var_ps ln_v rstd hn w2_ps hout yT t1 sum_ps "
                    "xa_in:16 outt out:16", 2, f"l{layer}")
        Q = signals(nc, ctx, "sc mx nb exp pt_ps pT", 2, f"l{layer}q", ahead=2 * NHP)
        M = signals(nc, ctx, "w1_ps gel hid", 2, f"l{layer}m", ahead=6)
        start_signals(nc, tuple(sems.values()), R, S, Q, M)
        rot_in, tab_made = R["rot_in"][0], R["tab"][0]
        flat = lambda t: t[:].rearrange("p c t -> p (c t)")
        shifted = lambda t: t[:].rearrange("p c t -> p (c t)")[:, 1:CC * P + 1]
        heads = lambda t, s: t[s][:].unsqueeze(2).broadcast_to([P, HEADS, DH])

        def program(att, mlp, prologue):
            def both(sa, ua, wa, sm, um, wm_):
                att(sa, ua, wa, 0)
                mlp(sm, um, wm_, 0)
                att(sa, ua, wa, 1)
                mlp(sm, um, wm_, 1)
                att(sa, ua, wa, 2)
                mlp(sm, um, wm_, 2)
                att(sa, ua, wa, 3)

            def body(i, more):
                for w in range(2):
                    u = 2 * i + w
                    both(1, u, w, 0, u, w)
                    if w == 0 or more:
                        both(0, u + 1, 1 - w, 1, u, w)
                    else:
                        for part in range(3):
                            mlp(1, u, w, part)

            prologue()
            for part in range(4):
                att(0, 0, 0, part)
            return body

        def run(eng, att, mlp, prologue=lambda: None):
            body = program(att, mlp, prologue)
            with eng.Fori(0, NW // 2 - 1) as i:
                body(i, True)
            body(NW // 2 - 1, False)

        with nc.Block() as block:
            @block.sync
            def _(sp):
                def att(s, u, w, part):
                    if part == 0:
                        sp.wait_ge(S["x1"][s].sem, S["x1"][s].after(u, 2))
                        sp.wait_ge(S["h_in"][s].sem, S["h_in"][s].after(u, 1))
                        sp.dma_start(hT[s][w][:], src[s, :, :, bass.ds(u * P, P + 1)]).then_inc(S["h_in"][s].sem, 16)
                        if s == 0:
                            sp.wait_ge(tab_made.sem, tab_made.after(u, 2))
                            sp.wait_ge(rot_in.sem, rot_in.after(u, 1))
                            sp.dma_start(rot[w][:], a["rotary"][bass.ds(u * P, P)]).then_inc(rot_in.sem, 16)

                def mlp(s, u, w, part):
                    if part == 0 and LAST:
                        sp.wait_ge(S["outt"][s].sem, S["outt"][s].after(u, 1))
                        sp.dma_start(xat[s][:], a["xa"][s, bass.ds(u * P, P), :]).then_inc(S["xa_in"][s].sem, 16)

                def prologue():
                    for dst, name in ((wqkv, "wqkv"), (wo, "wo"), (w1, "w1"), (w2, "w2"), (b1, "b1"), (lngb, "ln_gb"), (qks, "qk_scale")):
                        view = a[name][layer]
                        d = dst[:].rearrange("p c x n -> p c (x n)") if name == "w1" else dst[:]
                        sp.dma_start(d, view).then_inc(sems["w"], 16)
                    sp.dma_start(wm[:], a["winmask"]).then_inc(sems["w"], 16)

                run(sp, att, mlp, prologue)

            @block.gpsimd
            def _(pool):
                tt = nc.gpsimd.tensor_tensor

                def prologue():
                    for s in range(NB):
                        for t in (qz[s], kT[s], V[s]):
                            nc.gpsimd.memset(t[:], 0.0)
                        nc.gpsimd.memset(x1[s][1][:], 0.0)
                        nc.gpsimd.memset(mask[s][0][:], MASKED)
                    if not LAST:
                        nc.gpsimd.memset(zero[:], 0.0)
                    nc.gpsimd.memset(mean_w[:], 1.0 / C).then_inc(sems["set"], 1)
                    pool.wait_ge(sems["w"], 128)

                def att(s, u, w, part):
                    if part == 0 and s == 0:
                            pool.wait_ge(rot_in.sem, rot_in.after(u))
                            for b in range(NB):
                                pool.wait_ge(S["qm"][b].sem, S["qm"][b].after(u, 2))
                                pool.wait_ge(S["kr"][b].sem, S["kr"][b].after(u, 2))
                            tt(tab[w][:], rot[w][:], qks[:], ALU.mult).then_inc(tab_made.sem, 1)
                    if part == 1:
                        pool.wait_ge(S["kn"][s].sem, S["kn"][s].after(u))
                        pool.wait_ge(tab_made.sem, tab_made.after(u))
                        lo, hi = slice(0, DH // 2), slice(DH // 2, DH)
                        wide = lambda j, d: tab[w][:, j:j + 1, d].broadcast_to([P, HEADS, d.stop - d.start])
                        pool.wait_ge(S["kr"][s].sem, S["kr"][s].after(u, 1))
                        tt(k1[s][:], kn[s][:], wide(2, slice(0, DH)), ALU.mult)
                        tt(k2[s][:, :, lo], kn[s][:, :, hi], wide(3, lo), ALU.mult)
                        tt(k2[s][:, :, hi], kn[s][:, :, lo], wide(3, hi), ALU.mult).then_inc(S["k12"][s].sem, 1)
                        pool.wait_ge(S["k12"][s].sem, S["k12"][s].after(u))
                        pool.wait_ge(S["kT_ps"][s].sem, S["kT_ps"][s].after(u, 1))
                        tt(kr[s][:], k1[s][:], k2[s][:], ALU.add).then_inc(S["kr"][s].sem, 1)

                def mlp(s, u, w, part):
                    if part == 0:
                        pool.wait_ge(S["dev"][s].sem, S["dev"][s].after(u))
                        pool.wait_ge(S["rstd"][s].sem, S["rstd"][s].after(u))
                        pool.wait_ge(M["w1_ps"][s].sem, M["w1_ps"][s].after(u * 3 - 1))
                        tt(hn[s][:], dev[s][:], rstd[s][:].unsqueeze(1).broadcast_to([P, CC, P]), ALU.mult).then_inc(S["hn"][s].sem, 1)
                    if part == 2 and LAST:
                        pool.wait_ge(S["t1"][s].sem, S["t1"][s].after(u))
                        pool.wait_ge(S["xa_in"][s].sem, S["xa_in"][s].after(u))
                        pool.wait_ge(S["out"][s].sem, S["out"][s].after(u, 1))
                        tt(outt[s][:], t1[s][:], xat[s][:], ALU.add).then_inc(S["outt"][s].sem, 1)

                run(pool, att, mlp, prologue)

            @block.vector
            def _(dve):
                tt = nc.vector.tensor_tensor

                def prologue():
                    dve.wait_ge(sems["w"], 128)
                    dve.wait_ge(sems["bias"], 1)
                    dve.wait_ge(sems["set"], 1)
                    tt(b1c[:], bank[0][0][0:MW, 0:2 * MT].rearrange("p (x m) -> p x m", x=2), b1[:], ALU.add)
                    for k in range(CC):
                        nc.vector.tensor_scalar(w1[:, k], w1[:, k], lngb[:, 0, k:k + 1], None, ALU.mult)
                    for s in range(NB):
                        nc.vector.tensor_copy(mask[s][0][:, 0, :], wm[:, P:2 * P])
                        last = nc.vector.tensor_copy(mask[s][1][:].rearrange("p x n -> p (x n)"), wm[:])
                    last.then_inc(sems["prep"], 1)
                    dve.wait_ge(sems["prep"], 2)

                def att(s, u, w, part):
                    A, B, Cb, D = bank[s]
                    if part == 0:
                        dve.wait_ge(S["qsq"][s].sem, S["qsq"][s].after(u))
                        dve.wait_ge(S["clamped"][s].sem, S["clamped"][s].after(u, 1))
                        nc.vector.tensor_reduce(ss[s][:, 0:HEADS], sqq[s][:], AX.X, ALU.add)
                        dve.wait_ge(S["ksq"][s].sem, S["ksq"][s].after(u))
                        nc.vector.tensor_reduce(ss[s][:, HEADS:], sqk[s][:], AX.X, ALU.add).then_inc(S["ss"][s].sem, 1)
                        dve.wait_ge(S["ss"][s].sem, S["ss"][s].after(u))
                        dve.wait_ge(S["ln_n"][s].sem, S["ln_n"][s].after(u, 1))
                        nc.vector.tensor_scalar(ssc[s][:], ss[s][:], 1e-24, None, ALU.max).then_inc(S["clamped"][s].sem, 1)
                        dve.wait_ge(tab_made.sem, tab_made.after(u))
                        dve.wait_ge(S["qr"][s].sem, S["qr"][s].after(u, 1))
                        q = A[:].rearrange("p (h d) -> p h d", h=HEADS)
                        lo, hi = slice(0, DH // 2), slice(DH // 2, DH)
                        wide = lambda j, d: tab[w][:, j:j + 1, d].broadcast_to([P, HEADS, d.stop - d.start])
                        tt(q1[s][:], q, wide(0, slice(0, DH)), ALU.mult)
                        tt(q2[s][:, :, lo], q[:, :, hi], wide(1, lo), ALU.mult)
                        tt(q2[s][:, :, hi], q[:, :, lo], wide(1, hi), ALU.mult).then_inc(S["qm"][s].sem, 1)
                        dve.wait_ge(S["rn"][s].sem, S["rn"][s].after(u))
                        dve.wait_ge(S["kr"][s].sem, S["kr"][s].after(u, 1))
                        tt(kn[s][:], B[:].rearrange("p (h d) -> p h d", h=HEADS),
                           rn[s][:, HEADS:].unsqueeze(2).broadcast_to([P, HEADS, DH]), ALU.mult).then_inc(S["kn"][s].sem, 1)
                        dve.wait_ge(Q["exp"][s].sem, Q["exp"][s].after(u * NHP - 1))
                        nc.vector.tensor_scalar(rq8[s][:], rn[s][:, 0:HEADS], 8.0, None, ALU.mult).then_inc(S["rq8"][s].sem, 1)
                        dve.wait_ge(S["qm"][s].sem, S["qm"][s].after(u))
                        dve.wait_ge(S["qT_ps"][s].sem, S["qT_ps"][s].after(u, 1))
                        tt(qr[s][:], q1[s][:], q2[s][:], ALU.add).then_inc(S["qr"][s].sem, 1)
                    if part == 2:
                        dve.wait_ge(S["kT_ps"][s].sem, S["kT_ps"][s].after(u))
                        dve.wait_ge(Q["sc"][s].sem, Q["sc"][s].after(u * NHP - 1))
                        nc.vector.tensor_copy(kT[s][:, :, w, :], A[:].rearrange("p (h t) -> p h t", h=NHP)).then_inc(S["kT"][s].sem, 1)
                    if part == 3:
                        for hp in range(NHP + 1):
                            n = u * NHP + hp
                            if hp < NHP:
                                two_ = slice(2 * hp, 2 * hp + 2)
                                dve.wait_ge(Q["sc"][s].sem, Q["sc"][s].after(n))
                                dve.wait_ge(Q["nb"][s].sem, Q["nb"][s].after(n, NHP))
                                nc.vector.tensor_reduce(mx[s][:, two_], bank[s][1 + hp % 2][:].rearrange("p (h n) -> p h n", h=2),
                                                        AX.X, ALU.max).then_inc(Q["mx"][s].sem, 1)
                                dve.wait_ge(Q["mx"][s].sem, Q["mx"][s].after(n))
                                dve.wait_ge(S["rq8"][s].sem, S["rq8"][s].after(u))
                                dve.wait_ge(Q["exp"][s].sem, Q["exp"][s].after(n, NHP))
                                nc.vector.scalar_tensor_tensor(out=nb[s][:, two_], in0=mx[s][:, two_], scalar=-1.0, in1=rq8[s][:, two_],
                                                               op0=ALU.mult, op1=ALU.mult).then_inc(Q["nb"][s].sem, 1)
                            if hp > 0 and hp % 2 == 0:
                                evacuate(dve, nc.vector.tensor_copy, s, u, hp - 1)
                        if w == 0:
                            dve.wait_ge(Q["sc"][s].sem, Q["sc"][s].after(u * NHP + NHP - 1))
                            nc.vector.tensor_copy(mask[s][0][:, 1, :], wm[:, 0:P]).then_inc(S["mask0"][s].sem, 2)
                        dve.wait_ge(Q["exp"][s].sem, Q["exp"][s].after(u * NHP + NHP - 1))
                        dve.wait_ge(S["o"][s].sem, S["o"][s].after(u, 1))
                        nc.vector.reciprocal(rinv[s][:], sums[s][:]).then_inc(S["sum_ps"][s].sem, 1)
                        dve.wait_ge(S["sum_ps"][s].sem, S["sum_ps"][s].after(u))
                        dve.wait_ge(S["pv"][s].sem, S["pv"][s].after(u))
                        dve.wait_ge(S["oT_ps"][s].sem, S["oT_ps"][s].after(u, 1))
                        tt(o[s][:], D[:].rearrange("p (h d) -> p h d", h=HEADS), heads(rinv, s), ALU.mult).then_inc(S["o"][s].sem, 1)
                        dve.wait_ge(S["x1"][s].sem, S["x1"][s].after(u, 1))
                        dve.wait_ge(S["dev"][s].sem, S["dev"][s].after(u, 2))
                        dve.wait_ge(S["mean_ps"][s].sem, S["mean_ps"][s].after(u, 2))
                        nc.vector.tensor_copy(x1[s][w][:, :, 0:1], x1[s][1 - w][:, :, P:P + 1]).then_inc(S["carry"][s].sem, 1)
                        dve.wait_ge(S["wo_ps"][s].sem, S["wo_ps"][s].after(u))
                        dve.wait_ge(S["hout"][s].sem, S["hout"][s].after(u, 2))
                        dve.wait_ge(S["carry"][s].sem, S["carry"][s].after(u, 1))
                        tt(x1[s][w][:, :, 1:], B[:, 0:C].rearrange("p (c t) -> p c t", c=CC), hT[s][w][:, :, 1:], ALU.add
                           ).then_inc(S["x1"][s].sem, 1)

                def evacuate(eng, copy, s, u, hp):
                    eng.wait_ge(Q["pt_ps"][s].sem, Q["pt_ps"][s].after(u * NHP + hp))
                    eng.wait_ge(S["pv"][s].sem, S["pv"][s].after(u, 1))
                    copy(pT[s][:, 2 * hp:2 * hp + 2].rearrange("p h x t -> p (h x t)"), bank[s][0][:]).then_inc(Q["pT"][s].sem, 1)

                def mlp(s, u, w, part):
                    A, B, Cb, D = bank[s]
                    if part == 0:
                        dve.wait_ge(S["mean_ps"][s].sem, S["mean_ps"][s].after(u))
                        dve.wait_ge(S["hn"][s].sem, S["hn"][s].after(u, 1))
                        dve.wait_ge(S["dsq"][s].sem, S["dsq"][s].after(u, 1))
                        dve.wait_ge(S["x1"][s].sem, S["x1"][s].after(u))
                        dve.wait_ge(S["carry"][s].sem, S["carry"][s].after(u))
                        tt(dev[s][:], shifted(x1[s][w]).rearrange("p (c t) -> p c t", c=CC),
                           Cb[:, 0:P].unsqueeze(1).broadcast_to([P, CC, P]), ALU.subtract).then_inc(S["dev"][s].sem, 1)
                    if part == 1:
                        for j, tiles in enumerate(G):
                            n = 3 * u + j
                            dve.wait_ge(M["gel"][s].sem, M["gel"][s].after(n))
                            dve.wait_ge(S["w2_ps"][s].sem, S["w2_ps"][s].after(u, 1))
                            for x, m in enumerate(tiles):
                                last = nc.vector.scalar_tensor_tensor(out=hid[s][:, m], in0=bank[s][j][0:MW, 2 * x * P:(2 * x + 1) * P],
                                                                      scalar=b1c[:, 0, m:m + 1], in1=gel[s][:, m], op0=ALU.add, op1=ALU.mult)
                            last.then_inc(M["hid"][s].sem, 1)
                    if part == 2:
                        dve.wait_ge(S["w2_ps"][s].sem, S["w2_ps"][s].after(u))
                        dve.wait_ge(S["yT" if LAST else "out"][s].sem, S["yT" if LAST else "out"][s].after(u, 1))
                        for c in range(CC):
                            last = nc.vector.scalar_tensor_tensor(out=hout[s][:, c], in0=D[:, c * P:(c + 1) * P], scalar=lngb[:, 2, c:c + 1],
                                                                  in1=x1[s][w][:, c, 1:], op0=ALU.add, op1=ALU.add)
                        last.then_inc(S["hout"][s].sem, 1)
                        if LAST:
                            dve.wait_ge(S["yT"][s].sem, S["yT"][s].after(u))
                            dve.wait_ge(S["outt"][s].sem, S["outt"][s].after(u, 1))
                            tt(t1[s][:], D[:, C:2 * C], rows[:, (2 + s) * C:(3 + s) * C], ALU.mult).then_inc(S["t1"][s].sem, 1)

                run(dve, att, mlp, prologue)

            @block.scalar
            def _(act):
                def prologue():
                    act.wait_ge(sems["w"], 128)
                    act.wait_ge(sems["set"], 1)
                    nc.scalar.copy(identb[:], ident[:]).then_inc(sems["prep"], 1)
                    if not LAST:
                        for b in range(NB):
                            act.dma_start(a["h1"][b, :, :, 0:1], zero[:], allow_slow_non_contiguous=True).then_inc(sems["zero"], 16)
                        act.wait_ge(sems["zero"], 16 * NB)

                def evacuate(s, u, hp):
                    act.wait_ge(Q["pt_ps"][s].sem, Q["pt_ps"][s].after(u * NHP + hp))
                    act.wait_ge(S["pv"][s].sem, S["pv"][s].after(u, 1))
                    nc.scalar.copy(pT[s][:, 2 * hp:2 * hp + 2].rearrange("p h x t -> p (h x t)"), bank[s][0][:]).then_inc(Q["pT"][s].sem, 1)

                def att(s, u, w, part):
                    A, B, Cb, D = bank[s]
                    if part == 0:
                        act.preload_act_table_set(LN_EXP)
                        act.wait_ge(S["q_ps"][s].sem, S["q_ps"][s].after(u))
                        act.wait_ge(S["ss"][s].sem, S["ss"][s].after(u, 1))
                        nc.scalar.activation(sqq[s][:].rearrange("p h d -> p (h d)"), A[:], ACT.Square).then_inc(S["qsq"][s].sem, 1)
                        act.wait_ge(S["k_ps"][s].sem, S["k_ps"][s].after(u))
                        nc.scalar.activation(sqk[s][:].rearrange("p h d -> p (h d)"), B[:], ACT.Square).then_inc(S["ksq"][s].sem, 1)
                        act.wait_ge(S["v_ps"][s].sem, S["v_ps"][s].after(u))
                        act.wait_ge(S["pv"][s].sem, S["pv"][s].after(u, 1))
                        nc.scalar.copy(V[s][:, w].rearrange("p h d -> p (h d)"), Cb[:]).then_inc(S["v_sb"][s].sem, 1)
                        act.wait_ge(S["clamped"][s].sem, S["clamped"][s].after(u))
                        nc.scalar.activation(lnn[s][:], ssc[s][:], ACT.Ln, scale=LNSCALE).then_inc(S["ln_n"][s].sem, 1)
                        act.wait_ge(S["ln_n"][s].sem, S["ln_n"][s].after(u))
                        act.wait_ge(S["kn"][s].sem, S["kn"][s].after(u, 1))
                        act.wait_ge(S["rq8"][s].sem, S["rq8"][s].after(u, 1))
                        nc.scalar.activation(rn[s][:], lnn[s][:], ACT.Exp, scale=-0.5, bias=const[:, 2:3]).then_inc(S["rn"][s].sem, 1)
                    if part == 2:
                        act.wait_ge(S["qT_ps"][s].sem, S["qT_ps"][s].after(u))
                        act.wait_ge(Q["sc"][s].sem, Q["sc"][s].after(u * NHP - 1))
                        qT = D[:].rearrange("p (h t) -> p h t", h=NHP)
                        nc.scalar.copy(qz[s][0:DH, 0::2, :], qT[0:DH])
                        nc.scalar.copy(qz[s][DH:P, 1::2, :], qT[DH:P]).then_inc(S["qz"][s].sem, 1)
                        act.preload_act_table_set(LN_EXP)
                    if part == 3:
                        for hp in range(NHP + 1):
                            n = u * NHP + hp
                            if hp < NHP:
                                act.wait_ge(Q["nb"][s].sem, Q["nb"][s].after(n))
                                act.wait_ge(Q["pt_ps"][s].sem, Q["pt_ps"][s].after(n, NHP))
                                if hp == 0:
                                    act.wait_ge(S["sum_ps"][s].sem, S["sum_ps"][s].after(u, 1))
                                for x in range(2):
                                    h = 2 * hp + x
                                    last = nc.scalar.activation(prob[s][:, h], bank[s][1 + hp % 2][:, 2 * P * x:2 * P * (x + 1)], ACT.Exp,
                                                                scale=rq8[s][:, h:h + 1], bias=nb[s][:, h:h + 1],
                                                                accum_out=sums[s][:, h:h + 1])
                                last.then_inc(Q["exp"][s].sem, 1)
                            if hp % 2 == 1:
                                evacuate(s, u, hp - 1)
                        act.wait_ge(S["oT_ps"][s].sem, S["oT_ps"][s].after(u))
                        act.wait_ge(S["wo_ps"][s].sem, S["wo_ps"][s].after(u, 1))
                        nc.scalar.copy(oT[s][:].rearrange("p h t -> p (h t)"), A[:]).then_inc(S["oT"][s].sem, 1)

                def mlp(s, u, w, part):
                    A, B, Cb, D = bank[s]
                    if part == 0:
                        act.wait_ge(S["dev"][s].sem, S["dev"][s].after(u))
                        act.wait_ge(S["var_ps"][s].sem, S["var_ps"][s].after(u, 1))
                        nc.scalar.activation(dsq[s][:], dev[s][:], ACT.Square).then_inc(S["dsq"][s].sem, 1)
                        act.wait_ge(S["var_ps"][s].sem, S["var_ps"][s].after(u))
                        act.wait_ge(S["rstd"][s].sem, S["rstd"][s].after(u, 1))
                        nc.scalar.activation(lnv[s][:], Cb[:, P:2 * P], ACT.Ln, bias=const[:, 0:1]).then_inc(S["ln_v"][s].sem, 1)
                        act.wait_ge(S["ln_v"][s].sem, S["ln_v"][s].after(u))
                        act.wait_ge(S["hn"][s].sem, S["hn"][s].after(u, 1))
                        nc.scalar.activation(rstd[s][:], lnv[s][:], ACT.Exp, scale=-0.5).then_inc(S["rstd"][s].sem, 1)
                    if part == 1:
                        for j, tiles in enumerate(G):
                            n = 3 * u + j
                            act.wait_ge(M["w1_ps"][s].sem, M["w1_ps"][s].after(n))
                            act.wait_ge(M["hid"][s].sem, M["hid"][s].after(n, 3))
                            for x, m in enumerate(tiles):
                                last = nc.scalar.activation(gel[s][:, m], bank[s][j][0:MW, (2 * x + 1) * P:(2 * x + 2) * P], ACT.Gelu,
                                                            bias=b1c[:, 1, m:m + 1])
                            last.then_inc(M["gel"][s].sem, 1)
                    if part == 2:
                        act.wait_ge(S["outt" if LAST else "hout"][s].sem, S["outt" if LAST else "hout"][s].after(u))
                        if LAST:
                            act.dma_start(a["out"][s, bass.ds(u * P, P), :], outt[s][:]).then_inc(S["out"][s].sem, 16)
                        else:
                            act.dma_start(a["h1"][s, :, :, bass.ds(u * P + 1, P)], hout[s][:]).then_inc(S["out"][s].sem, 16)

                run(act, att, mlp, prologue)
                for s in range(NB):
                    act.wait_ge(S["out"][s].sem, S["out"][s].after(NW - 1))

            @block.tensor
            def _(pe):
                mm = nc.tensor.matmul

                def prologue():
                    pe.wait_ge(sems["w"], 128)
                    for x in range(2):
                        for m in range(MT):
                            for k in range(CC):
                                last = mm(bank[0][0][0:MW, x * MT + m:x * MT + m + 1], w1[:, k, x, m * MW:(m + 1) * MW], lngb[:, 1, k:k + 1],
                                          start=(k == 0), stop=(k == CC - 1))
                    last.then_inc(sems["bias"], 1)
                    pe.wait_ge(sems["prep"], 2)
                    pe.wait_ge(sems["set"], 1)

                def att(s, u, w, part):
                    A, B, Cb, D = bank[s]
                    if part == 0:
                        pe.wait_ge(S["h_in"][s].sem, S["h_in"][s].after(u))
                        h = shifted(hT[s][w])
                        for j, done in enumerate(("q_ps", "k_ps", "v_ps")):
                            pe.wait_ge(M["hid"][s].sem, M["hid"][s].after(3 * (u - 1) + j))
                            for k in range(CC):
                                last = mm(bank[s][j][:], h[:, k * P:(k + 1) * P], wqkv[:, k, j * INNER:(j + 1) * INNER],
                                          start=(k == 0), stop=(k == CC - 1))
                            last.then_inc(S[done][s].sem, 1)
                    if part == 1:
                        pe.wait_ge(S["qr"][s].sem, S["qr"][s].after(u))
                        pe.wait_ge(S["t1" if LAST else "hout"][s].sem, S["t1" if LAST else "hout"][s].after(u, 1))
                        for hp in range(NHP):
                            last = nc.tensor.transpose(D[:, hp * P:(hp + 1) * P],
                                                       qr[s][:, 2 * hp:2 * hp + 2].rearrange("p h d -> p (h d)"), ident[:])
                        last.then_inc(S["qT_ps"][s].sem, 1)
                        pe.wait_ge(S["kr"][s].sem, S["kr"][s].after(u))
                        pe.wait_ge(S["qsq"][s].sem, S["qsq"][s].after(u))
                        pe.wait_ge(S["qm"][s].sem, S["qm"][s].after(u))
                        for hp in range(NHP):
                            last = nc.tensor.transpose(A[:, hp * P:(hp + 1) * P],
                                                       kr[s][:, 2 * hp:2 * hp + 2].rearrange("p h d -> p (h d)"), ident[:])
                        last.then_inc(S["kT_ps"][s].sem, 1)
                    if part == 3:
                        def scores(hp):
                            n = u * NHP + hp
                            if hp == 0:
                                pe.wait_ge(S["qz"][s].sem, S["qz"][s].after(u))
                                pe.wait_ge(S["kT"][s].sem, S["kT"][s].after(u))
                                pe.wait_ge(S["kn"][s].sem, S["kn"][s].after(u))
                                if w == 0:
                                    pe.wait_ge(S["mask0"][s].sem, S["mask0"][s].after(u, 1))
                            if hp == 1:
                                pe.wait_ge(S["v_sb"][s].sem, S["v_sb"][s].after(u))
                            if hp > 1:
                                pe.wait_ge(Q["exp"][s].sem, Q["exp"][s].after(n, 2))
                            bk = bank[s][1 + hp % 2]
                            for x in range(2):
                                mm(bk[:, 2 * P * x:2 * P * (x + 1)], identb[:], mask[s][w][:].rearrange("p x n -> p (x n)"), start=True, stop=False)
                                last_ = mm(bk[:, 2 * P * x:2 * P * (x + 1)], qz[s][:, 2 * hp + x],
                                           kT[s][:, hp].rearrange("p x t -> p (x t)"), start=False, stop=True)
                            last_.then_inc(Q["sc"][s].sem, 1)

                        def turn(hp):
                            n = u * NHP + hp
                            pe.wait_ge(Q["exp"][s].sem, Q["exp"][s].after(n))
                            if hp > 0:
                                pe.wait_ge(Q["pT"][s].sem, Q["pT"][s].after(n, 1))
                            for x in range(2):
                                for slot in range(2):
                                    at = (2 * x + slot) * P
                                    last_ = nc.tensor.transpose(A[:, at:at + P], prob[s][:, 2 * hp + x, slot * P:(slot + 1) * P], ident[:])
                            last_.then_inc(Q["pt_ps"][s].sem, 1)

                        def values(hp):
                            pe.wait_ge(Q["pT"][s].sem, Q["pT"][s].after(u * NHP + hp))
                            for x in range(2):
                                h = 2 * hp + x
                                for slot in range(2):
                                    last_ = mm(D[:, h * DH:(h + 1) * DH], pT[s][:, h, slot], V[s][:, slot, h], start=(slot == 0), stop=(slot == 1))
                            return last_

                        scores(0)
                        scores(1)
                        for hp in range(NHP):
                            turn(hp)
                            if hp + 2 < NHP:
                                scores(hp + 2)
                            last = values(hp)
                        last.then_inc(S["pv"][s].sem, 1)
                        pe.wait_ge(S["o"][s].sem, S["o"][s].after(u))
                        for hp in range(NHP):
                            last = nc.tensor.transpose(A[:, hp * P:(hp + 1) * P], o[s][:, 2 * hp:2 * hp + 2].rearrange("p h d -> p (h d)"), ident[:])
                        last.then_inc(S["oT_ps"][s].sem, 1)
                        pe.wait_ge(S["oT"][s].sem, S["oT"][s].after(u))
                        for m in range(CC):
                            for k in range(NHP):
                                last = mm(B[:, m * P:(m + 1) * P], wo[:, k, m * P:(m + 1) * P], oT[s][:, k], start=(k == 0), stop=(k == NHP - 1))
                        last.then_inc(S["wo_ps"][s].sem, 1)

                def mlp(s, u, w, part):
                    A, B, Cb, D = bank[s]
                    if part == 0:
                        pe.wait_ge(S["x1"][s].sem, S["x1"][s].after(u))
                        for k in range(CC):
                            last = mm(Cb[:, 0:P], mean_w[:], shifted(x1[s][w])[:, k * P:(k + 1) * P], start=(k == 0), stop=(k == CC - 1))
                        last.then_inc(S["mean_ps"][s].sem, 1)
                        pe.wait_ge(S["dsq"][s].sem, S["dsq"][s].after(u))
                        for k in range(CC):
                            last = mm(Cb[:, P:2 * P], mean_w[:], dsq[s][:, k], start=(k == 0), stop=(k == CC - 1))
                        last.then_inc(S["var_ps"][s].sem, 1)
                    if part == 1:
                        pe.wait_ge(S["hn"][s].sem, S["hn"][s].after(u))
                        pe.wait_ge(S["ln_v"][s].sem, S["ln_v"][s].after(u))
                        for j, tiles in enumerate(G):
                            for x, m in enumerate(tiles):
                                for y in range(2):
                                    for k in range(CC):
                                        at = (2 * x + y) * P
                                        last = mm(bank[s][j][0:MW, at:at + P], w1[:, k, y, m * MW:(m + 1) * MW], hn[s][:, k],
                                                  start=(k == 0), stop=(k == CC - 1))
                            last.then_inc(M["w1_ps"][s].sem, 1)
                    if part == 2:
                        pe.wait_ge(M["hid"][s].sem, M["hid"][s].after(3 * u + 2))
                        for c in range(CC):
                            for m in range(MT):
                                last = mm(D[:, c * P:(c + 1) * P], w2[:, m, c * P:(c + 1) * P], hid[s][:, m], start=(m == 0), stop=(m == MT - 1))
                        last.then_inc(S["w2_ps"][s].sem, 1)
                        if LAST:
                            pe.wait_ge(S["hout"][s].sem, S["hout"][s].after(u))
                            for c in range(CC):
                                last = nc.tensor.transpose(D[:, C + c * P:C + (c + 1) * P], hout[s][:, c], ident[:])
                            last.then_inc(S["yT"][s].sem, 1)

                run(pe, att, mlp, prologue)


def run_stages(nc, a, T, stages=("setup", "mix", "scan", "gate", "local0", "local1")):
    with ExitStack() as ctx:
        sb = lambda n, s: ctx.enter_context(nc.sbuf_tensor(n, s, F32))
        persist = {"modc": sb("modc", [P, 24]), "rows": sb("rows", [P, 4 * C]), "vec": sb("vec", [P, len(VECS), CC]),
                   "half": sb("half", [P, 3, CC]), "const": sb("const", [P, 8]), "ident": sb("ident", [P, P])}
        if "setup" in stages:
            setup_stage(nc, persist, a)
        if "mix" in stages:
            mix_stage(nc, persist, a, T)
        if "scan" in stages:
            scan_stage(nc, persist, a, T)
        if "gate" in stages:
            gate_stage(nc, persist, a, T)
        for layer in range(2):
            if f"local{layer}" in stages:
                local_stage(nc, persist, a, T, layer)


def _cm(w):
    import numpy as np
    return np.ascontiguousarray(w.reshape(-1, P, w.shape[1]).transpose(1, 0, 2))


def _rows(n, *parts):
    import numpy as np
    out = np.zeros((n, parts[0][1].shape[1]), np.float32)
    for at, w in parts:
        out[at:at + w.shape[0]] = w
    return out


def lay_out(inp):
    import numpy as np
    g = lambda n: np.asarray(inp["L0_" + n])
    at = lambda n: g("attn_" + n)
    two = lambda w: _cm(w).reshape(P, -1)
    parts = dict(
        maa1=two(at("maa_w1").T), wr=two(at("Wr").T), gate1=two(at("gate_w1").T),
        wa1=two(_rows(P, (0, at("decay_w1")), (64, at("aaa_w1")), (96, at("ma_w1"))).T), wk=two(at("Wk").T),
        kk1=two(_rows(P, (0, at("kkk_w1")), (64, at("mk_w1"))).T), wv=two(at("Wv").T),
        **{f"maa2_{k}": _rows(P, (32 * k, at("maa_w2")[k])) for k in range(4)}, gate2=at("gate_w2"),
        decay2=_rows(P, (0, at("decay_w2"))), aaa2=_rows(P, (64, at("aaa_w2"))), ma2=_rows(P, (96, at("ma_w2"))),
        kkk2=_rows(P, (0, at("kkk_w2"))), mk2=_rows(P, (64, at("mk_w2"))))
    maa = at("time_maa").reshape(4, C)
    vecs = [at("time_maa_x"), maa[0], maa[1], maa[2], maa[3], at("time_decay"), at("time_aaaaa"), at("time_misc_a"),
            at("time_misc_k"), at("time_faaaa"), at("ln_w"), at("ln_b")]
    out = {"x": at("x"), "c_t": _cm(g("c").T), "wmod": _cm(g("wmod")),
           "mix_w": np.concatenate([parts[n] for n, _ in MIX_W], axis=1),
           "vecs": np.ascontiguousarray(np.stack(vecs).reshape(len(vecs), CC, P).transpose(2, 0, 1)),
           "ident": np.eye(P, dtype=np.float32),
           "ones16": np.kron(np.eye(HP, dtype=np.float32), np.ones((HS, HS), np.float32)),
           "resets": np.ascontiguousarray(np.broadcast_to((np.arange(CC * P) % CH != 0).astype(np.float32), (P, CC * P)))}
    out["wo_attn"] = _cm(at("Wo").T)
    m, t = np.arange(P)[:, None] % CH, np.arange(CH)[None, :]
    out["causal"] = np.stack([m < t, m <= t], axis=1).astype(np.float32)
    out["headmask"] = (np.arange(P)[:, None] // HS == np.arange(HP)[None, :]).astype(np.float32)
    out["eye16"] = np.ascontiguousarray(np.broadcast_to(np.eye(CH, dtype=np.float32), (P, 2, CH, CH)))
    q, kx = np.arange(P)[:, None], np.arange(P)[None, :]
    neg = np.float32(MASKED)
    before, own = np.where(kx < q, neg, 0), np.where(kx > q, neg, 0)
    out["winmask"] = np.concatenate([before, own], axis=1).astype(np.float32)
    n = out["x"].shape[1]
    half = np.arange(0, DH, 2, dtype=np.float32)
    inv = (1.0 / np.power(np.float32(10000.0), half / np.float32(DH))).astype(np.float32)
    tt = np.arange(n, dtype=np.float32)
    fr = tt[:, None] * inv[None, :]
    base = (half + np.float32(0.4 * DH)) / np.float32(1.4 * DH)
    power = (tt - n // 2) / np.float32(P // 2)
    scale = np.power(base[None, :], power[:, None]).astype(np.float32)
    cos, sin = np.cos(fr), np.sin(fr)
    cat = lambda u, w: np.concatenate([u, w], axis=1)
    out["rotary"] = np.stack([cat(cos * scale, cos * scale), cat(-sin * scale, sin * scale),
                              cat(cos / scale, cos / scale), cat(-sin / scale, sin / scale)], axis=1).astype(np.float32)
    f = lambda n_: g("ffn_" + n_)
    swap = lambda v: np.concatenate([v[:, DH // 2:], v[:, :DH // 2]], axis=1)
    qs, ks = f("q_scale"), f("k_scale")
    out["qk_scale"] = np.ascontiguousarray(np.broadcast_to(
        np.stack([qs, swap(qs), ks, swap(ks)], axis=1)[:, None], (2, P, 4, DH)))
    out["wqkv"] = np.stack([_cm(w) for w in f("wqkv")])
    out["wo"] = np.stack([_cm(w) for w in f("wo")])
    pad = MT * MW - HID
    halves = lambda w: np.pad(w.reshape(C, 2, HID), [(0, 0), (0, 0), (0, pad)]).reshape(C, -1)
    out["w1"] = np.stack([_cm(halves(w)) for w in f("w1")])
    tiles = lambda v: np.pad(v, [(0, pad)] + [(0, 0)] * (v.ndim - 1)).reshape(MT, MW, *v.shape[1:])
    out["w2"] = np.stack([tiles(w).transpose(1, 0, 2) for w in f("w2")])
    out["b1"] = np.stack([np.stack([tiles(b[:HID]), tiles(b[HID:])]).transpose(2, 0, 1) for b in f("b1")])
    col = lambda v: v.reshape(-1, CC, P).transpose(0, 2, 1)
    out["ln_gb"] = np.stack([col(f("ln_g")), col(f("ln_b")), col(f("b2"))], axis=2)
    return {k_: np.ascontiguousarray(v_) for k_, v_ in out.items()}


SCRATCH = lambda T: {
    "cm": [NB, T // P, P, CC * 4 * P], "gr": [NB, T // P, P, 2 * CC * P], "gl": [NB, T // P, P, CC * NCH],
    "v_stack": [NB, T // P, P, CC, NCH, HS], "att": [2 * (T // P), NB * CC * NCH // 2, HP, CH, CH],
    "inv": [2 * (T // P), NB * CC * NCH // 2, HP, CH, CH], "y_stack": [T // P, 2, P, NCH // 2 * NB * CC * HS],
    "xa": [NB, T, C], "h0": [NB, P, CC, T + 1], "h1": [NB, P, CC, T + 1]}


def kernel(**inputs):
    import concourse.bacc as bacc
    from concourse.bass_utils import run_bass_kernel_spmd

    arrays = lay_out(inputs)
    T = arrays["x"].shape[1]
    nc = bacc.Bacc("TRN2", target_bir_lowering=False, num_devices=1)
    a = {n: nc.dram_tensor("in_" + n, v.shape, mybir.dt.from_np(v.dtype), kind="ExternalInput").ap() for n, v in arrays.items()}
    a.update({n: nc.dram_tensor("scratch_" + n, s, F32, kind="Internal").ap() for n, s in SCRATCH(T).items()})
    a["out"] = nc.dram_tensor("out_0", [NB, T, C], F32, kind="ExternalOutput").ap()
    run_stages(nc, a, T)
    got = run_bass_kernel_spmd(nc, [{"in_" + n: v for n, v in arrays.items()}], core_ids=[0])
    return got.results[0]["out_0"]
```

```python
import math

import concourse.bass as bass
from concourse import mybir
from contextlib import ExitStack

F32 = mybir.dt.float32
BF16 = mybir.dt.bfloat16
ALU = mybir.AluOpType
ACT = mybir.ActivationFunctionType
AX = mybir.AxisListType

P = 128
NB = 2
C = 256
CC = C // P
HS = 16
CH = 16
NCH = P // CH
HP = P // HS
HEADS = 8
DH = 64
INNER = HEADS * DH
HID = 682
MT = 6
MW = 128
START = 2
LN_EXP = "natural_log_exp_and_others"
EXP_TANH = "exp_and_others"
KAPPA = math.exp(-0.5)
LNSCALE = 2.0 ** 40
MASKED = -1.0e30

MIX_W = [("maa1", 2 * 128), ("wr", 2 * C), ("gate1", 2 * 128), ("wa1", 2 * 128), ("wk", 2 * C), ("kk1", 2 * 128),
         ("wv", 2 * C), ("maa2_0", C), ("maa2_1", C), ("maa2_2", C), ("maa2_3", C), ("gate2", C), ("decay2", C),
         ("aaa2", C), ("ma2", C), ("kkk2", C), ("mk2", C)]
VECS = ["maa_x", "maa0", "maa1", "maa2", "maa3", "decay", "aaaaa", "misc_a", "misc_k", "faaaa", "ln_w", "ln_b"]


def places(parts):
    at, out = 0, {}
    for name, n in parts:
        out[name] = (at, n)
        at += n
    return out, at


class Signal:

    def __init__(self, sem, step, ahead):
        self.sem, self.step, self.ahead = sem, step, ahead

    def after(self, unit, back=0):
        return (unit + (self.ahead + 1 - back)) * self.step


def signals(nc, ctx, names, streams, tag, ahead=START):
    out = {}
    for item in names.split():
        name, _, step = item.partition(":")
        made = [Signal(ctx.enter_context(nc.semaphore(f"{tag}_{name}{b}")), int(step or 1), ahead) for b in range(streams)]
        out[name] = made
    return out


def start_signals(nc, plain, *tables):
    with nc.Block() as block:
        @block.gpsimd
        def _(pool):
            for sem in plain:
                pool.sem_clear(sem)
            for table in tables:
                for made in table.values():
                    for s in made:
                        pool.sem_clear(s.sem)
                        pool.sem_inc(s.sem, s.ahead * s.step)


def setup_stage(nc, persist, a):
    modc, rows, constant = persist["modc"], persist["rows"], persist["const"]
    with ExitStack() as ctx:
        sb = lambda n, s, d=F32: ctx.enter_context(nc.sbuf_tensor(n, s, d))
        sem = lambda n: ctx.enter_context(nc.semaphore(n))
        wmod = sb("wmod", [P, CC, 6 * C])
        cT = sb("cT", [P, CC, NB])
        ex = sb("ex", [P, CC, NB])
        den = sb("den", [P, CC, NB])
        inv = sb("inv", [P, CC, NB])
        sc = sb("sc", [P, CC, NB])
        scb = sb("scb", [P, CC, NB, P])
        ones = sb("ones", [P, P])
        raw = sb("raw", [P, 24])
        neg = sb("neg", [P, 4 * C])
        mag = sb("mag", [P, 4 * C])
        sgn = sb("sgn", [P, 4 * C])
        rraw = sb("rraw", [P, 4 * C])
        pm = ctx.enter_context(nc.psum_tensor("pmod", [P, 512], F32))
        pr = [ctx.enter_context(nc.psum_tensor(f"prow{k}", [P, 512], F32)) for k in range(2)]
        s_in, s_ex, s_v, s_sc, s_mm, s_rr, s_end = map(sem, ["su_in", "su_ex", "su_v", "su_sc", "su_mm", "su_rr", "su_end"])
        with nc.Block() as block:
            @block.sync
            def _(sp):
                sp.dma_start(wmod[:], a["wmod"]).then_inc(s_in, 16)
                sp.dma_start(cT[:], a["c_t"]).then_inc(s_in, 16)
                sp.dma_start(persist["vec"][:], a["vecs"]).then_inc(s_in, 16)
                sp.dma_start(persist["ident"][:], a["ident"]).then_inc(s_in, 16)

            @block.scalar
            def _(act):
                act.wait_ge(s_in, 64)
                nc.scalar.activation(ex[:], cT[:], ACT.Exp, scale=-1.0).then_inc(s_ex, 1)

            @block.gpsimd
            def _(pool):
                for k, v in enumerate([1e-5, 1.0, 20.0 * math.log(2.0), 0.00064, 0.0, 0.0, 0.0, 0.0]):
                    nc.gpsimd.memset(constant[:, k:k + 1], v)
                nc.gpsimd.memset(ones[:], 1.0).then_inc(s_end, 1)
                pool.wait_ge(s_end, 1)

            @block.vector
            def _(dve):
                dve.wait_ge(s_ex, 1)
                nc.vector.tensor_scalar(den[:], ex[:], 1.0, None, ALU.add).then_inc(s_v, 1)
                dve.wait_ge(s_v, 1)
                nc.vector.reciprocal(inv[:], den[:]).then_inc(s_v, 1)
                dve.wait_ge(s_v, 2)
                nc.vector.tensor_tensor(sc[:], inv[:], cT[:], ALU.mult).then_inc(s_v, 1)
                dve.wait_ge(s_v, 3)
                dve.wait_ge(s_end, 1)
                for k in range(CC):
                    for b in range(NB):
                        nc.vector.tensor_scalar(scb[:, k, b, :], ones[:], sc[:, k, b:b + 1], None, ALU.mult).then_inc(s_sc, 1)
                nc.vector.tensor_scalar(persist["half"][:], persist["vec"][:, 6:9, :], 0.5, None, ALU.mult).then_inc(s_v, 1)
                dve.wait_ge(s_mm, 1)
                nc.vector.tensor_copy(raw[:], pm[:, 0:24])
                for k in range(2):
                    last = nc.vector.tensor_copy(rraw[:, 512 * k:512 * (k + 1)], pr[k][:])
                last.then_inc(s_v, 1)
                dve.wait_ge(s_v, 5)
                nc.vector.tensor_copy(modc[:], raw[:]).then_inc(s_v, 1)
                dve.wait_ge(s_v, 6)
                for j in (1, 4):
                    nc.vector.tensor_scalar(modc[:, 4 * j:4 * j + 4], raw[:, 4 * j:4 * j + 4], 1.0, None, ALU.add)
                nc.vector.tensor_scalar(neg[:], rraw[:], -1.0, None, ALU.mult)
                nc.vector.tensor_scalar(sgn[:], rraw[:], 0.0, 2.0, ALU.is_ge, ALU.mult).then_inc(s_v, 1)
                dve.wait_ge(s_v, 7)
                nc.vector.tensor_tensor(mag[:], rraw[:], neg[:], ALU.max).then_inc(s_v, 1)
                dve.wait_ge(s_v, 8)
                nc.vector.tensor_scalar(neg[:], mag[:], 0.25, None, ALU.max).then_inc(s_v, 1)
                dve.wait_ge(s_v, 9)
                nc.vector.scalar_tensor_tensor(out=rows[:], in0=sgn[:], scalar=-1.0, in1=neg[:], op0=ALU.add,
                                               op1=ALU.mult).then_inc(s_v, 1)
                dve.wait_ge(s_v, 10)

            @block.tensor
            def _(pe):
                pe.wait_ge(s_sc, CC * NB)
                for j in range(6):
                    for m in range(CC):
                        for k in range(CC):
                            at = 4 * j + 2 * m
                            nc.tensor.matmul(pm[:, at:at + NB], wmod[:, k, j * C + m * P:j * C + (m + 1) * P], sc[:, k, :],
                                             start=(k == 0), stop=(k == CC - 1))
                for q, j in enumerate((2, 5)):
                    for b in range(NB):
                        for k in range(CC):
                            last = nc.tensor.matmul(pr[q][:, b * C:(b + 1) * C], scb[:, k, b, :], wmod[:, k, j * C:(j + 1) * C],
                                                    start=(k == 0), stop=(k == CC - 1))
                last.then_inc(s_mm, 1)


def mix_stage(nc, persist, a, T):
    NW = T // P
    modc, vec, half, const, ident = (persist[k] for k in ("modc", "vec", "half", "const", "ident"))
    W, ncols = places(MIX_W)
    with ExitStack() as ctx:
        sb = lambda n, s, d=F32: [ctx.enter_context(nc.sbuf_tensor(f"{n}{b}", s, d)) for b in range(NB)]
        wp = ctx.enter_context(nc.sbuf_tensor("mixw", [P, ncols], F32))
        ones16 = ctx.enter_context(nc.sbuf_tensor("ones16", [P, P], F32))
        bonus = ctx.enter_context(nc.sbuf_tensor("bonus", [P, CC, P], F32))
        resets = ctx.enter_context(nc.sbuf_tensor("resets", [P, CC * P], F32))
        xt, xn = sb("xt", [P, C]), sb("xn", [P, C])
        st, mv, lnv, rstd = sb("st", [P, 6]), sb("mv", [P, 2]), sb("lnv", [P, 1]), sb("rstd", [P, 1])
        h, xx, mix = sb("h", [P, CC, P + 1]), sb("xx", [P, CC, P]), sb("mix", [P, CC, P])
        lot, tm, xm = sb("lot", [P, P]), sb("tm", [P, 4, CC, P]), sb("xm", [P, 4, CC, P])
        th_g, th_w, th_k = sb("th_g", [P, P]), sb("th_w", [P, P]), sb("th_k", [P, P])
        full = [P, CC, P]
        r, k, v, zb, ta, tma, tmk = (sb(n, full) for n in ("r", "k", "v", "zb", "ta", "tma", "tmk"))
        kk, sq, nn, rn, az, ez, lz, nm, L1 = (sb(n, full) for n in ("kk", "sq", "nn", "rn", "az", "ez", "lz", "nm", "L1"))
        sg, cum, cprev, mkp, wm, ek = (sb(n, full) for n in ("sg", "cum", "cprev", "mkp", "wm", "ek"))
        gam, gami, gamp = (sb(n, full) for n in ("gam", "gami", "gamp"))
        kkn, aa, ba, m1, pq, kf, k2, k3, rk3 = (sb(n, full) for n in ("kkn", "aa", "ba", "m1", "pq", "kf", "k2", "k3", "rk3"))
        cm = sb("cm", [P, CC, 4, P])
        gr = sb("gr", [P, 2, CC, P])
        gl = sb("gl", [P, CC, NCH])
        vt = sb("vt", [P, C])
        pause = ctx.enter_context(nc.sbuf_tensor("pause", [P, NB], F32))
        bank = [[ctx.enter_context(nc.psum_tensor(f"mx{n}{b}", [P, 512], F32)) for n in "ABCD"] for b in range(NB)]
        S = signals(nc, ctx, "x_in:16 stats mean_var ln_var rstd xn xT carry h xx mix lo lo_tanh pm01 pm23 tm01 tm23 xm01 xm23 hidden rk_ps v_ps "
                    "hidden_sb rk_sb v_sb da_ps mm_ps g_ps kk_ps zb gates g_sb kk sq norm_ps clamped ln_norm inv_norm "
                    "abs_z exp_z ln_z min_z log_sig sig mk wm ek cum cprev gam gami gamp kkn a_t q_t aa ba b_t m1 pq kf "
                    "k2 k3 k_t rk3 rk_ps2 rkv gl vT_ps vT stored:48 v_stored:128", NB, "mx")
        s_w, s_c = ctx.enter_context(nc.semaphore("mx_w")), ctx.enter_context(nc.semaphore("mx_c"))
        start_signals(nc, (s_w, s_c), S)
        w = lambda name: wp[:, W[name][0]:W[name][0] + W[name][1]]
        w2 = lambda name: w(name).rearrange("p (k m) -> p k m", k=CC)
        flat = lambda t: t[:].rearrange("p c t -> p (c t)")
        vc = lambda name, c: vec[:, VECS.index(name), c:c + 1]
        with nc.Block() as block:
            @block.sync
            def _(sp):
                sp.dma_start(wp[:], a["mix_w"]).then_inc(s_w, 16)
                sp.dma_start(ones16[:], a["ones16"]).then_inc(s_w, 16)
                sp.dma_start(resets[:], a["resets"]).then_inc(s_w, 16)

                def load(i):
                    for b in range(NB):
                        sp.wait_ge(S["xn"][b].sem, S["xn"][b].after(i, 1))
                        sp.dma_start(xt[b][:], a["x"][b, bass.ds(i * P, P), :]).then_inc(S["x_in"][b].sem, 16)

                def window(i, more):
                    if more:
                        load(i + 1)
                    for b in range(NB):
                        sp.wait_ge(S["vT"][b].sem, S["vT"][b].after(i))
                        for c in range(NCH):
                            sp.dma_start(a["v_stack"][b, bass.ds(i, 1)].rearrange("o (h t) g c i -> (o c) t g h i", t=CH)[c],
                                         vt[b][c * CH:(c + 1) * CH, :].rearrange("t (g h i) -> t g h i", g=CC, h=HP)
                                         ).then_inc(S["v_stored"][b].sem, 16)
                        sp.wait_ge(S["a_t"][b].sem, S["a_t"][b].after(i))
                        sp.wait_ge(S["q_t"][b].sem, S["q_t"][b].after(i))
                        sp.wait_ge(S["b_t"][b].sem, S["b_t"][b].after(i))
                        sp.wait_ge(S["k_t"][b].sem, S["k_t"][b].after(i))
                        sp.dma_start(a["cm"][b, bass.ds(i, 1)].rearrange("o p n -> (o p) n"),
                                     cm[b][:].rearrange("p g x t -> p (g x t)")).then_inc(S["stored"][b].sem, 16)
                        sp.wait_ge(S["gl"][b].sem, S["gl"][b].after(i))
                        sp.dma_start(a["gl"][b, bass.ds(i, 1)].rearrange("o p n -> (o p) n"),
                                     gl[b][:].rearrange("p g c -> p (g c)")).then_inc(S["stored"][b].sem, 16)
                        sp.wait_ge(S["rkv"][b].sem, S["rkv"][b].after(i))
                        sp.wait_ge(S["g_sb"][b].sem, S["g_sb"][b].after(i))
                        sp.dma_start(a["gr"][b, bass.ds(i, 1)].rearrange("o p n -> (o p) n"),
                                     gr[b][:].rearrange("p x c t -> p (x c t)")).then_inc(S["stored"][b].sem, 16)

                load(0)
                with sp.Fori(0, NW - 1) as i:
                    window(i, True)
                window(NW - 1, False)
                for b in range(NB):
                    sp.wait_ge(S["stored"][b].sem, S["stored"][b].after(NW - 1))
                    sp.wait_ge(S["v_stored"][b].sem, S["v_stored"][b].after(NW - 1))

            @block.vector
            def _(dve):
                def window(i, more):
                    for b in range(NB):
                        for half_, (ready, done) in enumerate((("pm01", "tm01"), ("pm23", "tm23"))):
                            dve.wait_ge(S[ready][b].sem, S[ready][b].after(i))
                            if half_ == 0:
                                dve.wait_ge(S["xm01"][b].sem, S["xm01"][b].after(i, 1))
                            for g in (2 * half_, 2 * half_ + 1):
                                for c in range(CC):
                                    src = bank[b][2 + half_][:, (g % 2) * C + c * P:(g % 2) * C + (c + 1) * P]
                                    last = nc.vector.scalar_tensor_tensor(out=tm[b][:, g, c, :], in0=src, scalar=vc(f"maa{g}", c),
                                                                          in1=xx[b][:, c, :], op0=ALU.add, op1=ALU.mult)
                            last.then_inc(S[done][b].sem, 1)
                        dve.wait_ge(S["tm23"][b].sem, S["tm23"][b].after(i))
                        dve.wait_ge(S["v_ps"][b].sem, S["v_ps"][b].after(i, 1))
                        nc.vector.tensor_tensor(xm[b][:, 2:4], tm[b][:, 2:4], h[b][:, :, 1:P + 1].unsqueeze(1).broadcast_to([P, 2, CC, P]),
                                                ALU.add).then_inc(S["xm23"][b].sem, 1)
                    for b in range(NB):
                        dve.wait_ge(S["kk_ps"][b].sem, S["kk_ps"][b].after(i))
                        dve.wait_ge(S["rk_sb"][b].sem, S["rk_sb"][b].after(i))
                        nc.vector.tensor_tensor(kk[b][:], bank[b][0][:, 0:C].rearrange("p (c t) -> p c t", c=CC), k[b][:],
                                                ALU.add).then_inc(S["kk"][b].sem, 1)
                    for b in range(NB):
                        dve.wait_ge(S["zb"][b].sem, S["zb"][b].after(i))
                        nc.vector.tensor_scalar(nm[b][:], zb[b][:], 0.0, None, ALU.min).then_inc(S["min_z"][b].sem, 1)
                        dve.wait_ge(S["gates"][b].sem, S["gates"][b].after(i))
                        nc.vector.tensor_scalar(mkp[b][:], tmk[b][:], 0.5, 0.5, ALU.mult, ALU.add).then_inc(S["mk"][b].sem, 1)
                        nc.vector.tensor_scalar(aa[b][:], ta[b][:], 0.5, 0.5, ALU.mult, ALU.add).then_inc(S["aa"][b].sem, 1)
                        nc.vector.tensor_scalar(m1[b][:], tma[b][:], -1.0, None, ALU.add).then_inc(S["m1"][b].sem, 1)
                        dve.wait_ge(S["norm_ps"][b].sem, S["norm_ps"][b].after(i))
                        nc.vector.tensor_scalar(nn[b][:], bank[b][0][:, C:2 * C].rearrange("p (c t) -> p c t", c=CC), 1e-24, None,
                                                ALU.max).then_inc(S["clamped"][b].sem, 1)
                        dve.wait_ge(S["m1"][b].sem, S["m1"][b].after(i))
                        nc.vector.scalar_tensor_tensor(out=pq[b][:], in0=ta[b][:], scalar=-1.0, in1=m1[b][:], op0=ALU.add,
                                                       op1=ALU.mult).then_inc(S["pq"][b].sem, 1)
                    if more:
                        for b in range(NB):
                            dve.wait_ge(S["x_in"][b].sem, S["x_in"][b].after(i + 1))
                            nc.vector.bn_stats(st[b][:], xt[b][:]).then_inc(S["stats"][b].sem, 1)
                    if more:
                        for b in range(NB):
                            dve.wait_ge(S["stats"][b].sem, S["stats"][b].after(i + 1))
                            dve.wait_ge(S["ln_var"][b].sem, S["ln_var"][b].after(i + 1, 1))
                            nc.vector.memset(pause[:, b:b + 1], 0.0)
                            nc.vector.bn_aggr(mv[b][:], st[b][:]).then_inc(S["mean_var"][b].sem, 1)
                    for b in range(NB):
                        dve.wait_ge(S["ln_z"][b].sem, S["ln_z"][b].after(i))
                        dve.wait_ge(S["min_z"][b].sem, S["min_z"][b].after(i))
                        nc.vector.tensor_tensor(L1[b][:], nm[b][:], lz[b][:], ALU.subtract).then_inc(S["log_sig"][b].sem, 1)
                        dve.wait_ge(S["pq"][b].sem, S["pq"][b].after(i))
                        nc.vector.tensor_scalar(kf[b][:], pq[b][:], -0.25, 1.0, ALU.mult, ALU.add).then_inc(S["kf"][b].sem, 1)
                    for b in range(NB):
                        dve.wait_ge(S["mk"][b].sem, S["mk"][b].after(i))
                        dve.wait_ge(S["log_sig"][b].sem, S["log_sig"][b].after(i))
                        nc.vector.scalar_tensor_tensor(out=wm[b][:], in0=L1[b][:], scalar=-0.5, in1=mkp[b][:], op0=ALU.add,
                                                       op1=ALU.mult).then_inc(S["wm"][b].sem, 1)
                        dve.wait_ge(S["kf"][b].sem, S["kf"][b].after(i))
                        nc.vector.tensor_tensor(k2[b][:], k[b][:], kf[b][:], ALU.mult).then_inc(S["k2"][b].sem, 1)
                    if more:
                        for b in range(NB):
                            dve.wait_ge(S["rstd"][b].sem, S["rstd"][b].after(i + 1))
                            dve.wait_ge(S["xT"][b].sem, S["xT"][b].after(i + 1, 1))
                            nc.vector.tensor_scalar(xn[b][:], xt[b][:], mv[b][:, 0:1], rstd[b][:], ALU.subtract, ALU.mult
                                                    ).then_inc(S["xn"][b].sem, 1)
                    for b in range(NB):
                        dve.wait_ge(S["sig"][b].sem, S["sig"][b].after(i))
                        nc.vector.tensor_tensor_scan(flat(cum[b]), resets[:], flat(sg[b]), 0.0, ALU.mult, ALU.add
                                                     ).then_inc(S["cum"][b].sem, 1)
                    for b in range(NB):
                        dve.wait_ge(S["inv_norm"][b].sem, S["inv_norm"][b].after(i))
                        nc.vector.tensor_tensor(kkn[b][:], kk[b][:], rn[b][:], ALU.mult).then_inc(S["kkn"][b].sem, 1)
                        dve.wait_ge(S["k2"][b].sem, S["k2"][b].after(i))
                        dve.wait_ge(S["ek"][b].sem, S["ek"][b].after(i))
                        nc.vector.tensor_tensor(k3[b][:], k2[b][:], ek[b][:], ALU.mult).then_inc(S["k3"][b].sem, 1)
                    if more:
                        for b in range(NB):
                            dve.wait_ge(S["h"][b].sem, S["h"][b].after(i + 1))
                            nc.vector.tensor_tensor(xx[b][:], h[b][:, :, 0:P], h[b][:, :, 1:P + 1], ALU.subtract
                                                    ).then_inc(S["xx"][b].sem, 1)
                    if more:
                        for b in range(NB):
                            dve.wait_ge(S["xx"][b].sem, S["xx"][b].after(i + 1))
                            dve.wait_ge(S["lo"][b].sem, S["lo"][b].after(i + 1, 1))
                            for c in range(CC):
                                last = nc.vector.scalar_tensor_tensor(out=mix[b][:, c, :], in0=xx[b][:, c, :], scalar=vc("maa_x", c),
                                                                      in1=h[b][:, c, 1:P + 1], op0=ALU.mult, op1=ALU.add)
                            last.then_inc(S["mix"][b].sem, 1)
                    for b in range(NB):
                        dve.wait_ge(S["stored"][b].sem, S["stored"][b].after(i, 1))
                        dve.wait_ge(S["kkn"][b].sem, S["kkn"][b].after(i))
                        dve.wait_ge(S["gamp"][b].sem, S["gamp"][b].after(i))
                        nc.vector.tensor_tensor(cm[b][:, :, 0, :], kkn[b][:], gamp[b][:], ALU.mult).then_inc(S["a_t"][b].sem, 1)
                        dve.wait_ge(S["k3"][b].sem, S["k3"][b].after(i))
                        dve.wait_ge(S["gami"][b].sem, S["gami"][b].after(i))
                        nc.vector.tensor_tensor(cm[b][:, :, 3, :], k3[b][:], gami[b][:], ALU.mult).then_inc(S["k_t"][b].sem, 1)
                        dve.wait_ge(S["ba"][b].sem, S["ba"][b].after(i))
                        nc.vector.scalar_tensor_tensor(out=cm[b][:, :, 2, :], in0=ba[b][:], scalar=-1.0, in1=gami[b][:],
                                                       op0=ALU.mult, op1=ALU.mult).then_inc(S["b_t"][b].sem, 1)
                    for b in range(NB):
                        dve.wait_ge(S["rk_ps2"][b].sem, S["rk_ps2"][b].after(i))
                        nc.vector.tensor_tensor(gr[b][:, 1], bank[b][1][:, 0:C].rearrange("p (c t) -> p c t", c=CC), v[b][:],
                                                ALU.mult).then_inc(S["rkv"][b].sem, 1)


                dve.wait_ge(s_w, 48)
                for b in range(NB):
                    nc.vector.memset(h[b][:], 0.0)
                for c in range(CC):
                    last = nc.vector.tensor_scalar(bonus[:, c, :], ones16[:], vc("faaaa", c), None, ALU.mult)
                last.then_inc(s_c, 1)
                for b in range(NB):
                    dve.wait_ge(S["x_in"][b].sem, S["x_in"][b].after(0))
                    nc.vector.bn_stats(st[b][:], xt[b][:]).then_inc(S["stats"][b].sem, 1)
                for b in range(NB):
                    dve.wait_ge(S["stats"][b].sem, S["stats"][b].after(0))
                    dve.wait_ge(S["ln_var"][b].sem, S["ln_var"][b].after(0, 1))
                    nc.vector.memset(pause[:, b:b + 1], 0.0)
                    nc.vector.bn_aggr(mv[b][:], st[b][:]).then_inc(S["mean_var"][b].sem, 1)
                for b in range(NB):
                    dve.wait_ge(S["rstd"][b].sem, S["rstd"][b].after(0))
                    dve.wait_ge(S["xT"][b].sem, S["xT"][b].after(0, 1))
                    nc.vector.tensor_scalar(xn[b][:], xt[b][:], mv[b][:, 0:1], rstd[b][:], ALU.subtract, ALU.mult
                                            ).then_inc(S["xn"][b].sem, 1)
                for b in range(NB):
                    dve.wait_ge(S["h"][b].sem, S["h"][b].after(0))
                    nc.vector.tensor_tensor(xx[b][:], h[b][:, :, 0:P], h[b][:, :, 1:P + 1], ALU.subtract
                                            ).then_inc(S["xx"][b].sem, 1)
                for b in range(NB):
                    dve.wait_ge(S["xx"][b].sem, S["xx"][b].after(0))
                    dve.wait_ge(S["lo"][b].sem, S["lo"][b].after(0, 1))
                    for c in range(CC):
                        last = nc.vector.scalar_tensor_tensor(out=mix[b][:, c, :], in0=xx[b][:, c, :], scalar=vc("maa_x", c),
                                                              in1=h[b][:, c, 1:P + 1], op0=ALU.mult, op1=ALU.add)
                    last.then_inc(S["mix"][b].sem, 1)
                with dve.Fori(0, NW - 1) as i:
                    window(i, True)
                window(NW - 1, False)

            @block.gpsimd
            def _(pool):
                with pool.Fori(0, NW) as i:
                    for b in range(NB):
                        pool.wait_ge(S["tm01"][b].sem, S["tm01"][b].after(i))
                        pool.wait_ge(S["v_ps"][b].sem, S["v_ps"][b].after(i, 1))
                        nc.gpsimd.tensor_tensor(xm[b][:, 0:2], tm[b][:, 0:2], h[b][:, :, 1:P + 1].unsqueeze(1).broadcast_to([P, 2, CC, P]),
                                                ALU.add).then_inc(S["xm01"][b].sem, 1)
                    for b in range(NB):
                        pool.wait_ge(S["cum"][b].sem, S["cum"][b].after(i))
                        nc.gpsimd.tensor_tensor(cprev[b][:], cum[b][:], sg[b][:], ALU.subtract).then_inc(S["cprev"][b].sem, 1)
                    for b in range(NB):
                        pool.wait_ge(S["kkn"][b].sem, S["kkn"][b].after(i))
                        pool.wait_ge(S["aa"][b].sem, S["aa"][b].after(i))
                        nc.gpsimd.tensor_tensor(ba[b][:], kkn[b][:], aa[b][:], ALU.mult).then_inc(S["ba"][b].sem, 1)
                        pool.wait_ge(S["k3"][b].sem, S["k3"][b].after(i))
                        nc.gpsimd.tensor_tensor(rk3[b][:], r[b][:], k3[b][:], ALU.mult).then_inc(S["rk3"][b].sem, 1)
                        pool.wait_ge(S["gam"][b].sem, S["gam"][b].after(i))
                        pool.wait_ge(S["stored"][b].sem, S["stored"][b].after(i, 1))
                        nc.gpsimd.tensor_tensor(cm[b][:, :, 1, :], r[b][:], gam[b][:], ALU.mult).then_inc(S["q_t"][b].sem, 1)
                        nc.gpsimd.tensor_copy(gl[b][:], gam[b][:].rearrange("p g (c t) -> p g c t", t=CH)[:, :, :, CH - 1]
                                              ).then_inc(S["gl"][b].sem, 1)

            @block.scalar
            def _(act):
                def window(i, more):
                    for b in range(NB):
                        act.wait_ge(S["lo"][b].sem, S["lo"][b].after(i))
                        act.wait_ge(S["pm23"][b].sem, S["pm23"][b].after(i, 1))
                        nc.scalar.activation(lot[b][:], bank[b][0][:, 0:P], ACT.Tanh).then_inc(S["lo_tanh"][b].sem, 1)
                    for b in range(NB):
                        act.wait_ge(S["hidden"][b].sem, S["hidden"][b].after(i))
                        act.wait_ge(S["kk_ps"][b].sem, S["kk_ps"][b].after(i, 1))
                        act.wait_ge(S["g_ps"][b].sem, S["g_ps"][b].after(i, 1))
                        nc.scalar.activation(th_w[b][0:64, :], bank[b][1][0:64, 0:P], ACT.Tanh)
                        nc.scalar.copy(th_w[b][64:128, :], bank[b][1][64:128, 0:P])
                        nc.scalar.activation(th_g[b][:], bank[b][1][:, P:2 * P], ACT.Tanh)
                        nc.scalar.activation(th_k[b][0:64, :], bank[b][1][0:64, 2 * P:3 * P], ACT.Tanh)
                        nc.scalar.copy(th_k[b][64:128, :], bank[b][1][64:128, 2 * P:3 * P]).then_inc(S["hidden_sb"][b].sem, 1)
                        act.wait_ge(S["rk_ps"][b].sem, S["rk_ps"][b].after(i))
                        act.wait_ge(S["q_t"][b].sem, S["q_t"][b].after(i, 1))
                        act.wait_ge(S["k2"][b].sem, S["k2"][b].after(i, 1))
                        nc.scalar.copy(flat(r[b]), bank[b][0][:, 0:C])
                        nc.scalar.copy(flat(k[b]), bank[b][0][:, C:2 * C]).then_inc(S["rk_sb"][b].sem, 1)
                        act.wait_ge(S["v_ps"][b].sem, S["v_ps"][b].after(i))
                        act.wait_ge(S["rkv"][b].sem, S["rkv"][b].after(i, 1))
                        nc.scalar.copy(flat(v[b]), bank[b][2][:, 0:C]).then_inc(S["v_sb"][b].sem, 1)
                    for b in range(NB):
                        act.wait_ge(S["da_ps"][b].sem, S["da_ps"][b].after(i))
                        act.wait_ge(S["pq"][b].sem, S["pq"][b].after(i, 1))
                        act.wait_ge(S["aa"][b].sem, S["aa"][b].after(i, 1))
                        act.wait_ge(S["abs_z"][b].sem, S["abs_z"][b].after(i, 1))
                        for c in range(CC):
                            last = nc.scalar.activation(zb[b][:, c, :], bank[b][3][:, c * P:(c + 1) * P], ACT.Identity, bias=vc("decay", c))
                        last.then_inc(S["zb"][b].sem, 1)
                        for c in range(CC):
                            nc.scalar.activation(ta[b][:, c, :], bank[b][3][:, C + c * P:C + (c + 1) * P], ACT.Tanh, scale=0.5,
                                                 bias=half[:, 0, c:c + 1])
                        act.wait_ge(S["mm_ps"][b].sem, S["mm_ps"][b].after(i))
                        for c in range(CC):
                            nc.scalar.activation(tma[b][:, c, :], bank[b][1][:, c * P:(c + 1) * P], ACT.Tanh, scale=0.5,
                                                 bias=half[:, 1, c:c + 1])
                        for c in range(CC):
                            last = nc.scalar.activation(tmk[b][:, c, :], bank[b][1][:, C + c * P:C + (c + 1) * P], ACT.Tanh, scale=0.5,
                                                        bias=half[:, 2, c:c + 1])
                        last.then_inc(S["gates"][b].sem, 1)
                    act.preload_act_table_set(LN_EXP)
                    for b in range(NB):
                        act.wait_ge(S["kk"][b].sem, S["kk"][b].after(i))
                        nc.scalar.activation(sq[b][:], kk[b][:], ACT.Square).then_inc(S["sq"][b].sem, 1)
                        act.wait_ge(S["g_ps"][b].sem, S["g_ps"][b].after(i))
                        act.wait_ge(S["stored"][b].sem, S["stored"][b].after(i, 1))
                        nc.scalar.copy(gr[b][:, 0].rearrange("p c t -> p (c t)"), bank[b][2][:, 0:C]).then_inc(S["g_sb"][b].sem, 1)
                        act.wait_ge(S["vT_ps"][b].sem, S["vT_ps"][b].after(i))
                        act.wait_ge(S["v_stored"][b].sem, S["v_stored"][b].after(i, 1))
                        nc.scalar.copy(vt[b][:], bank[b][2][:, C:2 * C]).then_inc(S["vT"][b].sem, 1)
                        act.wait_ge(S["zb"][b].sem, S["zb"][b].after(i))
                        nc.scalar.activation(az[b][:], zb[b][:], ACT.Abs).then_inc(S["abs_z"][b].sem, 1)
                    if more:
                        for b in range(NB):
                            act.wait_ge(S["mean_var"][b].sem, S["mean_var"][b].after(i + 1))
                            nc.scalar.activation(lnv[b][:], mv[b][:, 1:2], ACT.Ln, bias=const[:, 0:1]).then_inc(S["ln_var"][b].sem, 1)
                            act.wait_ge(S["ln_var"][b].sem, S["ln_var"][b].after(i + 1))
                            act.wait_ge(S["xn"][b].sem, S["xn"][b].after(i + 1, 1))
                            nc.scalar.activation(rstd[b][:], lnv[b][:], ACT.Exp, scale=-0.5).then_inc(S["rstd"][b].sem, 1)
                    for b in range(NB):
                        act.wait_ge(S["abs_z"][b].sem, S["abs_z"][b].after(i))
                        nc.scalar.activation(ez[b][:], az[b][:], ACT.Exp, scale=-1.0).then_inc(S["exp_z"][b].sem, 1)
                    for b in range(NB):
                        act.wait_ge(S["exp_z"][b].sem, S["exp_z"][b].after(i))
                        nc.scalar.activation(lz[b][:], ez[b][:], ACT.Ln, bias=const[:, 1:2]).then_inc(S["ln_z"][b].sem, 1)
                    for b in range(NB):
                        act.wait_ge(S["clamped"][b].sem, S["clamped"][b].after(i))
                        nc.scalar.activation(az[b][:], nn[b][:], ACT.Ln, scale=LNSCALE).then_inc(S["ln_norm"][b].sem, 1)
                        act.wait_ge(S["log_sig"][b].sem, S["log_sig"][b].after(i))
                        nc.scalar.activation(sg[b][:], L1[b][:], ACT.Exp).then_inc(S["sig"][b].sem, 1)
                    for b in range(NB):
                        act.wait_ge(S["ln_norm"][b].sem, S["ln_norm"][b].after(i))
                        nc.scalar.activation(rn[b][:], az[b][:], ACT.Exp, scale=-0.5, bias=const[:, 2:3]).then_inc(S["inv_norm"][b].sem, 1)
                        act.wait_ge(S["wm"][b].sem, S["wm"][b].after(i))
                        nc.scalar.activation(ek[b][:], wm[b][:], ACT.Exp).then_inc(S["ek"][b].sem, 1)
                    if more:
                        for b in range(NB):
                            act.wait_ge(S["xT"][b].sem, S["xT"][b].after(i + 1))
                            act.wait_ge(S["xm01"][b].sem, S["xm01"][b].after(i + 1, 1))
                            act.wait_ge(S["xm23"][b].sem, S["xm23"][b].after(i + 1, 1))
                            act.wait_ge(S["h"][b].sem, S["h"][b].after(i + 1, 1))
                            nc.scalar.copy(h[b][:, :, 0:1], h[b][:, :, P:P + 1]).then_inc(S["carry"][b].sem, 1)
                            act.wait_ge(S["carry"][b].sem, S["carry"][b].after(i + 1))
                            for c in range(CC):
                                last = nc.scalar.activation(h[b][:, c, 1:P + 1], bank[b][0][:, c * P:(c + 1) * P], ACT.Identity,
                                                            scale=modc[:, 4 + 2 * c + b:5 + 2 * c + b], bias=modc[:, 2 * c + b:2 * c + b + 1])
                            last.then_inc(S["h"][b].sem, 1)
                    for b in range(NB):
                        act.wait_ge(S["cum"][b].sem, S["cum"][b].after(i))
                        act.wait_ge(S["gl"][b].sem, S["gl"][b].after(i, 1))
                        nc.scalar.activation(gam[b][:], cum[b][:], ACT.Exp, scale=-KAPPA).then_inc(S["gam"][b].sem, 1)
                        nc.scalar.activation(gami[b][:], cum[b][:], ACT.Exp, scale=KAPPA).then_inc(S["gami"][b].sem, 1)
                        act.wait_ge(S["cprev"][b].sem, S["cprev"][b].after(i))
                        nc.scalar.activation(gamp[b][:], cprev[b][:], ACT.Exp, scale=-KAPPA).then_inc(S["gamp"][b].sem, 1)
                    if more:
                        act.preload_act_table_set(EXP_TANH)


                act.preload_act_table_set(LN_EXP)
                for b in range(NB):
                    act.wait_ge(S["mean_var"][b].sem, S["mean_var"][b].after(0))
                    nc.scalar.activation(lnv[b][:], mv[b][:, 1:2], ACT.Ln, bias=const[:, 0:1]).then_inc(S["ln_var"][b].sem, 1)
                    act.wait_ge(S["ln_var"][b].sem, S["ln_var"][b].after(0))
                    act.wait_ge(S["xn"][b].sem, S["xn"][b].after(0, 1))
                    nc.scalar.activation(rstd[b][:], lnv[b][:], ACT.Exp, scale=-0.5).then_inc(S["rstd"][b].sem, 1)
                for b in range(NB):
                    act.wait_ge(S["xT"][b].sem, S["xT"][b].after(0))
                    act.wait_ge(S["xm01"][b].sem, S["xm01"][b].after(0, 1))
                    act.wait_ge(S["xm23"][b].sem, S["xm23"][b].after(0, 1))
                    act.wait_ge(S["h"][b].sem, S["h"][b].after(0, 1))
                    nc.scalar.copy(h[b][:, :, 0:1], h[b][:, :, P:P + 1]).then_inc(S["carry"][b].sem, 1)
                    act.wait_ge(S["carry"][b].sem, S["carry"][b].after(0))
                    for c in range(CC):
                        last = nc.scalar.activation(h[b][:, c, 1:P + 1], bank[b][0][:, c * P:(c + 1) * P], ACT.Identity,
                                                    scale=modc[:, 4 + 2 * c + b:5 + 2 * c + b], bias=modc[:, 2 * c + b:2 * c + b + 1])
                    last.then_inc(S["h"][b].sem, 1)
                act.preload_act_table_set(EXP_TANH)
                with act.Fori(0, NW - 1) as i:
                    window(i, True)
                window(NW - 1, False)

            @block.tensor
            def _(pe):
                mm = nc.tensor.matmul

                def project(out, name, m0, m1_, x):
                    for kc in range(CC):
                        last_ = mm(out, w2(name)[:, kc, m0:m1_], x[:, kc, :], start=(kc == 0), stop=(kc == CC - 1))
                    return last_

                def window(i, more):
                    for b in range(NB):
                        A, B, Cb, D = bank[b]
                        pe.wait_ge(S["lo_tanh"][b].sem, S["lo_tanh"][b].after(i))
                        pe.wait_ge(S["vT"][b].sem, S["vT"][b].after(i, 1))
                        pe.wait_ge(S["gates"][b].sem, S["gates"][b].after(i, 1))
                        for g in range(4):
                            for c in range(CC):
                                at = (g % 2) * C + c * P
                                last = mm([Cb, D][g // 2][:, at:at + P], w(f"maa2_{g}")[:, c * P:(c + 1) * P], lot[b][:],
                                          start=True, stop=True)
                            if g == 1:
                                last.then_inc(S["pm01"][b].sem, 1)
                        last.then_inc(S["pm23"][b].sem, 1)
                    for b in range(NB):
                        A, B, Cb, D = bank[b]
                        pe.wait_ge(S["xm01"][b].sem, S["xm01"][b].after(i))
                        pe.wait_ge(S["rkv"][b].sem, S["rkv"][b].after(i, 1))
                        project(B[:, 0:P], "wa1", 0, P, xm[b][:, 1])
                        project(B[:, P:2 * P], "gate1", 0, P, xm[b][:, 0])
                        pe.wait_ge(S["xm23"][b].sem, S["xm23"][b].after(i))
                        project(B[:, 2 * P:3 * P], "kk1", 0, P, xm[b][:, 2]).then_inc(S["hidden"][b].sem, 1)
                        for m in range(CC):
                            project(A[:, m * P:(m + 1) * P], "wr", m * P, (m + 1) * P, xm[b][:, 0])
                        for m in range(CC):
                            last = project(A[:, C + m * P:C + (m + 1) * P], "wk", m * P, (m + 1) * P, xm[b][:, 2])
                        last.then_inc(S["rk_ps"][b].sem, 1)
                        for m in range(CC):
                            last = project(Cb[:, m * P:(m + 1) * P], "wv", m * P, (m + 1) * P, xm[b][:, 3])
                        last.then_inc(S["v_ps"][b].sem, 1)
                    for b in range(NB):
                        A, B, Cb, D = bank[b]
                        pe.wait_ge(S["hidden_sb"][b].sem, S["hidden_sb"][b].after(i))
                        for m in range(CC):
                            mm(D[:, m * P:(m + 1) * P], w("decay2")[:, m * P:(m + 1) * P], th_w[b][:], start=True, stop=True)
                        for m in range(CC):
                            last = mm(D[:, C + m * P:C + (m + 1) * P], w("aaa2")[:, m * P:(m + 1) * P], th_w[b][:],
                                      start=True, stop=True)
                        last.then_inc(S["da_ps"][b].sem, 1)
                        for m in range(CC):
                            mm(B[:, m * P:(m + 1) * P], w("ma2")[:, m * P:(m + 1) * P], th_w[b][:], start=True, stop=True)
                        for m in range(CC):
                            last = mm(B[:, C + m * P:C + (m + 1) * P], w("mk2")[:, m * P:(m + 1) * P], th_k[b][:],
                                      start=True, stop=True)
                        last.then_inc(S["mm_ps"][b].sem, 1)
                        pe.wait_ge(S["rk_sb"][b].sem, S["rk_sb"][b].after(i))
                        for m in range(CC):
                            last = mm(A[:, m * P:(m + 1) * P], w("kkk2")[:, m * P:(m + 1) * P], th_k[b][:], start=True, stop=True)
                        last.then_inc(S["kk_ps"][b].sem, 1)
                        pe.wait_ge(S["v_sb"][b].sem, S["v_sb"][b].after(i))
                        for m in range(CC):
                            last = mm(Cb[:, m * P:(m + 1) * P], w("gate2")[:, m * P:(m + 1) * P], th_g[b][:], start=True, stop=True)
                        last.then_inc(S["g_ps"][b].sem, 1)
                    for b in range(NB):
                        A, B, Cb, D = bank[b]
                        pe.wait_ge(S["g_sb"][b].sem, S["g_sb"][b].after(i))
                        for c in range(CC):
                            last = nc.tensor.transpose(Cb[:, C + c * P:C + (c + 1) * P], v[b][:, c, :], ident[:])
                        last.then_inc(S["vT_ps"][b].sem, 1)
                        pe.wait_ge(S["sq"][b].sem, S["sq"][b].after(i))
                        mm(A[:, C:2 * C], ones16[:], flat(sq[b]), start=True, stop=True).then_inc(S["norm_ps"][b].sem, 1)
                    if more:
                        for b in range(NB):
                            A, B, Cb, D = bank[b]
                            pe.wait_ge(S["xn"][b].sem, S["xn"][b].after(i + 1))
                            pe.wait_ge(S["clamped"][b].sem, S["clamped"][b].after(i + 1, 1))
                            pe.wait_ge(S["kk"][b].sem, S["kk"][b].after(i + 1, 1))
                            for c in range(CC):
                                last = nc.tensor.transpose(A[:, c * P:(c + 1) * P], xn[b][:, c * P:(c + 1) * P], ident[:])
                            last.then_inc(S["xT"][b].sem, 1)
                    if more:
                        for b in range(NB):
                            pe.wait_ge(S["mix"][b].sem, S["mix"][b].after(i + 1))
                            project(bank[b][0][:, 0:P], "maa1", 0, P, mix[b]).then_inc(S["lo"][b].sem, 1)
                    for b in range(NB):
                        A, B, Cb, D = bank[b]
                        pe.wait_ge(S["rk3"][b].sem, S["rk3"][b].after(i))
                        pe.wait_ge(S["gates"][b].sem, S["gates"][b].after(i))
                        for c in range(CC):
                            last = mm(B[:, c * P:(c + 1) * P], bonus[:, c, :], rk3[b][:, c, :], start=True, stop=True)
                        last.then_inc(S["rk_ps2"][b].sem, 1)


                pe.wait_ge(s_w, 48)
                pe.wait_ge(s_c, 1)
                for b in range(NB):
                    A, B, Cb, D = bank[b]
                    pe.wait_ge(S["xn"][b].sem, S["xn"][b].after(0))
                    pe.wait_ge(S["clamped"][b].sem, S["clamped"][b].after(0, 1))
                    pe.wait_ge(S["kk"][b].sem, S["kk"][b].after(0, 1))
                    for c in range(CC):
                        last = nc.tensor.transpose(A[:, c * P:(c + 1) * P], xn[b][:, c * P:(c + 1) * P], ident[:])
                    last.then_inc(S["xT"][b].sem, 1)
                for b in range(NB):
                    pe.wait_ge(S["mix"][b].sem, S["mix"][b].after(0))
                    project(bank[b][0][:, 0:P], "maa1", 0, P, mix[b]).then_inc(S["lo"][b].sem, 1)
                with pe.Fori(0, NW - 1) as i:
                    window(i, True)
                window(NW - 1, False)


def scan_stage(nc, persist, a, T):
    NW = T // P
    BG = NB * CC
    HALF = NCH // 2
    const, ident = persist["const"], persist["ident"]
    with ExitStack() as ctx:
        sb = lambda n, s: ctx.enter_context(nc.sbuf_tensor("sc_" + n, s, F32))
        cm = [sb(f"cm{k}", [P, NB, CC, 4, P // 2]) for k in range(2)]
        v = [sb(f"v{k}", [P, NB, CC, HALF, HS]) for k in range(2)]
        gl = [sb(f"gl{k}", [P, NB, CC, HALF]) for k in range(2)]
        bx, kx = ([sb(f"{n}{k}", [P, BG, HP, CH]) for k in range(2)] for n in ("bx", "kx"))
        ax, qx = ([sb(f"{n}{c}", [P, BG, HP, CH]) for c in range(NCH)] for n in ("ax", "qx"))
        bT, kT = ([sb(f"{n}{c}", [P, BG, P]) for c in range(NCH)] for n in ("bT", "kT"))
        att = sb("att", [P, NCH, BG, 2, 2, CH])
        tt = [sb(f"tt{k}", [P, HALF, BG, CH]) for k in range(2)]
        d_ak, d_t, d_qb, d_qk = ([sb(f"{n}{k}", [P, BG, HP, CH]) for k in range(2)] for n in ("d_ak", "d_t", "d_qb", "d_qk"))
        prob = [sb(f"prob{k}", [P, CH, CH]) for k in range(2)]
        sol = [sb(f"sol{k}", [P, CH, CH]) for k in range(2)]
        step_ = sb("step", [P, CH * CH])
        causal, headmask, eye = sb("causal", [P, 2, CH]), sb("headmask", [P, HP]), sb("eye", [P, CH, CH])
        state = [sb(f"state{k}", [P, BG, HS]) for k in range(2)]
        p_sb, sa_sb, s_sum = sb("p", [P, BG, HS]), sb("sa", [P, BG, HS]), sb("ssum", [P, BG, HS])
        y = [sb(f"y{k}", [P, HALF, BG, HS]) for k in range(2)]
        dev, ysq, yn = (sb(n, [P, HALF * BG, HS]) for n in ("dev", "ysq", "yn"))
        mean, mean16, var, lnv, rs = (sb(n, [P, HALF * BG]) for n in ("mean", "mean16", "var", "lnv", "rs"))
        ps = lambda n: ctx.enter_context(nc.psum_tensor("sc_" + n, [P, 512], F32))
        P_ps, SA_ps, S_ps, Y_ps, AB_ps, AK_ps, TB_ps, TK_ps = (ps(n) for n in ("P", "SA", "S", "Y", "AB", "AK", "TB", "TK"))
        first16 = lambda bank: bank[:].rearrange("p (q r i) -> p q r i", q=BG, i=HS)[:, :, 0, :]
        S = signals(nc, ctx, "bk_x aq_x ab_ps tb_ps tk_ps att_sb bT kT d_ak d_t d_qb d_qk p_ps p_sb sa_ps sa_sb s_ps s_sum s_sb y_ps y_sb",
                    1, "sc", ahead=2 * NCH)
        Hf = signals(nc, ctx, "cm_in:32 v_in:64 att_out:16 prob_in:16 solved inv_out:16 tt_in:16 sum dev ysq var lnv rs yn mean y_out:16", 2, "sh")
        s_c, s_chain, s_state = (ctx.enter_context(nc.semaphore(n)) for n in ("sc_const", "sc_chain", "sc_state0"))
        start_signals(nc, (s_c, s_chain, s_state), S, Hf)
        S = {k_: v_[0] for k_, v_ in S.items()}
        chain = [0]

        def bg(t, q):
            return t[:, q // CC, q % CC]

        def chunk_tokens(c):
            return slice(c * CH, (c + 1) * CH)

        with nc.Block() as block:
            @block.sync
            def _(sp):
                sp.dma_start(causal[:], a["causal"]).then_inc(s_c, 16)
                sp.dma_start(headmask[:], a["headmask"]).then_inc(s_c, 16)
                sp.dma_start(eye[:], a["eye16"][:, 0]).then_inc(s_c, 16)

                def load_cm(u, k):
                    sp.wait_ge(S["aq_x"].sem, S["aq_x"].after(u * NCH - NCH + HALF * (k + 1) - 1))
                    sp.wait_ge(S["ab_ps"].sem, S["ab_ps"].after(u * NCH - NCH + HALF * (k + 1) - 1))
                    for b in range(NB):
                        sp.dma_start(cm[k][:, b].rearrange("p g x t -> p (g x) t"),
                                     a["cm"][b, bass.ds(u, 1)].rearrange("o p (gx t) -> (o p) gx t", t=P)[:, :, k * P // 2:(k + 1) * P // 2]
                                     ).then_inc(Hf["cm_in"][k].sem, 16)

                def load_v(u, k):
                    sp.wait_ge(S["y_ps"].sem, S["y_ps"].after(u * NCH - NCH + HALF * (k + 1) - 1))
                    sp.wait_ge(S["s_sb"].sem, S["s_sb"].after(u * NCH - NCH + HALF * (k + 1) - 1))
                    for b in range(NB):
                        sp.dma_start(v[k][:, b], a["v_stack"][b, bass.ds(u, 1), :, :, k * HALF:(k + 1) * HALF, :]
                                     .rearrange("o p g c i -> (o p) g c i")).then_inc(Hf["v_in"][k].sem, 16)
                        sp.dma_start(gl[k][:, b], a["gl"][b, bass.ds(u, 1)].rearrange("o p (g c) -> (o p) g c", g=CC)
                                     [:, :, k * HALF:(k + 1) * HALF]).then_inc(Hf["v_in"][k].sem, 16)

                def pose(u, k):
                    sp.wait_ge(S["att_sb"].sem, S["att_sb"].after(u * NCH + HALF * (k + 1) - 1))
                    q = bass.ds(2 * u + k, 1)
                    sp.dma_start(a["att"][q].rearrange("o (c q) h m t -> (o h m) c q t", c=HALF),
                                 att[:, k * HALF:(k + 1) * HALF, :, 0, 0, :]).then_inc(Hf["att_out"][k].sem, 16)
                    sp.wait_ge(Hf["att_out"][k].sem, Hf["att_out"][k].after(u))
                    sp.wait_ge(Hf["solved"][k].sem, Hf["solved"][k].after(u, 1))
                    sp.dma_start(prob[k][:], a["att"][q].rearrange("o q h m t -> (o q h) m t")).then_inc(Hf["prob_in"][k].sem, 16)

                def fetch(u, k):
                    q = bass.ds(2 * u + k, 1)
                    sp.wait_ge(Hf["solved"][k].sem, Hf["solved"][k].after(u))
                    sp.dma_start(a["inv"][q].rearrange("o q h m t -> (o q h) m t"), sol[k][:]).then_inc(Hf["inv_out"][k].sem, 16)
                    sp.wait_ge(Hf["inv_out"][k].sem, Hf["inv_out"][k].after(u))
                    sp.wait_ge(S["d_t"].sem, S["d_t"].after(u * NCH + HALF * (k + 1) - 1 - NCH))
                    sp.dma_start(tt[k][:], a["inv"][q].rearrange("o (c q) h m t -> (o h m) c q t", c=HALF)).then_inc(Hf["tt_in"][k].sem, 16)

                def store_y(u, k):
                    sp.wait_ge(Hf["yn"][k].sem, Hf["yn"][k].after(u))
                    sp.dma_start(a["y_stack"][bass.ds(u, 1), k].rearrange("o p n -> (o p) n"),
                                 yn[:].rearrange("p q i -> p (q i)")).then_inc(Hf["y_out"][k].sem, 16)

                load_cm(0, 0)
                load_cm(0, 1)
                load_v(0, 0)
                load_v(0, 1)
                pose(0, 0)
                load_cm(1, 0)
                fetch(0, 0)
                pose(0, 1)
                load_cm(1, 1)

                def body(u, more, further):
                    fetch(u, 1)
                    if more:
                        pose(u + 1, 0)
                        load_v(u + 1, 0)
                    if further:
                        load_cm(u + 2, 0)
                    store_y(u, 0)
                    if more:
                        fetch(u + 1, 0)
                        pose(u + 1, 1)
                        load_v(u + 1, 1)
                    store_y(u, 1)
                    if further:
                        load_cm(u + 2, 1)

                with sp.Fori(0, NW - 2) as i:
                    body(i, True, True)
                body(NW - 2, True, False)
                body(NW - 1, False, False)
                for k in range(2):
                    sp.wait_ge(Hf["y_out"][k].sem, Hf["y_out"][k].after(NW - 1))

            @block.gpsimd
            def _(pool):
                def expand(dst, x, c):
                    src = cm[c // HALF][:].rearrange("p b g x t -> p (b g) x t")[:, :, x, chunk_tokens(c % HALF)]
                    return nc.gpsimd.tensor_tensor(dst[:], src.unsqueeze(2).broadcast_to([P, BG, HP, CH]),
                                                   headmask[:].unsqueeze(1).unsqueeze(3).broadcast_to([P, BG, HP, CH]), ALU.mult)

                def prepare(u, c):
                    n = u * NCH + c
                    if c % HALF == 0:
                        pool.wait_ge(Hf["cm_in"][c // HALF].sem, Hf["cm_in"][c // HALF].after(u))
                    pool.wait_ge(S["tk_ps"].sem, S["tk_ps"].after(n, 2))
                    expand(bx[c % 2], 2, c)
                    expand(kx[c % 2], 3, c).then_inc(S["bk_x"].sem, 1)
                    pool.wait_ge(S["y_ps"].sem, S["y_ps"].after(n, NCH))
                    expand(ax[c], 0, c)
                    expand(qx[c], 1, c).then_inc(S["aq_x"].sem, 1)

                pool.wait_ge(s_c, 48)
                with pool.Fori(0, NW) as i:
                    for c in range(NCH):
                        prepare(i, c)

            @block.tensor
            def _(pe):
                mm = nc.tensor.matmul

                def prepare_products(u, c):
                    n = u * NCH + c
                    pe.wait_ge(S["bk_x"].sem, S["bk_x"].after(n))
                    pe.wait_ge(S["att_sb"].sem, S["att_sb"].after(n, 1))
                    for q in range(BG):
                        rhs = bg(cm[c // HALF], q)[:, 0:2, chunk_tokens(c % HALF)].unsqueeze(1).broadcast_to([P, P // (2 * CH), 2, CH])
                        for src, bank in ((bx, AB_ps), (kx, AK_ps)):
                            last = mm(bank[:, q * P:(q + 1) * P], src[c % 2][:, q].rearrange("p h t -> p (h t)"), rhs, start=True, stop=True)
                    last.then_inc(S["ab_ps"].sem, 1)

                def prepare_transposes(u, c):
                    n = u * NCH + c
                    for src, bank, free, done in ((bx, TB_ps, "bT", "tb_ps"), (kx, TK_ps, "kT", "tk_ps")):
                        pe.wait_ge(S[free].sem, S[free].after(n, 1))
                        for q in range(BG):
                            last = nc.tensor.transpose(bank[:, q * P:(q + 1) * P], src[c % 2][:, q].rearrange("p h t -> p (h t)"), ident[:])
                        last.then_inc(S[done].sem, 1)

                def stacked(bank, lhs, rhs, first, last_):
                    for q in range(BG):
                        ins = mm(bank[:, q * P:(q + 1) * P], lhs(q), rhs(q).unsqueeze(1).broadcast_to([P, HP, HS]), start=first and q == 0,
                                 stop=last_, skip_group_check=True)
                    return ins

                diag = lambda t: (lambda q: t[:, q].rearrange("p h t -> p (h t)"))

                def values(c):
                    return lambda q: bg(v[c // HALF], q)[:, c % HALF, :]

                def value_part(n, c):
                    pe.wait_ge(S["d_ak"].sem, S["d_ak"].after(n))
                    pe.wait_ge(S["p_sb"].sem, S["p_sb"].after(n, 1))
                    stacked(P_ps, diag(d_ak[c % 2]), values(c), True, False)

                def chunk(u, c, more):
                    n = u * NCH + c
                    s_in = state[c % 2]
                    pe.wait_ge(S["aq_x"].sem, S["aq_x"].after(n))
                    pe.wait_ge(S["s_sb"].sem, S["s_sb"].after(n, 1))
                    stacked(P_ps, diag(ax[c]), lambda q: s_in[:, q], False, True).then_inc(S["p_ps"].sem, 1)
                    pe.wait_ge(S["y_sb"].sem, S["y_sb"].after(n, 1))
                    stacked(Y_ps, diag(qx[c]), lambda q: s_in[:, q], True, False)
                    pe.wait_ge(S["d_qk"].sem, S["d_qk"].after(n))
                    stacked(Y_ps, diag(d_qk[c % 2]), values(c), False, False)
                    pe.wait_ge(S["d_t"].sem, S["d_t"].after(n))
                    pe.wait_ge(S["sa_sb"].sem, S["sa_sb"].after(n, 1))
                    pe.wait_ge(S["p_sb"].sem, S["p_sb"].after(n))
                    stacked(SA_ps, diag(d_t[c % 2]), lambda q: p_sb[:, q], True, True).then_inc(S["sa_ps"].sem, 1)
                    pe.wait_ge(S["kT"].sem, S["kT"].after(n))
                    stacked(S_ps, lambda q: kT[c][:, q], values(c), True, False)
                    if more:
                        prepare_products(u + 1, c)
                    pe.wait_ge(S["sa_sb"].sem, S["sa_sb"].after(n))
                    stacked(S_ps, lambda q: bT[c][:, q], lambda q: sa_sb[:, q], False, True).then_inc(S["s_ps"].sem, 1)
                    pe.wait_ge(S["d_qb"].sem, S["d_qb"].after(n))
                    stacked(Y_ps, diag(d_qb[c % 2]), lambda q: sa_sb[:, q], False, True).then_inc(S["y_ps"].sem, 1)
                    if c < NCH - 1 or more:
                        k = (c + 1) % NCH
                        if k % HALF == 0:
                            pe.wait_ge(Hf["v_in"][k // HALF].sem, Hf["v_in"][k // HALF].after(u + (c + 1) // NCH))
                        value_part(n + 1, k)
                    if more:
                        prepare_transposes(u + 1, c)

                for c in range(NCH):
                    prepare_products(0, c)
                    prepare_transposes(0, c)
                pe.wait_ge(Hf["v_in"][0].sem, Hf["v_in"][0].after(0))
                pe.wait_ge(s_state, 1)
                pe.wait_ge(S["aq_x"].sem, S["aq_x"].after(NCH - 1))
                value_part(0, 0)
                with pe.Fori(0, NW - 1) as i:
                    for c in range(NCH):
                        chunk(i, c, True)
                for c in range(NCH):
                    chunk(NW - 1, c, False)

            @block.scalar
            def _(act):
                def prepare(u, c):
                    n = u * NCH + c
                    act.wait_ge(S["tb_ps"].sem, S["tb_ps"].after(n))
                    act.wait_ge(S["s_ps"].sem, S["s_ps"].after(n, NCH))
                    nc.scalar.copy(bT[c][:].rearrange("p q t -> p (q t)"), TB_ps[:]).then_inc(S["bT"].sem, 1)
                    act.wait_ge(S["tk_ps"].sem, S["tk_ps"].after(n))
                    nc.scalar.copy(kT[c][:].rearrange("p q t -> p (q t)"), TK_ps[:]).then_inc(S["kT"].sem, 1)

                def head_norm(u, k):
                    act.wait_ge(Hf["dev"][k].sem, Hf["dev"][k].after(u))
                    nc.scalar.activation(ysq[:], dev[:], ACT.Square).then_inc(Hf["ysq"][k].sem, 1)
                    act.wait_ge(Hf["var"][k].sem, Hf["var"][k].after(u))
                    nc.scalar.activation(lnv[:], var[:], ACT.Ln, scale=1.0 / HS, bias=const[:, 3:4]).then_inc(Hf["lnv"][k].sem, 1)
                    act.wait_ge(Hf["lnv"][k].sem, Hf["lnv"][k].after(u))
                    nc.scalar.activation(rs[:], lnv[:], ACT.Exp, scale=-0.5).then_inc(Hf["rs"][k].sem, 1)

                def chunk(u, c, more):
                    n = u * NCH + c
                    act.wait_ge(S["sa_ps"].sem, S["sa_ps"].after(n))
                    act.wait_ge(S["y_ps"].sem, S["y_ps"].after(n, 1))
                    nc.scalar.copy(sa_sb[:], first16(SA_ps)).then_inc(S["sa_sb"].sem, 1)
                    act.wait_ge(S["y_ps"].sem, S["y_ps"].after(n))
                    if c % HALF == 0:
                        act.wait_ge(Hf["dev"][c // HALF].sem, Hf["dev"][c // HALF].after(u, 1))
                        act.wait_ge(Hf["sum"][c // HALF].sem, Hf["sum"][c // HALF].after(u, 1))
                    nc.scalar.copy(y[c // HALF][:, c % HALF], first16(Y_ps)).then_inc(S["y_sb"].sem, 1)
                    if more:
                        prepare(u + 1, c)
                    if c == HALF:
                        head_norm(u, 0)
                    if c == NCH - 1:
                        head_norm(u, 1)

                act.preload_act_table_set(LN_EXP)
                for c in range(NCH):
                    prepare(0, c)
                with act.Fori(0, NW - 1) as i:
                    for c in range(NCH):
                        chunk(i, c, True)
                for c in range(NCH):
                    chunk(NW - 1, c, False)

            @block.vector
            def _(dve):
                dve.wait_ge(s_c, 48)
                nc.vector.memset(state[0][:], 0.0).then_inc(s_state, 1)

                def mask_products(u, c):
                    n = u * NCH + c
                    dve.wait_ge(S["ab_ps"].sem, S["ab_ps"].after(n))
                    if c % HALF == 0:
                        dve.wait_ge(Hf["att_out"][c // HALF].sem, Hf["att_out"][c // HALF].after(u, 1))
                    dve.wait_ge(S["d_qk"].sem, S["d_qk"].after(n, NCH))
                    dve.wait_ge(S["d_qb"].sem, S["d_qb"].after(n, NCH))
                    dve.wait_ge(S["d_ak"].sem, S["d_ak"].after(n, NCH))
                    for x, bank in enumerate((AB_ps, AK_ps)):
                        last = nc.vector.tensor_tensor(att[:, c, :, x].rearrange("p q y t -> p q (y t)"),
                                                       bank[:].rearrange("p (q r t) -> p q r t", q=BG, t=2 * CH)[:, :, 0, :],
                                                       causal[:].rearrange("p y t -> p (y t)").unsqueeze(1).broadcast_to([P, BG, 2 * CH]),
                                                       ALU.mult)
                    last.then_inc(S["att_sb"].sem, 1)

                def diagonal(dst, src, done):
                    nc.vector.tensor_tensor(dst[:], src.unsqueeze(2).broadcast_to([P, BG, HP, CH]),
                                            headmask[:].unsqueeze(1).unsqueeze(3).broadcast_to([P, BG, HP, CH]), ALU.mult
                                            ).then_inc(done.sem, 1)

                def diagonals(u, c, which):
                    n = u * NCH + c
                    k = c % 2
                    if which == 0:
                        dve.wait_ge(S["y_ps"].sem, S["y_ps"].after(n, 2))
                        dve.wait_ge(S["att_sb"].sem, S["att_sb"].after(n))
                        diagonal(d_ak[k], att[:, c, :, 1, 0, :], S["d_ak"])
                        diagonal(d_qk[k], att[:, c, :, 1, 1, :], S["d_qk"])
                    else:
                        diagonal(d_qb[k], att[:, c, :, 0, 1, :], S["d_qb"])
                        if c % HALF == 0:
                            dve.wait_ge(Hf["tt_in"][c // HALF].sem, Hf["tt_in"][c // HALF].after(u))
                        diagonal(d_t[k], tt[c // HALF][:, c % HALF], S["d_t"])

                def solve(u, k, m0, m1, wrap):
                    x = sol[k]
                    if m0 == 0:
                        dve.wait_ge(Hf["prob_in"][k].sem, Hf["prob_in"][k].after(u))
                        dve.wait_ge(Hf["inv_out"][k].sem, Hf["inv_out"][k].after(u, 1))
                        nc.vector.tensor_copy(x[:], eye[:]).then_inc(s_chain, 1)
                        chain[0] += 1
                    for m in range(m0, m1):
                        rows, cols = m + 1, CH - 1 - m
                        prod = step_[:, 0:rows * cols].rearrange("p (r t) -> p r t", r=rows)
                        dve.wait_ge(s_chain, chain[0])
                        nc.vector.tensor_tensor(prod, prob[k][:, m:m + 1, m + 1:CH].broadcast_to([P, rows, cols]),
                                                x[:, 0:rows, m:m + 1].broadcast_to([P, rows, cols]), ALU.mult).then_inc(s_chain, 1)
                        chain[0] += 1
                        dve.wait_ge(s_chain, chain[0])
                        ins = nc.vector.tensor_tensor(x[:, 0:rows, m + 1:CH], x[:, 0:rows, m + 1:CH], prod, ALU.add)
                        if m < CH - 2:
                            ins.then_inc(s_chain, 1)
                            chain[0] += 1
                        else:
                            ins.then_inc(Hf["solved"][k].sem, 1)
                            dve.sem_clear(s_chain)
                            chain[0] = 0

                def head_norm(u, k):
                    yk = y[k][:].rearrange("p c q i -> p (c q) i")
                    dve.wait_ge(S["y_sb"].sem, S["y_sb"].after(u * NCH + HALF * (k + 1) - 1))
                    nc.vector.tensor_reduce(mean[:], yk, AX.X, ALU.add).then_inc(Hf["sum"][k].sem, 1)
                    dve.wait_ge(Hf["sum"][k].sem, Hf["sum"][k].after(u))
                    nc.vector.tensor_scalar(mean16[:], mean[:], 1.0 / HS, None, ALU.mult).then_inc(Hf["mean"][k].sem, 1)
                    dve.wait_ge(Hf["mean"][k].sem, Hf["mean"][k].after(u))
                    nc.vector.tensor_tensor(dev[:], yk, mean16[:].unsqueeze(2).broadcast_to([P, HALF * BG, HS]), ALU.subtract
                                            ).then_inc(Hf["dev"][k].sem, 1)

                def head_norm_end(u, k):
                    dve.wait_ge(Hf["ysq"][k].sem, Hf["ysq"][k].after(u))
                    nc.vector.tensor_reduce(var[:], ysq[:], AX.X, ALU.add).then_inc(Hf["var"][k].sem, 1)
                    dve.wait_ge(Hf["rs"][k].sem, Hf["rs"][k].after(u))
                    dve.wait_ge(Hf["y_out"][1 - k].sem, Hf["y_out"][1 - k].after(u, 1 - k))
                    nc.vector.tensor_tensor(yn[:].rearrange("p (g cb) i -> p cb g i", g=CC), dev[:].rearrange("p (cb g) i -> p cb g i", g=CC),
                                            rs[:].rearrange("p (cb g) -> p cb g", g=CC).unsqueeze(3).broadcast_to([P, HALF * NB, CC, HS]),
                                            ALU.mult).then_inc(Hf["yn"][k].sem, 1)

                def chunk(u, c, more):
                    n = u * NCH + c
                    ahead = c < NCH - 1 or more
                    nu, ncn = (u, c + 1) if c < NCH - 1 else (u + 1, 0)
                    dve.wait_ge(S["p_ps"].sem, S["p_ps"].after(n))
                    dve.wait_ge(S["sa_ps"].sem, S["sa_ps"].after(n, 1))
                    nc.vector.tensor_copy(p_sb[:], first16(P_ps)).then_inc(S["p_sb"].sem, 1)
                    if ahead:
                        diagonals(nu, ncn, 0)
                    if c in (1, 2):
                        solve(u, 1, *((0, 8) if c == 1 else (8, CH - 1)), c)
                    if c in (5, 6) and more:
                        solve(u + 1, 0, *((0, 8) if c == 5 else (8, CH - 1)), c)
                    dve.wait_ge(S["s_ps"].sem, S["s_ps"].after(n))
                    dve.wait_ge(S["s_sb"].sem, S["s_sb"].after(n, 1))
                    nc.vector.tensor_tensor(s_sum[:], first16(S_ps), state[c % 2][:], ALU.add).then_inc(S["s_sum"].sem, 1)
                    dve.wait_ge(S["y_ps"].sem, S["y_ps"].after(n, 1))
                    dve.wait_ge(S["s_sum"].sem, S["s_sum"].after(n))
                    nc.vector.tensor_tensor(state[(c + 1) % 2][:], s_sum[:],
                                            gl[c // HALF][:].rearrange("p b g c -> p (b g) c")[:, :, c % HALF:c % HALF + 1]
                                            .broadcast_to([P, BG, HS]), ALU.mult).then_inc(S["s_sb"].sem, 1)
                    if more:
                        mask_products(u + 1, c)
                    if ahead:
                        diagonals(nu, ncn, 1)
                    if c == HALF:
                        head_norm(u, 0)
                        head_norm_end(u, 0)
                    if c == NCH - 1:
                        head_norm(u, 1)
                        head_norm_end(u, 1)

                for c in range(NCH):
                    mask_products(0, c)
                dve.wait_ge(Hf["v_in"][0].sem, Hf["v_in"][0].after(0))
                diagonals(0, 0, 0)
                solve(0, 0, 0, CH - 1, -1)
                diagonals(0, 0, 1)
                with dve.Fori(0, NW - 1) as i:
                    for c in range(NCH):
                        chunk(i, c, True)
                for c in range(NCH):
                    chunk(NW - 1, c, False)


def gate_stage(nc, persist, a, T):
    NW = T // P
    SW = 2
    modc, rows, vec, const, ident = (persist[k] for k in ("modc", "rows", "vec", "const", "ident"))
    streams = [(w, b) for w in range(SW) for b in range(NB)]
    with ExitStack() as ctx:
        sb = lambda n, s: [ctx.enter_context(nc.sbuf_tensor(f"ga_{n}{k}", s, F32)) for k in range(len(streams))]
        wo = ctx.enter_context(nc.sbuf_tensor("ga_wo", [P, CC, C], F32))
        wos = [ctx.enter_context(nc.sbuf_tensor(f"ga_wos{b}", [P, CC, C], F32)) for b in range(NB)]
        zero = ctx.enter_context(nc.sbuf_tensor("ga_zero", [P, CC, 1], F32))
        pause = ctx.enter_context(nc.sbuf_tensor("ga_pause", [P, len(streams)], F32))
        yt, gr, xt = sb("yt", [P, C]), sb("gr", [P, 2, C]), sb("xt", [P, C])
        yl, z1, z, xa = sb("yl", [P, C]), sb("z1", [P, C]), sb("z", [P, C]), sb("xa", [P, C])
        st, mv, lnv, rstd = sb("st", [P, 6]), sb("mv", [P, 2]), sb("lnv", [P, 1]), sb("rstd", [P, 1])
        xn, h0 = sb("xn", [P, C]), sb("h0", [P, C])
        bank = [[ctx.enter_context(nc.psum_tensor(f"ga{n}{k}", [P, 512], F32)) for n in "AB"] for k in range(len(streams))]
        S = signals(nc, ctx, "y_in:128 gr_in:16 x_in:16 yT yl z1 z out_ps xa stats mean_var ln_var rstd xn xT h0 xa_out:16 h0_out:16",
                    len(streams), "ga")
        s_c, s_ws, s_zero = (ctx.enter_context(nc.semaphore(f"ga_{n}")) for n in ("const", "wos", "zero"))
        start_signals(nc, (s_c, s_ws, s_zero), S)
        each = lambda: enumerate(streams)
        with nc.Block() as block:
            @block.sync
            def _(sp):
                sp.dma_start(wo[:], a["wo_attn"]).then_inc(s_c, 16)

                def load_y(i):
                    for k, (w, b) in each():
                        sp.wait_ge(S["yT"][k].sem, S["yT"][k].after(i, 1))
                        for c in range(NCH):
                            sp.dma_start(yt[k][c * CH:(c + 1) * CH, :].rearrange("t (g h i) -> t g h i", g=CC, h=HP),
                                         a["y_stack"][bass.ds(i * SW + w, 1), c * 2 // NCH].rearrange(
                                             "o (h t) (g c b i) -> (o c) b t g h i", t=CH, b=NB, g=CC, i=HS)[c % (NCH // 2), b]
                                         ).then_inc(S["y_in"][k].sem, 16)

                def load_gr(i):
                    for k, (w, b) in each():
                        sp.wait_ge(S["z"][k].sem, S["z"][k].after(i, 1))
                        sp.dma_start(gr[k][:], a["gr"][b, bass.ds(i * SW + w, 1)].rearrange("o p (x n) -> (o p) x n", x=2)
                                     ).then_inc(S["gr_in"][k].sem, 16)

                def load_x(i):
                    for k, (w, b) in each():
                        sp.wait_ge(S["xa"][k].sem, S["xa"][k].after(i, 1))
                        sp.dma_start(xt[k][:], a["x"][b, bass.ds((i * SW + w) * P, P), :]).then_inc(S["x_in"][k].sem, 16)

                def body(i, more):
                    if more:
                        load_y(i + 1)
                        load_gr(i + 1)
                        load_x(i + 1)
                    for k, (w, b) in each():
                        sp.wait_ge(S["xa"][k].sem, S["xa"][k].after(i))
                        sp.dma_start(a["xa"][b, bass.ds((i * SW + w) * P, P), :], xa[k][:]).then_inc(S["xa_out"][k].sem, 16)
                    for k, (w, b) in each():
                        sp.wait_ge(S["h0"][k].sem, S["h0"][k].after(i))
                        sp.dma_start(a["h0"][b, :, :, bass.ds((i * SW + w) * P + 1, P)], h0[k][:].rearrange("p (c t) -> p c t", c=CC)
                                     ).then_inc(S["h0_out"][k].sem, 16)

                load_y(0)
                load_gr(0)
                load_x(0)
                with sp.Fori(0, NW // SW - 1) as i:
                    body(i, True)
                body(NW // SW - 1, False)
                for k, _ in each():
                    sp.wait_ge(S["xa_out"][k].sem, S["xa_out"][k].after(NW // SW - 1))
                    sp.wait_ge(S["h0_out"][k].sem, S["h0_out"][k].after(NW // SW - 1))

            @block.scalar
            def _(act):
                act.preload_act_table_set(LN_EXP)
                act.wait_ge(s_zero, 1)
                for b in range(NB):
                    act.dma_start(a["h0"][b, :, :, 0:1], zero[:], allow_slow_non_contiguous=True).then_inc(s_zero, 16)
                with act.Fori(0, NW // SW) as i:
                    for k, (w, b) in each():
                        act.wait_ge(S["yT"][k].sem, S["yT"][k].after(i))
                        act.wait_ge(S["z1"][k].sem, S["z1"][k].after(i, 1))
                        for c in range(CC):
                            last = nc.scalar.activation(yl[k][:, c * P:(c + 1) * P], bank[k][0][:, c * P:(c + 1) * P], ACT.Identity,
                                                        scale=vec[:, 10, c:c + 1], bias=vec[:, 11, c:c + 1])
                        last.then_inc(S["yl"][k].sem, 1)
                    for k, (w, b) in each():
                        act.wait_ge(S["mean_var"][k].sem, S["mean_var"][k].after(i))
                        nc.scalar.activation(lnv[k][:], mv[k][:, 1:2], ACT.Ln, bias=const[:, 0:1]).then_inc(S["ln_var"][k].sem, 1)
                        act.wait_ge(S["ln_var"][k].sem, S["ln_var"][k].after(i))
                        act.wait_ge(S["xn"][k].sem, S["xn"][k].after(i, 1))
                        nc.scalar.activation(rstd[k][:], lnv[k][:], ACT.Exp, scale=-0.5).then_inc(S["rstd"][k].sem, 1)
                    for k, (w, b) in each():
                        act.wait_ge(S["xT"][k].sem, S["xT"][k].after(i))
                        act.wait_ge(S["h0_out"][k].sem, S["h0_out"][k].after(i, 1))
                        for c in range(CC):
                            last = nc.scalar.activation(h0[k][:, c * P:(c + 1) * P], bank[k][1][:, c * P:(c + 1) * P], ACT.Identity,
                                                        scale=modc[:, 16 + 2 * c + b:17 + 2 * c + b],
                                                        bias=modc[:, 12 + 2 * c + b:13 + 2 * c + b])
                        last.then_inc(S["h0"][k].sem, 1)
                act.wait_ge(s_zero, 1 + 16 * NB)

            @block.vector
            def _(dve):
                nc.vector.memset(zero[:], 0.0).then_inc(s_zero, 1)
                dve.wait_ge(s_c, 16)
                for b in range(NB):
                    last = nc.vector.tensor_tensor(wos[b][:], wo[:], rows[:, b * C:(b + 1) * C].unsqueeze(1).broadcast_to([P, CC, C]), ALU.mult)
                last.then_inc(s_ws, 1)
                with dve.Fori(0, NW // SW) as i:
                    for k, (w, b) in each():
                        dve.wait_ge(S["yl"][k].sem, S["yl"][k].after(i))
                        dve.wait_ge(S["gr_in"][k].sem, S["gr_in"][k].after(i))
                        dve.wait_ge(S["z"][k].sem, S["z"][k].after(i, 1))
                        nc.vector.tensor_tensor(z1[k][:], yl[k][:], gr[k][:, 1], ALU.add).then_inc(S["z1"][k].sem, 1)
                    for k, (w, b) in each():
                        dve.wait_ge(S["z1"][k].sem, S["z1"][k].after(i))
                        dve.wait_ge(S["out_ps"][k].sem, S["out_ps"][k].after(i, 1))
                        nc.vector.tensor_tensor(z[k][:], z1[k][:], gr[k][:, 0], ALU.mult).then_inc(S["z"][k].sem, 1)
                    for k, (w, b) in each():
                        dve.wait_ge(S["out_ps"][k].sem, S["out_ps"][k].after(i))
                        dve.wait_ge(S["x_in"][k].sem, S["x_in"][k].after(i))
                        dve.wait_ge(S["xa_out"][k].sem, S["xa_out"][k].after(i, 1))
                        nc.vector.tensor_tensor(xa[k][:], bank[k][0][:, C:2 * C], xt[k][:], ALU.add).then_inc(S["xa"][k].sem, 1)
                    for k, (w, b) in each():
                        dve.wait_ge(S["xa"][k].sem, S["xa"][k].after(i))
                        nc.vector.bn_stats(st[k][:], xa[k][:]).then_inc(S["stats"][k].sem, 1)
                    for k, (w, b) in each():
                        dve.wait_ge(S["stats"][k].sem, S["stats"][k].after(i))
                        dve.wait_ge(S["ln_var"][k].sem, S["ln_var"][k].after(i, 1))
                        nc.vector.memset(pause[:, k:k + 1], 0.0)
                        nc.vector.bn_aggr(mv[k][:], st[k][:]).then_inc(S["mean_var"][k].sem, 1)
                    for k, (w, b) in each():
                        dve.wait_ge(S["rstd"][k].sem, S["rstd"][k].after(i))
                        dve.wait_ge(S["xT"][k].sem, S["xT"][k].after(i, 1))
                        nc.vector.tensor_scalar(xn[k][:], xa[k][:], mv[k][:, 0:1], rstd[k][:], ALU.subtract, ALU.mult
                                                ).then_inc(S["xn"][k].sem, 1)

            @block.tensor
            def _(pe):
                pe.wait_ge(s_ws, 1)
                with pe.Fori(0, NW // SW) as i:
                    for k, (w, b) in each():
                        pe.wait_ge(S["y_in"][k].sem, S["y_in"][k].after(i))
                        pe.wait_ge(S["yl"][k].sem, S["yl"][k].after(i, 1))
                        pe.wait_ge(S["xa"][k].sem, S["xa"][k].after(i, 1))
                        for c in range(CC):
                            last = nc.tensor.transpose(bank[k][0][:, c * P:(c + 1) * P], yt[k][:, c * P:(c + 1) * P], ident[:])
                        last.then_inc(S["yT"][k].sem, 1)
                    for k, (w, b) in each():
                        pe.wait_ge(S["z"][k].sem, S["z"][k].after(i))
                        for c in range(CC):
                            last = nc.tensor.matmul(bank[k][0][:, C:2 * C], z[k][:, c * P:(c + 1) * P], wos[b][:, c, :],
                                                    start=(c == 0), stop=(c == CC - 1))
                        last.then_inc(S["out_ps"][k].sem, 1)
                    for k, (w, b) in each():
                        pe.wait_ge(S["xn"][k].sem, S["xn"][k].after(i))
                        pe.wait_ge(S["h0"][k].sem, S["h0"][k].after(i, 1))
                        for c in range(CC):
                            last = nc.tensor.transpose(bank[k][1][:, c * P:(c + 1) * P], xn[k][:, c * P:(c + 1) * P], ident[:])
                        last.then_inc(S["xT"][k].sem, 1)


def local_stage(nc, persist, a, T, layer):
    NW = T // P
    NHP = HEADS // 2
    LAST = layer == 1
    rows, const, ident = (persist[k] for k in ("rows", "const", "ident"))
    src = a["h1"] if LAST else a["h0"]
    G = ((0, 1), (2, 3), (4, 5))
    with ExitStack() as ctx:
        one = lambda n, s, d=F32: ctx.enter_context(nc.sbuf_tensor(f"l{layer}_{n}", s, d))
        two = lambda n, s, d=F32: [one(f"{n}{k}", s, d) for k in range(2)]
        wqkv, wo = one("wqkv", [P, CC, 3 * INNER]), one("wo", [P, NHP, C])
        w1, w2 = one("w1", [P, CC, 2, MT * MW]), one("w2", [MW, MT, C])
        b1, b1c, lngb = one("b1", [MW, 2, MT]), one("b1c", [MW, 2, MT]), one("lngb", [P, 3, CC])
        qks, rot, tab = one("qks", [P, 4, DH]), two("rot", [P, 4, DH]), two("tab", [P, 4, DH])
        wm = one("wm", [P, 2 * P])
        mean_w, pause = one("mean_w", [P, P]), one("pause", [P, NB])
        mask = [two(f"mask{s}_", [P, 2, P]) for s in range(NB)]
        hT = [two(f"h{s}_", [P, CC, P + 1]) for s in range(NB)]
        x1 = [two(f"x1{s}_", [P, CC, P + 1]) for s in range(NB)]
        sqq, sqk, q1, q2, qr, kn, k1, k2, kr = (two(n, [P, HEADS, DH]) for n in "sqq sqk q1 q2 qr kn k1 k2 kr".split())
        ss, ssc, lnn, rn = (two(n, [P, 2 * HEADS]) for n in ("ss", "ssc", "lnn", "rn"))
        rq8, mx, nb, sums, rinv = (two(n, [P, HEADS]) for n in ("rq8", "mx", "nb", "sums", "rinv"))
        qz, kT = two("qz", [P, HEADS, P]), two("kT", [P, NHP, 2, P])
        V, prob, pT = two("V", [P, 2, HEADS, DH]), two("prob", [P, HEADS, 2 * P]), two("pT", [P, HEADS, 2, P])
        oT, pn = two("oT", [P, NHP, P]), two("pn", [P, HEADS, 2 * P])
        dev, dsq, hn, hout = (two(n, [P, CC, P]) for n in ("dev", "dsq", "hn", "hout"))
        lnv, rstd = two("lnv", [P, P]), two("rstd", [P, P])
        gel, hid = two("gel", [MW, MT, P]), two("hid", [MW, MT, P])
        if LAST:
            xat, t1, outt = two("xat", [P, C]), two("t1", [P, C]), two("outt", [P, C])
        else:
            zero = one("zero", [P, CC, 1])
        bank = [[ctx.enter_context(nc.psum_tensor(f"l{layer}{n}{s}", [P, 512], F32)) for n in "ABCD"] for s in range(NB)]
        sems = {n: ctx.enter_context(nc.semaphore(f"l{layer}_{n}")) for n in ("w", "set", "prep", "bias", "zero")}
        R = signals(nc, ctx, "tab", 1, f"l{layer}r")
        S = signals(nc, ctx, "q_ps k_ps v_ps qsq ksq v_sb ss_q ss clamped ln_n rn rq8 kn qm qr k12 kr qT_ps kT_ps qz kT "
                    "mask0 wo_ps carry x1 mean_ps dev dsq var_ps ln_v rstd hn w2_ps hout yT t1 "
                    "xa_in:16 outt out:16", 2, f"l{layer}")
        Q = signals(nc, ctx, "sc mx nb exp rinv pn pt_ps pv oT", 2, f"l{layer}q", ahead=2 * NHP)
        M = signals(nc, ctx, "w1_ps gel hid", 2, f"l{layer}m", ahead=6)
        parity = ("pT_even", "pT_odd")
        E = signals(nc, ctx, "pT_even pT_odd", 2, f"l{layer}e", ahead=NHP)
        I = [signals(nc, ctx, "h_in:8 rot_in:8", 2, f"l{layer}i{w}_") for w in range(2)]
        start_signals(nc, tuple(sems.values()), R, S, Q, M, E, *I)
        tab_made = R["tab"][0]
        flat = lambda t: t[:].rearrange("p c t -> p (c t)")
        shifted = lambda t: t[:].rearrange("p c t -> p (c t)")[:, 1:CC * P + 1]
        heads = lambda t, s: t[s][:].unsqueeze(2).broadcast_to([P, HEADS, DH])

        def program(att, mlp, prologue, mean_first):
            def both(sa, ua, wa, sm, um, wm_):
                if mean_first:
                    mlp(sm, um, wm_, "mean")
                att(sa, ua, wa, "q")
                if not mean_first:
                    mlp(sm, um, wm_, "mean")
                att(sa, ua, wa, "k")
                mlp(sm, um, wm_, "variance")
                att(sa, ua, wa, "v")
                att(sa, ua, wa, "turn_q")
                mlp(sm, um, wm_, "hidden")
                att(sa, ua, wa, "turn_k")
                att(sa, ua, wa, "scores")
                att(sa, ua, wa, "sums")
                mlp(sm, um, wm_, "out")
                att(sa, ua, wa, "values")

            def body(i, more):
                for w in range(2):
                    u = 2 * i + w
                    both(1, u, w, 0, u, w)
                    if w == 0 or more:
                        both(0, u + 1, 1 - w, 1, u, w)
                    else:
                        for part in ("mean", "variance", "hidden", "out"):
                            mlp(1, u, w, part)

            prologue()
            for part in ("q", "k", "v", "turn_q", "turn_k", "scores", "sums", "values"):
                att(0, 0, 0, part)
            return body

        def run(eng, att, mlp, prologue, mean_first=False):
            body = program(att, mlp, prologue, mean_first)
            with eng.Fori(0, NW // 2 - 1) as i:
                body(i, True)
            body(NW // 2 - 1, False)

        turned = lambda s, hp: bank[s][hp % (NHP - 1)]
        OUT = (3, 1)

        with nc.Block() as block:
            @block.sync
            def _(sp):
                def att(s, u, w, part):
                    if part == "q":
                        sp.wait_ge(S["x1"][s].sem, S["x1"][s].after(u, 2))
                        sp.dma_start(hT[s][w][:], src[s, :, :, bass.ds(u * P, P + 1)]).then_inc(I[w]["h_in"][s].sem, 16)
                        if s == 0:
                            sp.wait_ge(tab_made.sem, tab_made.after(u, 2))
                            sp.dma_start(rot[w][:], a["rotary"][bass.ds(u * P, P)]).then_inc(I[w]["rot_in"][0].sem, 16)

                def mlp(s, u, w, part):
                    if part == "mean" and LAST:
                        sp.wait_ge(S["outt"][s].sem, S["outt"][s].after(u, 1))
                        sp.dma_start(xat[s][:], a["xa"][s, bass.ds(u * P, P), :]).then_inc(S["xa_in"][s].sem, 16)

                    if part == "out":
                        sp.wait_ge(S["outt" if LAST else "hout"][s].sem, S["outt" if LAST else "hout"][s].after(u))
                        if LAST:
                            sp.dma_start(a["out"][s, bass.ds(u * P, P), :], outt[s][:]).then_inc(S["out"][s].sem, 16)
                        else:
                            sp.dma_start(a["h1"][s, :, :, bass.ds(u * P + 1, P)], hout[s][:]).then_inc(S["out"][s].sem, 16)

                def prologue():
                    for dst, name in ((wqkv, "wqkv"), (wo, "wo"), (w1, "w1"), (w2, "w2"), (b1, "b1"), (lngb, "ln_gb"), (qks, "qk_scale")):
                        view = a[name][layer]
                        d = dst[:].rearrange("p c x n -> p c (x n)") if name == "w1" else dst[:]
                        sp.dma_start(d, view).then_inc(sems["w"], 16)
                    sp.dma_start(wm[:], a["winmask"]).then_inc(sems["w"], 16)

                run(sp, att, mlp, prologue)
                for s in range(NB):
                    sp.wait_ge(S["out"][s].sem, S["out"][s].after(NW - 1))

            @block.gpsimd
            def _(pool):
                tt = nc.gpsimd.tensor_tensor

                def prologue():
                    for s in range(NB):
                        for t in (qz[s], kT[s], V[s]):
                            nc.gpsimd.memset(t[:], 0.0)
                        nc.gpsimd.memset(x1[s][1][:], 0.0)
                        nc.gpsimd.memset(mask[s][0][:], MASKED)
                    if not LAST:
                        nc.gpsimd.memset(zero[:], 0.0)
                    nc.gpsimd.memset(mean_w[:], 1.0 / C).then_inc(sems["set"], 1)
                    pool.wait_ge(sems["w"], 128)

                def att(s, u, w, part):
                    if part == "q" and s == 0:
                            pool.wait_ge(I[w]["rot_in"][0].sem, I[w]["rot_in"][0].after(u - w, -1))
                            for b in range(NB):
                                pool.wait_ge(S["qm"][b].sem, S["qm"][b].after(u, 2))
                                pool.wait_ge(S["kr"][b].sem, S["kr"][b].after(u, 2))
                            tt(tab[w][:], rot[w][:], qks[:], ALU.mult).then_inc(tab_made.sem, 1)
                    if part == "turn_k":
                        pool.wait_ge(S["kn"][s].sem, S["kn"][s].after(u))
                        pool.wait_ge(tab_made.sem, tab_made.after(u))
                        lo, hi = slice(0, DH // 2), slice(DH // 2, DH)
                        wide = lambda j, d: tab[w][:, j:j + 1, d].broadcast_to([P, HEADS, d.stop - d.start])
                        pool.wait_ge(S["kr"][s].sem, S["kr"][s].after(u, 1))
                        tt(k1[s][:], kn[s][:], wide(2, slice(0, DH)), ALU.mult)
                        tt(k2[s][:, :, lo], kn[s][:, :, hi], wide(3, lo), ALU.mult)
                        tt(k2[s][:, :, hi], kn[s][:, :, lo], wide(3, hi), ALU.mult).then_inc(S["k12"][s].sem, 1)
                        pool.wait_ge(S["k12"][s].sem, S["k12"][s].after(u))
                        pool.wait_ge(S["kT_ps"][s].sem, S["kT_ps"][s].after(u, 1))
                        tt(kr[s][:], k1[s][:], k2[s][:], ALU.add).then_inc(S["kr"][s].sem, 1)
                    if part == "sums":
                        for hp in range(NHP):
                            n = u * NHP + hp
                            pool.wait_ge(Q["rinv"][s].sem, Q["rinv"][s].after(n))
                            pool.wait_ge(Q["pt_ps"][s].sem, Q["pt_ps"][s].after(n, NHP))
                            pair = slice(2 * hp, 2 * hp + 2)
                            tt(pn[s][:, pair], prob[s][:, pair], rinv[s][:, pair].unsqueeze(2).broadcast_to([P, 2, 2 * P]), ALU.mult
                               ).then_inc(Q["pn"][s].sem, 1)

                def mlp(s, u, w, part):
                    if part == "hidden":
                        pool.wait_ge(S["dev"][s].sem, S["dev"][s].after(u))
                        pool.wait_ge(S["rstd"][s].sem, S["rstd"][s].after(u))
                        pool.wait_ge(M["w1_ps"][s].sem, M["w1_ps"][s].after(u * 3 - 1))
                        tt(hn[s][:], dev[s][:], rstd[s][:].unsqueeze(1).broadcast_to([P, CC, P]), ALU.mult).then_inc(S["hn"][s].sem, 1)
                    if part == "out" and LAST:
                        pool.wait_ge(S["t1"][s].sem, S["t1"][s].after(u))
                        pool.wait_ge(S["xa_in"][s].sem, S["xa_in"][s].after(u))
                        pool.wait_ge(S["out"][s].sem, S["out"][s].after(u, 1))
                        tt(outt[s][:], t1[s][:], xat[s][:], ALU.add).then_inc(S["outt"][s].sem, 1)

                run(pool, att, mlp, prologue)

            @block.vector
            def _(dve):
                tt = nc.vector.tensor_tensor

                def prologue():
                    dve.wait_ge(sems["w"], 128)
                    dve.wait_ge(sems["bias"], 1)
                    dve.wait_ge(sems["set"], 1)
                    tt(b1c[:], bank[0][0][0:MW, 0:2 * MT].rearrange("p (x m) -> p x m", x=2), b1[:], ALU.add)
                    for k in range(CC):
                        nc.vector.tensor_scalar(w1[:, k], w1[:, k], lngb[:, 0, k:k + 1], None, ALU.mult)
                    for s in range(NB):
                        nc.vector.tensor_copy(mask[s][0][:, 0, :], wm[:, P:2 * P])
                        last = nc.vector.tensor_copy(mask[s][1][:].rearrange("p x n -> p (x n)"), wm[:])
                    last.then_inc(sems["prep"], 1)
                    dve.wait_ge(sems["prep"], 1)

                def att(s, u, w, part):
                    A, B, Cb, D = bank[s]
                    lo, hi = slice(0, DH // 2), slice(DH // 2, DH)
                    if part == "q":
                        dve.wait_ge(S["qsq"][s].sem, S["qsq"][s].after(u))
                        dve.wait_ge(S["clamped"][s].sem, S["clamped"][s].after(u, 1))
                        nc.vector.tensor_reduce(ss[s][:, 0:HEADS], sqq[s][:], AX.X, ALU.add).then_inc(S["ss_q"][s].sem, 1)
                        dve.wait_ge(tab_made.sem, tab_made.after(u))
                        dve.wait_ge(S["qr"][s].sem, S["qr"][s].after(u, 1))
                        q = A[:].rearrange("p (h d) -> p h d", h=HEADS)
                        wide = lambda j, d: tab[w][:, j:j + 1, d].broadcast_to([P, HEADS, d.stop - d.start])
                        tt(q1[s][:], q, wide(0, slice(0, DH)), ALU.mult)
                        tt(q2[s][:, :, lo], q[:, :, hi], wide(1, lo), ALU.mult)
                        tt(q2[s][:, :, hi], q[:, :, lo], wide(1, hi), ALU.mult).then_inc(S["qm"][s].sem, 1)
                    if part == "k":
                        dve.wait_ge(S["ksq"][s].sem, S["ksq"][s].after(u))
                        dve.wait_ge(S["ss_q"][s].sem, S["ss_q"][s].after(u))
                        nc.vector.tensor_reduce(ss[s][:, HEADS:], sqk[s][:], AX.X, ALU.add).then_inc(S["ss"][s].sem, 1)
                        dve.wait_ge(S["ss"][s].sem, S["ss"][s].after(u))
                        dve.wait_ge(S["ln_n"][s].sem, S["ln_n"][s].after(u, 1))
                        nc.vector.tensor_scalar(ssc[s][:], ss[s][:], 1e-24, None, ALU.max).then_inc(S["clamped"][s].sem, 1)
                        dve.wait_ge(S["qm"][s].sem, S["qm"][s].after(u))
                        dve.wait_ge(S["qT_ps"][s].sem, S["qT_ps"][s].after(u, 1))
                        tt(qr[s][:], q1[s][:], q2[s][:], ALU.add).then_inc(S["qr"][s].sem, 1)
                    if part == "v":
                        dve.wait_ge(S["rn"][s].sem, S["rn"][s].after(u))
                        dve.wait_ge(S["kr"][s].sem, S["kr"][s].after(u, 1))
                        tt(kn[s][:], B[:].rearrange("p (h d) -> p h d", h=HEADS),
                           rn[s][:, HEADS:].unsqueeze(2).broadcast_to([P, HEADS, DH]), ALU.mult).then_inc(S["kn"][s].sem, 1)
                        dve.wait_ge(Q["exp"][s].sem, Q["exp"][s].after(u * NHP - 1))
                        nc.vector.tensor_scalar(rq8[s][:], rn[s][:, 0:HEADS], 8.0, None, ALU.mult).then_inc(S["rq8"][s].sem, 1)
                    if part == "scores":
                        for hp in range(NHP):
                            row_max(s, u, w, hp)
                    if part == "sums":
                        inverse_sums(s, u, 0)
                        inverse_sums(s, u, 1)
                        inverse_sums(s, u, 2)
                    if part == "values":
                        inverse_sums(s, u, 3)
                        evacuate(dve, nc.vector.tensor_copy, s, u, 1)
                        head_out(s, u, 0)
                        evacuate(dve, nc.vector.tensor_copy, s, u, 3)
                        head_out(s, u, 1)
                        head_out(s, u, 2)
                        dve.wait_ge(S["x1"][s].sem, S["x1"][s].after(u, 1))
                        dve.wait_ge(S["dev"][s].sem, S["dev"][s].after(u, 2))
                        dve.wait_ge(S["mean_ps"][s].sem, S["mean_ps"][s].after(u, 2))
                        nc.vector.tensor_copy(x1[s][w][:, :, 0:1], x1[s][1 - w][:, :, P:P + 1]).then_inc(S["carry"][s].sem, 1)
                        head_out(s, u, 3)
                        if w == 0:
                            dve.wait_ge(Q["mx"][s].sem, Q["mx"][s].after(u * NHP + NHP - 1))
                            nc.vector.tensor_copy(mask[s][0][:, 1, :], wm[:, 0:P]).then_inc(S["mask0"][s].sem, 2)
                        dve.wait_ge(S["wo_ps"][s].sem, S["wo_ps"][s].after(u))
                        dve.wait_ge(S["hout"][s].sem, S["hout"][s].after(u, 2))
                        dve.wait_ge(S["carry"][s].sem, S["carry"][s].after(u, 1))
                        tt(x1[s][w][:, :, 1:], B[:, 0:C].rearrange("p (c t) -> p c t", c=CC), hT[s][w][:, :, 1:], ALU.add
                           ).then_inc(S["x1"][s].sem, 1)

                def inverse_sums(s, u, hp):
                    n = u * NHP + hp
                    pair = slice(2 * hp, 2 * hp + 2)
                    dve.wait_ge(Q["exp"][s].sem, Q["exp"][s].after(n))
                    dve.wait_ge(Q["pn"][s].sem, Q["pn"][s].after(n, NHP))
                    nc.vector.reciprocal(rinv[s][:, pair], sums[s][:, pair]).then_inc(Q["rinv"][s].sem, 1)

                def row_max(s, u, w, hp):
                    n = u * NHP + hp
                    pair = slice(2 * hp, 2 * hp + 2)
                    dve.wait_ge(Q["sc"][s].sem, Q["sc"][s].after(n))
                    dve.wait_ge(Q["nb"][s].sem, Q["nb"][s].after(n, NHP))
                    dve.wait_ge(Q["pn"][s].sem, Q["pn"][s].after(n, NHP))
                    if hp == 0 and w == 0:
                        dve.wait_ge(S["mask0"][s].sem, S["mask0"][s].after(u, 1))
                    nc.vector.memset(pause[:, s:s + 1], 0.0)
                    for x in range(2):
                        last_ = nc.vector.tensor_tensor_reduce(out=prob[s][:, 2 * hp + x], in0=bank[s][1 + hp % 2][:, 2 * P * x:2 * P * (x + 1)],
                                                               in1=mask[s][w][:].rearrange("p x n -> p (x n)"), scale=1.0, scalar=3 * MASKED,
                                                               op0=ALU.add, op1=ALU.max, accum_out=mx[s][:, 2 * hp + x:2 * hp + x + 1])
                    last_.then_inc(Q["mx"][s].sem, 1)
                    dve.wait_ge(Q["mx"][s].sem, Q["mx"][s].after(n))
                    dve.wait_ge(S["rq8"][s].sem, S["rq8"][s].after(u))
                    dve.wait_ge(Q["exp"][s].sem, Q["exp"][s].after(n, NHP))
                    nc.vector.scalar_tensor_tensor(out=nb[s][:, pair], in0=mx[s][:, pair], scalar=-1.0, in1=rq8[s][:, pair],
                                                   op0=ALU.mult, op1=ALU.mult).then_inc(Q["nb"][s].sem, 1)

                def head_out(s, u, hp):
                    dve.wait_ge(Q["pv"][s].sem, Q["pv"][s].after(u * NHP + hp))
                    dve.wait_ge(S["wo_ps"][s].sem, S["wo_ps"][s].after(u, 1))
                    for x in range(2):
                        last_ = nc.vector.tensor_copy(oT[s][x * DH:(x + 1) * DH, hp],
                                                      bank[s][OUT[hp % 2]][x * DH:(x + 1) * DH, x * P:(x + 1) * P])
                    last_.then_inc(Q["oT"][s].sem, 1)

                def evacuate(eng, copy, s, u, hp):
                    eng.wait_ge(Q["pt_ps"][s].sem, Q["pt_ps"][s].after(u * NHP + hp))
                    eng.wait_ge(Q["pv"][s].sem, Q["pv"][s].after(u * NHP - 1))
                    copy(pT[s][:, 2 * hp:2 * hp + 2].rearrange("p h x t -> p (h x t)"), turned(s, hp)[:]).then_inc(E["pT_odd"][s].sem, 1)

                def mlp(s, u, w, part):
                    A, B, Cb, D = bank[s]
                    if part == "mean":
                        dve.wait_ge(S["mean_ps"][s].sem, S["mean_ps"][s].after(u))
                        dve.wait_ge(S["hn"][s].sem, S["hn"][s].after(u, 1))
                        dve.wait_ge(S["dsq"][s].sem, S["dsq"][s].after(u, 1))
                        dve.wait_ge(S["x1"][s].sem, S["x1"][s].after(u))
                        dve.wait_ge(S["carry"][s].sem, S["carry"][s].after(u))
                        tt(dev[s][:], shifted(x1[s][w]).rearrange("p (c t) -> p c t", c=CC),
                           Cb[:, 0:P].unsqueeze(1).broadcast_to([P, CC, P]), ALU.subtract).then_inc(S["dev"][s].sem, 1)
                    if part == "hidden":
                        for j, tiles in enumerate(G):
                            n = 3 * u + j
                            dve.wait_ge(M["gel"][s].sem, M["gel"][s].after(n))
                            dve.wait_ge(S["w2_ps"][s].sem, S["w2_ps"][s].after(u, 1))
                            for x, m in enumerate(tiles):
                                last = nc.vector.scalar_tensor_tensor(out=hid[s][:, m], in0=bank[s][j][0:MW, 2 * x * P:(2 * x + 1) * P],
                                                                      scalar=b1c[:, 0, m:m + 1], in1=gel[s][:, m], op0=ALU.add, op1=ALU.mult)
                            last.then_inc(M["hid"][s].sem, 1)
                    if part == "out":
                        dve.wait_ge(S["w2_ps"][s].sem, S["w2_ps"][s].after(u))
                        dve.wait_ge(S["yT" if LAST else "out"][s].sem, S["yT" if LAST else "out"][s].after(u, 1))
                        for c in range(CC):
                            last = nc.vector.scalar_tensor_tensor(out=hout[s][:, c], in0=D[:, c * P:(c + 1) * P], scalar=lngb[:, 2, c:c + 1],
                                                                  in1=x1[s][w][:, c, 1:], op0=ALU.add, op1=ALU.add)
                        last.then_inc(S["hout"][s].sem, 1)
                        if LAST:
                            dve.wait_ge(S["yT"][s].sem, S["yT"][s].after(u))
                            dve.wait_ge(S["outt"][s].sem, S["outt"][s].after(u, 1))
                            tt(t1[s][:], D[:, C:2 * C], rows[:, (2 + s) * C:(3 + s) * C], ALU.mult).then_inc(S["t1"][s].sem, 1)

                run(dve, att, mlp, prologue, mean_first=True)

            @block.scalar
            def _(act):
                def prologue():
                    act.wait_ge(sems["w"], 128)
                    act.wait_ge(sems["set"], 1)
                    act.preload_act_table_set(LN_EXP)
                    if not LAST:
                        for b in range(NB):
                            act.dma_start(a["h1"][b, :, :, 0:1], zero[:], allow_slow_non_contiguous=True).then_inc(sems["zero"], 16)
                        act.wait_ge(sems["zero"], 16 * NB)

                def evacuate(s, u, hp):
                    act.wait_ge(Q["pt_ps"][s].sem, Q["pt_ps"][s].after(u * NHP + hp))
                    act.wait_ge(Q["pv"][s].sem, Q["pv"][s].after(u * NHP - 1))
                    nc.scalar.copy(pT[s][:, 2 * hp:2 * hp + 2].rearrange("p h x t -> p (h x t)"), turned(s, hp)[:]).then_inc(E["pT_even"][s].sem, 1)

                def att(s, u, w, part):
                    A, B, Cb, D = bank[s]
                    if part == "q":
                        act.wait_ge(S["q_ps"][s].sem, S["q_ps"][s].after(u))
                        act.wait_ge(S["ss"][s].sem, S["ss"][s].after(u, 1))
                        nc.scalar.activation(sqq[s][:].rearrange("p h d -> p (h d)"), A[:], ACT.Square).then_inc(S["qsq"][s].sem, 1)
                    if part == "k":
                        act.wait_ge(S["k_ps"][s].sem, S["k_ps"][s].after(u))
                        nc.scalar.activation(sqk[s][:].rearrange("p h d -> p (h d)"), B[:], ACT.Square).then_inc(S["ksq"][s].sem, 1)
                    if part == "v":
                        act.wait_ge(S["v_ps"][s].sem, S["v_ps"][s].after(u))
                        act.wait_ge(Q["pv"][s].sem, Q["pv"][s].after(u * NHP - 1))
                        nc.scalar.copy(V[s][:, w].rearrange("p h d -> p (h d)"), Cb[:]).then_inc(S["v_sb"][s].sem, 1)
                        act.wait_ge(S["clamped"][s].sem, S["clamped"][s].after(u))
                        nc.scalar.activation(lnn[s][:], ssc[s][:], ACT.Ln, scale=LNSCALE).then_inc(S["ln_n"][s].sem, 1)
                        act.wait_ge(S["ln_n"][s].sem, S["ln_n"][s].after(u))
                        act.wait_ge(S["kn"][s].sem, S["kn"][s].after(u, 1))
                        act.wait_ge(S["rq8"][s].sem, S["rq8"][s].after(u, 1))
                        nc.scalar.activation(rn[s][:], lnn[s][:], ACT.Exp, scale=-0.5, bias=const[:, 2:3]).then_inc(S["rn"][s].sem, 1)
                    if part == "turn_q":
                        act.wait_ge(S["qT_ps"][s].sem, S["qT_ps"][s].after(u))
                        act.wait_ge(Q["sc"][s].sem, Q["sc"][s].after(u * NHP - 1))
                        qT = D[:].rearrange("p (h t) -> p h t", h=NHP)
                        nc.scalar.copy(qz[s][0:DH, 0::2, :], qT[0:DH])
                        nc.scalar.copy(qz[s][DH:P, 1::2, :], qT[DH:P]).then_inc(S["qz"][s].sem, 1)
                    if part == "turn_k":
                        act.wait_ge(S["kT_ps"][s].sem, S["kT_ps"][s].after(u))
                        act.wait_ge(Q["sc"][s].sem, Q["sc"][s].after(u * NHP - 1))
                        nc.scalar.copy(kT[s][:, :, w, :], A[:].rearrange("p (h t) -> p h t", h=NHP)).then_inc(S["kT"][s].sem, 1)
                    if part == "sums":
                        act.preload_act_table_set(LN_EXP)
                        for hp in range(NHP):
                            n = u * NHP + hp
                            act.wait_ge(Q["nb"][s].sem, Q["nb"][s].after(n))
                            act.wait_ge(Q["pn"][s].sem, Q["pn"][s].after(n, NHP))
                            act.wait_ge(Q["rinv"][s].sem, Q["rinv"][s].after(n, NHP))
                            for x in range(2):
                                h = 2 * hp + x
                                last = nc.scalar.activation(prob[s][:, h], prob[s][:, h], ACT.Exp,
                                                            scale=rq8[s][:, h:h + 1], bias=nb[s][:, h:h + 1],
                                                            accum_out=sums[s][:, h:h + 1])
                            last.then_inc(Q["exp"][s].sem, 1)
                    if part == "values":
                        evacuate(s, u, 0)
                        evacuate(s, u, 2)

                def mlp(s, u, w, part):
                    A, B, Cb, D = bank[s]
                    if part == "mean":
                        act.wait_ge(S["dev"][s].sem, S["dev"][s].after(u))
                        act.wait_ge(S["var_ps"][s].sem, S["var_ps"][s].after(u, 1))
                        nc.scalar.activation(dsq[s][:], dev[s][:], ACT.Square).then_inc(S["dsq"][s].sem, 1)
                    if part == "variance":
                        act.wait_ge(S["var_ps"][s].sem, S["var_ps"][s].after(u))
                        act.wait_ge(S["rstd"][s].sem, S["rstd"][s].after(u, 1))
                        nc.scalar.activation(lnv[s][:], Cb[:, P:2 * P], ACT.Ln, bias=const[:, 0:1]).then_inc(S["ln_v"][s].sem, 1)
                        act.wait_ge(S["ln_v"][s].sem, S["ln_v"][s].after(u))
                        act.wait_ge(S["hn"][s].sem, S["hn"][s].after(u, 1))
                        nc.scalar.activation(rstd[s][:], lnv[s][:], ACT.Exp, scale=-0.5).then_inc(S["rstd"][s].sem, 1)
                    if part == "hidden":
                        for j, tiles in enumerate(G):
                            n = 3 * u + j
                            act.wait_ge(M["w1_ps"][s].sem, M["w1_ps"][s].after(n))
                            act.wait_ge(M["hid"][s].sem, M["hid"][s].after(n, 3))
                            for x, m in enumerate(tiles):
                                last = nc.scalar.activation(gel[s][:, m], bank[s][j][0:MW, (2 * x + 1) * P:(2 * x + 2) * P], ACT.Gelu,
                                                            bias=b1c[:, 1, m:m + 1])
                            last.then_inc(M["gel"][s].sem, 1)
                run(act, att, mlp, prologue)

            @block.tensor
            def _(pe):
                mm = nc.tensor.matmul

                def prologue():
                    pe.wait_ge(sems["w"], 128)
                    for x in range(2):
                        for m in range(MT):
                            for k in range(CC):
                                last = mm(bank[0][0][0:MW, x * MT + m:x * MT + m + 1], w1[:, k, x, m * MW:(m + 1) * MW], lngb[:, 1, k:k + 1],
                                          start=(k == 0), stop=(k == CC - 1))
                    last.then_inc(sems["bias"], 1)
                    pe.wait_ge(sems["prep"], 1)
                    pe.wait_ge(sems["set"], 1)

                def att(s, u, w, part):
                    A, B, Cb, D = bank[s]
                    if part in ("q", "k", "v"):
                        j = "qkv".index(part)
                        pe.wait_ge(I[w]["h_in"][s].sem, I[w]["h_in"][s].after(u - w, -1))
                        h = shifted(hT[s][w])
                        pe.wait_ge(M["hid"][s].sem, M["hid"][s].after(3 * (u - 1) + j))
                        for k in range(CC):
                            last = mm(bank[s][j][:], h[:, k * P:(k + 1) * P], wqkv[:, k, j * INNER:(j + 1) * INNER],
                                      start=(k == 0), stop=(k == CC - 1))
                        last.then_inc(S[f"{part}_ps"][s].sem, 1)
                    if part == "turn_q":
                        pe.wait_ge(S["qr"][s].sem, S["qr"][s].after(u))
                        pe.wait_ge(S["t1" if LAST else "hout"][s].sem, S["t1" if LAST else "hout"][s].after(u, 1))
                        for hp in range(NHP):
                            last = nc.tensor.transpose(D[:, hp * P:(hp + 1) * P],
                                                       qr[s][:, 2 * hp:2 * hp + 2].rearrange("p h d -> p (h d)"), ident[:])
                        last.then_inc(S["qT_ps"][s].sem, 1)
                    if part == "turn_k":
                        pe.wait_ge(S["kr"][s].sem, S["kr"][s].after(u))
                        pe.wait_ge(S["qsq"][s].sem, S["qsq"][s].after(u))
                        pe.wait_ge(S["qm"][s].sem, S["qm"][s].after(u))
                        for hp in range(NHP):
                            last = nc.tensor.transpose(A[:, hp * P:(hp + 1) * P],
                                                       kr[s][:, 2 * hp:2 * hp + 2].rearrange("p h d -> p (h d)"), ident[:])
                        last.then_inc(S["kT_ps"][s].sem, 1)
                    if part in ("scores", "values"):
                        def scores(hp):
                            n = u * NHP + hp
                            if hp == 0:
                                pe.wait_ge(S["qz"][s].sem, S["qz"][s].after(u))
                                pe.wait_ge(S["kT"][s].sem, S["kT"][s].after(u))
                                pe.wait_ge(S["kn"][s].sem, S["kn"][s].after(u))
                            if hp == 1:
                                pe.wait_ge(S["v_sb"][s].sem, S["v_sb"][s].after(u))
                            if hp > 1:
                                pe.wait_ge(Q["mx"][s].sem, Q["mx"][s].after(n, 2))
                            bk = bank[s][1 + hp % 2]
                            for x in range(2):
                                last_ = mm(bk[:, 2 * P * x:2 * P * (x + 1)], qz[s][:, 2 * hp + x],
                                           kT[s][:, hp].rearrange("p x t -> p (x t)"), start=True, stop=True)
                            last_.then_inc(Q["sc"][s].sem, 1)

                        def turn(hp):
                            n = u * NHP + hp
                            pe.wait_ge(Q["pn"][s].sem, Q["pn"][s].after(n))
                            if hp in (1, 2):
                                pe.wait_ge(Q["mx"][s].sem, Q["mx"][s].after(n + 1))
                            if hp == 3:
                                pe.wait_ge(E["pT_even"][s].sem, E["pT_even"][s].after(2 * u))
                            for x in range(2):
                                for slot in range(2):
                                    at = (2 * x + slot) * P
                                    last_ = nc.tensor.transpose(turned(s, hp)[:, at:at + P], pn[s][:, 2 * hp + x, slot * P:(slot + 1) * P], ident[:])
                            last_.then_inc(Q["pt_ps"][s].sem, 1)

                        def values(hp):
                            n = u * NHP + hp
                            pe.wait_ge(E[parity[hp % 2]][s].sem, E[parity[hp % 2]][s].after(2 * u + hp // 2))
                            pe.wait_ge(Q["oT"][s].sem, Q["oT"][s].after(n, 2))
                            for slot in range(2):
                                last_ = mm(bank[s][OUT[hp % 2]][:, 0:2 * P], V[s][:, slot, 2 * hp:2 * hp + 2].rearrange("p h d -> p (h d)"),
                                           pT[s][:, 2 * hp:2 * hp + 2, slot], start=(slot == 0), stop=(slot == 1))
                            last_.then_inc(Q["pv"][s].sem, 1)

                    if part == "scores":
                        for hp in range(NHP):
                            scores(hp)
                    if part == "values":
                        turn(0)
                        turn(1)
                        turn(2)
                        values(0)
                        turn(3)
                        for hp in range(1, NHP):
                            values(hp)
                        pe.wait_ge(Q["oT"][s].sem, Q["oT"][s].after(u * NHP + NHP - 1))
                        pe.wait_ge(Q["exp"][s].sem, Q["exp"][s].after(u * NHP + NHP - 1))
                        for m in range(CC):
                            for k in range(NHP):
                                last = mm(B[:, m * P:(m + 1) * P], wo[:, k, m * P:(m + 1) * P], oT[s][:, k], start=(k == 0), stop=(k == NHP - 1))
                        last.then_inc(S["wo_ps"][s].sem, 1)

                def mlp(s, u, w, part):
                    A, B, Cb, D = bank[s]
                    if part == "mean":
                        pe.wait_ge(S["x1"][s].sem, S["x1"][s].after(u))
                        for k in range(CC):
                            last = mm(Cb[:, 0:P], mean_w[:], shifted(x1[s][w])[:, k * P:(k + 1) * P], start=(k == 0), stop=(k == CC - 1))
                        last.then_inc(S["mean_ps"][s].sem, 1)
                    if part == "variance":
                        pe.wait_ge(S["dsq"][s].sem, S["dsq"][s].after(u))
                        for k in range(CC):
                            last = mm(Cb[:, P:2 * P], mean_w[:], dsq[s][:, k], start=(k == 0), stop=(k == CC - 1))
                        last.then_inc(S["var_ps"][s].sem, 1)
                    if part == "hidden":
                        pe.wait_ge(S["hn"][s].sem, S["hn"][s].after(u))
                        pe.wait_ge(S["ln_v"][s].sem, S["ln_v"][s].after(u))
                        for j, tiles in enumerate(G):
                            for x, m in enumerate(tiles):
                                for y in range(2):
                                    for k in range(CC):
                                        at = (2 * x + y) * P
                                        last = mm(bank[s][j][0:MW, at:at + P], w1[:, k, y, m * MW:(m + 1) * MW], hn[s][:, k],
                                                  start=(k == 0), stop=(k == CC - 1))
                            last.then_inc(M["w1_ps"][s].sem, 1)
                    if part == "out":
                        pe.wait_ge(M["hid"][s].sem, M["hid"][s].after(3 * u + 2))
                        for c in range(CC):
                            for m in range(MT):
                                last = mm(D[:, c * P:(c + 1) * P], w2[:, m, c * P:(c + 1) * P], hid[s][:, m], start=(m == 0), stop=(m == MT - 1))
                        last.then_inc(S["w2_ps"][s].sem, 1)
                        if LAST:
                            pe.wait_ge(S["hout"][s].sem, S["hout"][s].after(u))
                            for c in range(CC):
                                last = nc.tensor.transpose(D[:, C + c * P:C + (c + 1) * P], hout[s][:, c], ident[:])
                            last.then_inc(S["yT"][s].sem, 1)

                run(pe, att, mlp, prologue)


def run_stages(nc, a, T, stages=("setup", "mix", "scan", "gate", "local0", "local1")):
    with ExitStack() as ctx:
        sb = lambda n, s: ctx.enter_context(nc.sbuf_tensor(n, s, F32))
        persist = {"modc": sb("modc", [P, 24]), "rows": sb("rows", [P, 4 * C]), "vec": sb("vec", [P, len(VECS), CC]),
                   "half": sb("half", [P, 3, CC]), "const": sb("const", [P, 8]), "ident": sb("ident", [P, P])}
        if "setup" in stages:
            setup_stage(nc, persist, a)
        if "mix" in stages:
            mix_stage(nc, persist, a, T)
        if "scan" in stages:
            scan_stage(nc, persist, a, T)
        if "gate" in stages:
            gate_stage(nc, persist, a, T)
        for layer in range(2):
            if f"local{layer}" in stages:
                local_stage(nc, persist, a, T, layer)


def _cm(w):
    import numpy as np
    return np.ascontiguousarray(w.reshape(-1, P, w.shape[1]).transpose(1, 0, 2))


def _rows(n, *parts):
    import numpy as np
    out = np.zeros((n, parts[0][1].shape[1]), np.float32)
    for at, w in parts:
        out[at:at + w.shape[0]] = w
    return out


def lay_out(inp):
    import numpy as np
    g = lambda n: np.asarray(inp["L0_" + n])
    at = lambda n: g("attn_" + n)
    two = lambda w: _cm(w).reshape(P, -1)
    parts = dict(
        maa1=two(at("maa_w1").T), wr=two(at("Wr").T), gate1=two(at("gate_w1").T),
        wa1=two(_rows(P, (0, at("decay_w1")), (64, at("aaa_w1")), (96, at("ma_w1"))).T), wk=two(at("Wk").T),
        kk1=two(_rows(P, (0, at("kkk_w1")), (64, at("mk_w1"))).T), wv=two(at("Wv").T),
        **{f"maa2_{k}": _rows(P, (32 * k, at("maa_w2")[k])) for k in range(4)}, gate2=at("gate_w2"),
        decay2=_rows(P, (0, at("decay_w2"))), aaa2=_rows(P, (64, at("aaa_w2"))), ma2=_rows(P, (96, at("ma_w2"))),
        kkk2=_rows(P, (0, at("kkk_w2"))), mk2=_rows(P, (64, at("mk_w2"))))
    maa = at("time_maa").reshape(4, C)
    vecs = [at("time_maa_x"), maa[0], maa[1], maa[2], maa[3], at("time_decay"), at("time_aaaaa"), at("time_misc_a"),
            at("time_misc_k"), at("time_faaaa"), at("ln_w"), at("ln_b")]
    out = {"x": at("x"), "c_t": _cm(g("c").T), "wmod": _cm(g("wmod")),
           "mix_w": np.concatenate([parts[n] for n, _ in MIX_W], axis=1),
           "vecs": np.ascontiguousarray(np.stack(vecs).reshape(len(vecs), CC, P).transpose(2, 0, 1)),
           "ident": np.eye(P, dtype=np.float32),
           "ones16": np.kron(np.eye(HP, dtype=np.float32), np.ones((HS, HS), np.float32)),
           "resets": np.ascontiguousarray(np.broadcast_to((np.arange(CC * P) % CH != 0).astype(np.float32), (P, CC * P)))}
    out["wo_attn"] = _cm(at("Wo").T)
    m, t = np.arange(P)[:, None] % CH, np.arange(CH)[None, :]
    out["causal"] = np.stack([m < t, m <= t], axis=1).astype(np.float32)
    out["headmask"] = (np.arange(P)[:, None] // HS == np.arange(HP)[None, :]).astype(np.float32)
    out["eye16"] = np.ascontiguousarray(np.broadcast_to(np.eye(CH, dtype=np.float32), (P, 2, CH, CH)))
    q, kx = np.arange(P)[:, None], np.arange(P)[None, :]
    neg = np.float32(MASKED)
    before, own = np.where(kx < q, neg, 0), np.where(kx > q, neg, 0)
    out["winmask"] = np.concatenate([before, own], axis=1).astype(np.float32)
    n = out["x"].shape[1]
    half = np.arange(0, DH, 2, dtype=np.float32)
    inv = (1.0 / np.power(np.float32(10000.0), half / np.float32(DH))).astype(np.float32)
    tt = np.arange(n, dtype=np.float32)
    fr = tt[:, None] * inv[None, :]
    base = (half + np.float32(0.4 * DH)) / np.float32(1.4 * DH)
    power = (tt - n // 2) / np.float32(P // 2)
    scale = np.power(base[None, :], power[:, None]).astype(np.float32)
    cos, sin = np.cos(fr), np.sin(fr)
    cat = lambda u, w: np.concatenate([u, w], axis=1)
    out["rotary"] = np.stack([cat(cos * scale, cos * scale), cat(-sin * scale, sin * scale),
                              cat(cos / scale, cos / scale), cat(-sin / scale, sin / scale)], axis=1).astype(np.float32)
    f = lambda n_: g("ffn_" + n_)
    swap = lambda v: np.concatenate([v[:, DH // 2:], v[:, :DH // 2]], axis=1)
    qs, ks = f("q_scale"), f("k_scale")
    out["qk_scale"] = np.ascontiguousarray(np.broadcast_to(
        np.stack([qs, swap(qs), ks, swap(ks)], axis=1)[:, None], (2, P, 4, DH)))
    out["wqkv"] = np.stack([_cm(w) for w in f("wqkv")])
    out["wo"] = np.stack([_cm(w) for w in f("wo")])
    pad = MT * MW - HID
    halves = lambda w: np.pad(w.reshape(C, 2, HID), [(0, 0), (0, 0), (0, pad)]).reshape(C, -1)
    out["w1"] = np.stack([_cm(halves(w)) for w in f("w1")])
    tiles = lambda v: np.pad(v, [(0, pad)] + [(0, 0)] * (v.ndim - 1)).reshape(MT, MW, *v.shape[1:])
    out["w2"] = np.stack([tiles(w).transpose(1, 0, 2) for w in f("w2")])
    out["b1"] = np.stack([np.stack([tiles(b[:HID]), tiles(b[HID:])]).transpose(2, 0, 1) for b in f("b1")])
    col = lambda v: v.reshape(-1, CC, P).transpose(0, 2, 1)
    out["ln_gb"] = np.stack([col(f("ln_g")), col(f("ln_b")), col(f("b2"))], axis=2)
    return {k_: np.ascontiguousarray(v_) for k_, v_ in out.items()}


SCRATCH = lambda T: {
    "cm": [NB, T // P, P, CC * 4 * P], "gr": [NB, T // P, P, 2 * CC * P], "gl": [NB, T // P, P, CC * NCH],
    "v_stack": [NB, T // P, P, CC, NCH, HS], "att": [2 * (T // P), NB * CC * NCH // 2, HP, CH, CH],
    "inv": [2 * (T // P), NB * CC * NCH // 2, HP, CH, CH], "y_stack": [T // P, 2, P, NCH // 2 * NB * CC * HS],
    "xa": [NB, T, C], "h0": [NB, P, CC, T + 1], "h1": [NB, P, CC, T + 1]}


def kernel(**inputs):
    import concourse.bacc as bacc
    from concourse.bass_utils import run_bass_kernel_spmd

    arrays = lay_out(inputs)
    T = arrays["x"].shape[1]
    nc = bacc.Bacc("TRN2", target_bir_lowering=False, num_devices=1)
    a = {n: nc.dram_tensor("in_" + n, v.shape, mybir.dt.from_np(v.dtype), kind="ExternalInput").ap() for n, v in arrays.items()}
    a.update({n: nc.dram_tensor("scratch_" + n, s, F32, kind="Internal").ap() for n, s in SCRATCH(T).items()})
    a["out"] = nc.dram_tensor("out_0", [NB, T, C], F32, kind="ExternalOutput").ap()
    run_stages(nc, a, T)
    got = run_bass_kernel_spmd(nc, [{"in_" + n: v for n, v in arrays.items()}], core_ids=[0])
    return got.results[0]["out_0"]
```
